# Optimizing a Trainium2 kernel written in Bass

```python
import numpy as np
import jax
import jax.numpy as jnp

def _softmax(x, axis=-1):
    return jax.nn.softmax(x, axis=axis)

def _gelu(x):
    return jax.nn.gelu(x, approximate=True)

def _silu(x):
    return jax.nn.silu(x)

def _sigmoid(x):
    return jax.nn.sigmoid(x)

def _layernorm(x, axis=-1, eps=1e-05):
    m = jnp.mean(x, axis=axis, keepdims=True)
    v = jnp.var(x, axis=axis, keepdims=True)
    return (x - m) / jnp.sqrt(v + eps)

def _scatter_add(tgt, idx, src, axis=0):
    return tgt.at[idx].add(src)

def _segment_sum(src, seg, n):
    return jax.ops.segment_sum(src, seg, n)
kernel_name = 'mk_sandwich_d1_jaxref_r4_36db59'

def setup_inputs(seed: int=0):
    np.random.seed(seed)
    _w = jnp.asarray

    def _L0_attn_setup():
        import jax, jax.numpy as jnp
        import numpy as np
        D_IN = 512
        D_OUT = 512
        N_HEADS = 16
        D_KV_COMP = 128
        D_ROPE = 32
        D_HEAD = D_OUT // N_HEADS
        SPLIT = D_HEAD - D_ROPE
        B, S = (2, 512)

        def _rotary_cos_sin(seq_len):
            inv_freq = 1.0 / 10000.0 ** (jnp.arange(0, D_ROPE, 2, dtype=jnp.float32) / D_ROPE)
            freqs = jnp.arange(seq_len, dtype=jnp.float32)[:, None] * inv_freq[None, :]
            emb = jnp.concatenate([freqs, freqs], axis=-1)
            cos = jnp.cos(emb)[None, :, None, :]
            sin = jnp.sin(emb)[None, :, None, :]
            return (cos, sin)

        def _apply_rotary(t, cos, sin):
            t1, t2 = jnp.split(t, 2, axis=-1)
            rot = jnp.concatenate([-t2, t1], axis=-1)
            return t * cos + rot * sin

        def _reference_tuple_inner(x, W_dkv, b_dkv, W_dq, b_dq, W_uk, b_uk, W_uv, b_uv, W_uq, b_uq, W_qr, b_qr, W_kr, b_kr, W_o, b_o):
            B_, S_, _ = x.shape
            c_kv = x @ W_dkv + b_dkv
            k = (c_kv @ W_uk + b_uk).reshape(B_, S_, N_HEADS, SPLIT)
            v = (c_kv @ W_uv + b_uv).reshape(B_, S_, N_HEADS, D_HEAD)
            c_q = x @ W_dq + b_dq
            q_base = (c_q @ W_uq + b_uq).reshape(B_, S_, N_HEADS, SPLIT)
            q_rot = (c_q @ W_qr + b_qr).reshape(B_, S_, N_HEADS, D_ROPE)
            cos, sin = _rotary_cos_sin(S_)
            q_rot = _apply_rotary(q_rot, cos, sin)
            k_rot = _apply_rotary((x @ W_kr + b_kr).reshape(B_, S_, N_HEADS, D_ROPE), cos, sin)
            q = jnp.concatenate([q_base, q_rot], axis=-1)
            k = jnp.concatenate([k, k_rot], axis=-1)
            scores = jnp.einsum('bqhd,bkhd->bhqk', q, k) / jnp.sqrt(jnp.float32(D_HEAD))
            attn = jax.nn.softmax(scores, axis=-1)
            out = jnp.einsum('bhqk,bkhd->bqhd', attn, v)
            out = out.reshape(B_, S_, N_HEADS * D_HEAD) @ W_o + b_o
            return (out, c_kv, k_rot)
        key = jax.random.key(seed)
        ks = jax.random.split(key, 16)
        sd = lambda fan_in: 1.0 / np.sqrt(fan_in)

        def lin(k, fan_in, fan_out):
            kw, kb = jax.random.split(k)
            W = jax.random.uniform(kw, (fan_in, fan_out), jnp.float32, -sd(fan_in), sd(fan_in))
            b = jax.random.uniform(kb, (fan_out,), jnp.float32, -sd(fan_in), sd(fan_in))
            return (W, b)
        W_dkv, b_dkv = lin(ks[0], D_OUT, D_KV_COMP)
        W_dq, b_dq = lin(ks[1], D_OUT, D_KV_COMP)
        W_uk, b_uk = lin(ks[2], D_KV_COMP, N_HEADS * SPLIT)
        W_uv, b_uv = lin(ks[3], D_KV_COMP, N_HEADS * D_HEAD)
        W_uq, b_uq = lin(ks[4], D_KV_COMP, N_HEADS * SPLIT)
        W_qr, b_qr = lin(ks[5], D_KV_COMP, N_HEADS * D_ROPE)
        W_kr, b_kr = lin(ks[6], D_IN, N_HEADS * D_ROPE)
        W_o, b_o = lin(ks[7], N_HEADS * D_HEAD, D_OUT)
        x = jax.random.normal(ks[8], (B, S, D_IN), jnp.float32)
        return dict(x=x, W_dkv=W_dkv, b_dkv=b_dkv, W_dq=W_dq, b_dq=b_dq, W_uk=W_uk, b_uk=b_uk, W_uv=W_uv, b_uv=b_uv, W_uq=W_uq, b_uq=b_uq, W_qr=W_qr, b_qr=b_qr, W_kr=W_kr, b_kr=b_kr, W_o=W_o, b_o=b_o)
    _L0_attn_in = _L0_attn_setup()

    def _L0_ffn_setup():
        import jax, jax.numpy as jnp
        import numpy as np
        HIDDEN = 512
        INTER = 2048
        SCALE = 64.0

        def fwht(x):
            orig_shape = x.shape
            n = orig_shape[-1]
            x = x.reshape(-1, n)
            h = 1
            while h < n:
                x = x.reshape(-1, n // (2 * h), 2, h)
                a, b = (x[:, :, 0, :], x[:, :, 1, :])
                x = jnp.stack([a + b, a - b], axis=2).reshape(-1, n)
                h *= 2
            return (x / jnp.sqrt(jnp.asarray(n, x.dtype))).reshape(orig_shape)
        key = jax.random.key(seed)
        ks = jax.random.split(key, 8)
        inp = jax.random.normal(ks[0], (4, 512, HIDDEN), dtype=jnp.float32)
        SU_ug = jnp.where(jax.random.bernoulli(ks[1], 0.5, (HIDDEN,)), 1.0, -1.0).astype(jnp.float32)
        SU_dp = jnp.where(jax.random.bernoulli(ks[2], 0.5, (INTER,)), 1.0, -1.0).astype(jnp.float32)
        Wscale_ug = jax.random.uniform(ks[3], (2 * INTER,), jnp.float32, 0.5, 1.5)
        Wscale_dp = jax.random.uniform(ks[4], (HIDDEN,), jnp.float32, 0.5, 1.5)
        W_up = jax.random.normal(ks[5], (INTER, HIDDEN), dtype=jnp.float32) * 0.02
        W_gate = jax.random.normal(ks[6], (INTER, HIDDEN), dtype=jnp.float32) * 0.02
        W_down = jax.random.normal(ks[7], (HIDDEN, INTER), dtype=jnp.float32) * 0.02
        return {'input': inp, 'SU_ug': SU_ug, 'SU_dp': SU_dp, 'Wscale_ug': Wscale_ug, 'Wscale_dp': Wscale_dp, 'W_up': W_up, 'W_gate': W_gate, 'W_down': W_down}
    _L0_ffn_in = _L0_ffn_setup()
    _d = {'L0_attn_x': _L0_attn_in['x'], 'L0_attn_W_dkv': _L0_attn_in['W_dkv'], 'L0_attn_b_dkv': _L0_attn_in['b_dkv'], 'L0_attn_W_dq': _L0_attn_in['W_dq'], 'L0_attn_b_dq': _L0_attn_in['b_dq'], 'L0_attn_W_uk': _L0_attn_in['W_uk'], 'L0_attn_b_uk': _L0_attn_in['b_uk'], 'L0_attn_W_uv': _L0_attn_in['W_uv'], 'L0_attn_b_uv': _L0_attn_in['b_uv'], 'L0_attn_W_uq': _L0_attn_in['W_uq'], 'L0_attn_b_uq': _L0_attn_in['b_uq'], 'L0_attn_W_qr': _L0_attn_in['W_qr'], 'L0_attn_b_qr': _L0_attn_in['b_qr'], 'L0_attn_W_kr': _L0_attn_in['W_kr'], 'L0_attn_b_kr': _L0_attn_in['b_kr'], 'L0_attn_W_o': _L0_attn_in['W_o'], 'L0_attn_b_o': _L0_attn_in['b_o'], 'L0_ffn_SU_ug': _L0_ffn_in['SU_ug'], 'L0_ffn_SU_dp': _L0_ffn_in['SU_dp'], 'L0_ffn_Wscale_ug': _L0_ffn_in['Wscale_ug'], 'L0_ffn_Wscale_dp': _L0_ffn_in['Wscale_dp'], 'L0_ffn_W_up': _L0_ffn_in['W_up'], 'L0_ffn_W_gate': _L0_ffn_in['W_gate'], 'L0_ffn_W_down': _L0_ffn_in['W_down']}
    _x0 = _d['L0_attn_x']
    _d['L0_attn_x'] = jax.random.normal(jax.random.fold_in(jax.random.key(seed), 1), (8, 512, 512), dtype=_x0.dtype)
    del _x0
    return _d

def reference(L0_attn_x, L0_attn_W_dkv, L0_attn_b_dkv, L0_attn_W_dq, L0_attn_b_dq, L0_attn_W_uk, L0_attn_b_uk, L0_attn_W_uv, L0_attn_b_uv, L0_attn_W_uq, L0_attn_b_uq, L0_attn_W_qr, L0_attn_b_qr, L0_attn_W_kr, L0_attn_b_kr, L0_attn_W_o, L0_attn_b_o, L0_ffn_SU_ug, L0_ffn_SU_dp, L0_ffn_Wscale_ug, L0_ffn_Wscale_dp, L0_ffn_W_up, L0_ffn_W_gate, L0_ffn_W_down):

    def _L0_attn_ref(x, W_dkv, b_dkv, W_dq, b_dq, W_uk, b_uk, W_uv, b_uv, W_uq, b_uq, W_qr, b_qr, W_kr, b_kr, W_o, b_o):
        import jax, jax.numpy as jnp
        import numpy as np
        D_IN = 512
        D_OUT = 512
        N_HEADS = 16
        D_KV_COMP = 128
        D_ROPE = 32
        D_HEAD = D_OUT // N_HEADS
        SPLIT = D_HEAD - D_ROPE
        B, S = (2, 512)

        def _rotary_cos_sin(seq_len):
            inv_freq = 1.0 / 10000.0 ** (jnp.arange(0, D_ROPE, 2, dtype=jnp.float32) / D_ROPE)
            freqs = jnp.arange(seq_len, dtype=jnp.float32)[:, None] * inv_freq[None, :]
            emb = jnp.concatenate([freqs, freqs], axis=-1)
            cos = jnp.cos(emb)[None, :, None, :]
            sin = jnp.sin(emb)[None, :, None, :]
            return (cos, sin)

        def _apply_rotary(t, cos, sin):
            t1, t2 = jnp.split(t, 2, axis=-1)
            rot = jnp.concatenate([-t2, t1], axis=-1)
            return t * cos + rot * sin

        def _reference_tuple_inner(x, W_dkv, b_dkv, W_dq, b_dq, W_uk, b_uk, W_uv, b_uv, W_uq, b_uq, W_qr, b_qr, W_kr, b_kr, W_o, b_o):
            B_, S_, _ = x.shape
            c_kv = x @ W_dkv + b_dkv
            k = (c_kv @ W_uk + b_uk).reshape(B_, S_, N_HEADS, SPLIT)
            v = (c_kv @ W_uv + b_uv).reshape(B_, S_, N_HEADS, D_HEAD)
            c_q = x @ W_dq + b_dq
            q_base = (c_q @ W_uq + b_uq).reshape(B_, S_, N_HEADS, SPLIT)
            q_rot = (c_q @ W_qr + b_qr).reshape(B_, S_, N_HEADS, D_ROPE)
            cos, sin = _rotary_cos_sin(S_)
            q_rot = _apply_rotary(q_rot, cos, sin)
            k_rot = _apply_rotary((x @ W_kr + b_kr).reshape(B_, S_, N_HEADS, D_ROPE), cos, sin)
            q = jnp.concatenate([q_base, q_rot], axis=-1)
            k = jnp.concatenate([k, k_rot], axis=-1)
            scores = jnp.einsum('bqhd,bkhd->bhqk', q, k) / jnp.sqrt(jnp.float32(D_HEAD))
            attn = jax.nn.softmax(scores, axis=-1)
            out = jnp.einsum('bhqk,bkhd->bqhd', attn, v)
            out = out.reshape(B_, S_, N_HEADS * D_HEAD) @ W_o + b_o
            return (out, c_kv, k_rot)
        return _reference_tuple_inner(x, W_dkv, b_dkv, W_dq, b_dq, W_uk, b_uk, W_uv, b_uv, W_uq, b_uq, W_qr, b_qr, W_kr, b_kr, W_o, b_o)[0]

    def _L0_ffn_ref(input, SU_ug, SU_dp, Wscale_ug, Wscale_dp, W_up, W_gate, W_down):
        import jax, jax.numpy as jnp
        import numpy as np
        HIDDEN = 512
        INTER = 2048
        SCALE = 64.0

        def fwht(x):
            orig_shape = x.shape
            n = orig_shape[-1]
            x = x.reshape(-1, n)
            h = 1
            while h < n:
                x = x.reshape(-1, n // (2 * h), 2, h)
                a, b = (x[:, :, 0, :], x[:, :, 1, :])
                x = jnp.stack([a + b, a - b], axis=2).reshape(-1, n)
                h *= 2
            return (x / jnp.sqrt(jnp.asarray(n, x.dtype))).reshape(orig_shape)
        n = SU_ug.shape[0]
        x = input.reshape(-1, n)
        x = fwht(x * SU_ug) / SCALE
        x_up = x @ W_up.T * (Wscale_ug[:INTER] * SCALE)
        x_gate = x @ W_gate.T * (Wscale_ug[INTER:] * SCALE)
        x = jax.nn.silu(x_gate) * x_up
        x = fwht(x * SU_dp) / SCALE
        x = x @ W_down.T * (Wscale_dp * SCALE)
        return x.reshape(input.shape)
    x = L0_attn_x
    x = x + _layernorm(_L0_attn_ref(_layernorm(x, axis=-1), L0_attn_W_dkv, L0_attn_b_dkv, L0_attn_W_dq, L0_attn_b_dq, L0_attn_W_uk, L0_attn_b_uk, L0_attn_W_uv, L0_attn_b_uv, L0_attn_W_uq, L0_attn_b_uq, L0_attn_W_qr, L0_attn_b_qr, L0_attn_W_kr, L0_attn_b_kr, L0_attn_W_o, L0_attn_b_o), axis=-1)
    x = x + _layernorm(_L0_ffn_ref(_layernorm(x, axis=-1), L0_ffn_SU_ug, L0_ffn_SU_dp, L0_ffn_Wscale_ug, L0_ffn_Wscale_dp, L0_ffn_W_up, L0_ffn_W_gate, L0_ffn_W_down), axis=-1)
    return x

_drawn_inputs = setup_inputs


def setup_inputs(seed=0):
    import zlib

    import numpy as np

    out = dict(_drawn_inputs(seed))
    spreads = {}
    factors = {'L0_attn_b_dq': 32.013, 'L0_attn_b_qr': 8.0, 'L0_attn_b_kr': 28.73}
    for name, (base, spread) in spreads.items():
        noise = np.random.default_rng([zlib.crc32(name.encode()), seed]).standard_normal(out[name].shape)
        drawn = base * np.exp(spread * noise) if base else spread * noise
        out[name] = jnp.asarray(drawn.astype(out[name].dtype))
    for name, factor in factors.items():
        out[name] = (out[name] * factor).astype(out[name].dtype)
    return out
```

```python
from contextlib import ExitStack

import numpy as np

import concourse.bass as bass
from concourse import mybir

F32 = mybir.dt.float32
F16 = mybir.dt.float16
U32 = mybir.dt.uint32
ALU = mybir.AluOpType
ACT = mybir.ActivationFunctionType
AX = mybir.AxisListType
RMAX = bass.bass_isa.ReduceOp.max

P = 128
NB, S, D = 8, 512, 512
T = S // P
KT = D // P
NH, DH = 16, 32
HG = P // DH
NG = NH // HG
INTER = 2048
NJ = INTER // P
HALF = 256
STACK = 3 * DH
EPS = 1e-5
PASSES = ((0, 0), (0, 1), (1, 0))

W_TOP = 16.0
D_TOP = 256.0
Q_SHIFT, K_SHIFT = 2.0 ** -17, 2.0 ** -4
V_SHIFT = 2.0 ** -12
MAX_SHIFT = 2.0 ** 15
H_SHIFT = 2.0 ** -14
ROW_SHIFT = 2.0 ** 12

A_KR, A_O, A_DQ, A_DKV, A_QR, A_UV, A_N = 0, 4, 8, 9, 10, 11, 12
(C_DQ, C_DKV, C_QR, C_KR, C_UV, C_O, C_UP, C_GATE, C_DOWN, C_SU, C_PROD, C_N) = range(12)


def build_schedule():
    att = [("ln1", t) for t in range(T)] + [("c", 0), ("c", 1)] + [("v", t) for t in range(T)]
    att += [("proj", 0, 0), ("proj", 0, 1)]
    ffn_after = {}
    for g in range(NG):
        att += [("stack", g, w, j) for w in (0, 1) for j in range(2)]
        ffn_after[len(att) - 3] = 1
        ffn_after[len(att) - 1] = 1
        for n in range(HG * T):
            att.append(("smax", g, n // T, n % T))
            if n % 6 == 5:
                ffn_after[len(att) - 1] = 1
        att += [("maxrow", g, 0), ("maxrow", g, 1)]
        if g + 1 < NG:
            att += [("proj", g + 1, 0), ("proj", g + 1, 1)]
        for u in range(2 * T):
            att += [("st", g, u, 0), ("st", g, u, 1)]
            if u % 2 == 0:
                ffn_after[len(att) - 1] = 1
            if u:
                att.append(("av", g, u - 1))
        att += [("av", g, 2 * T - 1), ("norm", g)]
    att += [("o", 0), ("o", 1), ("ln2", 0), ("o", 2), ("ln2", 1), ("o", 3), ("ln2", 2), ("ln2", 3)]
    ffn = []
    for hf in range(2):
        ffn += [("ffn", hf * NJ + j) for j in range(NJ + 2)][: NJ]
        ffn += [("flush", hf), ("fin", hf, 0), ("fin", hf, 1)]
    both, left = [], list(ffn)
    for n, step in enumerate(att):
        both.append(step)
        for _ in range(ffn_after.get(n, 0)):
            while left and left[0][0] != "ffn":
                both.append(left.pop(0))
            if left:
                both.append(left.pop(0))
        if step == ("norm", NG - 1):
            both += left
            left = []
    return att, both, ffn


ATT, BOTH, FFN = build_schedule()
ITEMS = [s for s in ATT if s[0] not in ("av", "norm")]
ITEM = {s: n for n, s in enumerate(ITEMS)}
IPB = len(ITEMS) // 2
assert len(ITEMS) % 2 == 0 and [s for s in BOTH if s in ITEM] == ITEMS
SCRATCH = [s for s in ATT if s[0] in ("ln1", "proj", "norm", "ln2")]
SCR = {s: n for n, s in enumerate(SCRATCH)}
NS = len(SCRATCH)
NST = NG * 2 * T * 2
NAV = NG * 2 * T


def setup_block(nc, a, ps, ps16, sem, sb, w):
    with ExitStack() as stage:
        def tmp(name, shape, dt=F32):
            return sb(name, shape, dt, stage)

        scale = w["scale"]
        nat = [tmp("nat0", [P, NJ, D]), tmp("nat1", [P, NJ, D])]
        fly = tmp("fly", [P, 2048])
        hadT = tmp("hadT", [P, 2048])
        ident32 = tmp("ident32", [P, P])
        had = tmp("had", [P, P])
        b512 = hadT[:, 0:1024].rearrange("p (i n) -> p i n", n=512)
        bo = fly[:, 0:512]
        b_uv_col = tmp("b_uv_col", [P, KT])
        b_uv_rep = fly[:, 512:1024].rearrange("p (k n) -> p k n", k=KT)
        c_raw = tmp("c_raw", [P, 2])
        su_ug = tmp("su_ug", [P, KT])
        su_dp = tmp("su_dp", [P, NJ])
        ws_up = tmp("ws_up", [P, NJ])
        ws_gate = tmp("ws_gate", [P, NJ])
        ws_dp = tmp("ws_dp", [P, KT])
        prod = tmp("prod", [P, NJ])
        m_own = tmp("m_own", [P, C_N])
        m_all = tmp("m_all", [P, C_N])
        m_bias = tmp("m_bias", [P, 8])
        bound = tmp("bound", [P, C_N])
        inv = tmp("inv", [P, C_N])
        one = tmp("one", [P, 8])
        up_f = tmp("up_f", [P, KT])
        gate_f = tmp("gate_f", [P, KT])
        down_f = tmp("down_f", [P, NJ])
        split32 = hadT[:, 1024:2048].rearrange("p (i n) -> p i n", n=512)

        s_attw, s_bias, s_small = sem("s_attw"), sem("s_bias"), sem("s_small")
        s_up, s_gate, s_down = sem("s_up"), sem("s_gate"), sem("s_down")
        s_own = sem("s_own")
        s_pool = sem("s_pool")
        s_max, s_maxall = sem("s_max"), sem("s_maxall")
        s_bo, s_bo_used = sem("s_bo"), sem("s_bo_used")
        s_scaled, s_hi, s_lo = sem("s_scaled"), sem("s_hi"), sem("s_lo")
        s_add, s_sub = sem("s_add"), sem("s_sub")
        s_tp, s_tc, s_hp = sem("s_tp"), sem("s_tc"), sem("s_hp")
        s_whi, s_wlo = sem("s_whi"), sem("s_wlo")
        s_factors = sem("s_factors")
        s_dscaled = sem("s_dscaled")

        attr = w["att_raw"]
        CH = 4
        chunks = [(m, c) for m in range(3) for c in range(CH)]

        def natural(m, c):
            return nat[m % 2][:, 4 * c:4 * c + 4, :].rearrange("p i n -> p (i n)")

        def stages(m):
            return [(1, 2), (2, 1)] if m < 2 else [(1, 8), (2, 4), (4, 2), (8, 1)]

        def halves(t, m, h):
            n = 2048 // (2 * h * P)
            r = t.rearrange("p (n r q) -> p n r q", n=n, r=2)
            return r[:, :, 0, :], r[:, :, 1, :]

        n_tr = 0
        block = stage.enter_context(nc.Block())

        @block.sync
        def _(sp):
            sp.dma_start(attr[:, A_KR:A_KR + KT, :], a["W_kr"].rearrange("(k p) n -> p k n", p=P)).then_inc(s_attw, 16)
            sp.dma_start(attr[:, A_O:A_O + KT, :], a["W_o"].rearrange("(k p) n -> p k n", p=P)).then_inc(s_attw, 16)
            sp.dma_start(attr[:, A_DQ, :].rearrange("p (k n) -> p k n", k=KT),
                         a["W_dq"].rearrange("(k p) n -> p k n", p=P)).then_inc(s_attw, 16)
            sp.dma_start(attr[:, A_DKV, :].rearrange("p (k n) -> p k n", k=KT),
                         a["W_dkv"].rearrange("(k p) n -> p k n", p=P)).then_inc(s_attw, 16)
            sp.dma_start(attr[:, A_QR, :], a["W_qr"]).then_inc(s_attw, 16)
            sp.dma_start(attr[:, A_UV, :], a["W_uv"]).then_inc(s_attw, 16)
            for m, (name, s) in enumerate((("W_up", s_up), ("W_gate", s_gate))):
                src = a[name].rearrange("(i p) n -> p i n", p=P)
                for c in range(CH):
                    sp.dma_start(nat[m][:, 4 * c:4 * c + 4, :], src[:, 4 * c:4 * c + 4, :]).then_inc(s, 16)
            src = a["W_down"].rearrange("(o p) n -> p o n", p=P)
            sp.wait_ge(s_tp, CH * 4)
            for c in range(CH):
                sp.dma_start(natural(2, c), src[:, c, :]).then_inc(s_down, 16)

        @block.gpsimd
        def _(pool):
            nc.gpsimd.memset(ident32[:], 0.0).then_inc(s_pool, 1)
            nc.gpsimd.memset(w["ident"][:], 0.0).then_inc(s_pool, 1)
            pool.wait_ge(s_pool, 2)
            for t in (ident32, w["ident"]):
                nc.gpsimd.affine_select(out=t[:], in_=t[:], compare_op=ALU.not_equal, fill=1.0, base=0,
                                        pattern=[[-1, P]], channel_multiplier=1).then_inc(s_pool, 1)
            pool.wait_ge(s_max, 1)
            nc.gpsimd.partition_all_reduce(m_all[:, 0:C_N], m_own[:, 0:C_N], P, RMAX).then_inc(s_maxall, 1)
            k = 0
            for n, (m, c) in enumerate(chunks):
                if m == 2 and c == 0:
                    pool.wait_ge(s_max, 2)
                    nc.gpsimd.partition_all_reduce(m_all[:, C_DOWN:C_DOWN + 1], m_own[:, C_DOWN:C_DOWN + 1], P,
                                                   RMAX).then_inc(s_maxall, 1)
                pool.wait_ge((s_up, s_gate, s_dscaled)[m], 16 * CH if m < 2 else c + 1)
                for i, (h, _) in enumerate(stages(m)):
                    src, dst = (natural(m, c), fly[:]) if i % 2 == 0 else (fly[:], natural(m, c))
                    if i:
                        pool.wait_ge(s_add, k)
                    elif n:
                        pool.wait_ge(s_add, k)
                    if k == 0:
                        pool.wait_ge(s_bo_used, 1)
                    x0, x1 = halves(src, m, h)
                    nc.gpsimd.tensor_tensor(halves(dst, m, h)[1], x0, x1, ALU.subtract).then_inc(s_sub, 1)
                    k += 1
                    pool.wait_ge(s_sub, k)

        @block.scalar
        def _(sc):
            for dst, name in ((b512[:, 0, :], "b_kr"), (b512[:, 1, :], "b_qr"), (bo, "b_o")):
                sc.dma_start(dst, a[name].partition_broadcast(P)).then_inc(s_bias, 16)
            small = [(b_uv_col[:], a["b_uv"].rearrange("(k p) -> p k", p=P)),
                     (c_raw[:, 0:1], a["b_dq"].rearrange("(p o) -> p o", o=1)),
                     (c_raw[:, 1:2], a["b_dkv"].rearrange("(p o) -> p o", o=1)),
                     (su_ug[:], a["SU_ug"].rearrange("(k p) -> p k", p=P)),
                     (su_dp[:], a["SU_dp"].rearrange("(k p) -> p k", p=P)),
                     (ws_up[:], a["Wscale_ug"][0:INTER].rearrange("(k p) -> p k", p=P)),
                     (ws_gate[:], a["Wscale_ug"][INTER:2 * INTER].rearrange("(k p) -> p k", p=P)),
                     (ws_dp[:], a["Wscale_dp"].rearrange("(k p) -> p k", p=P)),
                     (w["rope"][:], a["rope"].rearrange("i (t p) d -> p i t d", p=P)),
                     (had[:], a["had"])]
            for dst, src in small:
                sc.dma_start(dst, src, allow_slow_non_contiguous=True).then_inc(s_small, 16)
            for n in range(A_N):
                sc.wait_ge(s_scaled, n + 1)
                nc.scalar.activation(w["att_w"][:, n, 0, :], split32[:, n % 2, :], ACT.Copy).then_inc(s_hi, 1)
            hp = 0
            tc = 0

            def rotated(n_tiles, fac, dst):
                nonlocal hp
                for i in range(n_tiles):
                    sc.wait_ge(s_hp, hp + 1)
                    nc.scalar.activation(dst(i)[0], ps[:, 4 + hp % 4, :], ACT.Copy, scale=fac(i)).then_inc(s_whi, 1)
                    hp += 1

            sc.wait_ge(s_factors, 1)
            sc.wait_ge(s_lo, A_N)
            for n, (m, c) in enumerate(chunks):
                for q in range(4):
                    sc.wait_ge(s_tp, tc + 1)
                    if m < 2:
                        if tc >= 4:
                            sc.wait_ge(s_hp, tc - 3)
                        dst = hadT[:, q * 512:(q + 1) * 512]
                    else:
                        if tc == 32:
                            sc.wait_ge(s_wlo, 32)
                        dst = w["down_raw"][:, 4 * q:4 * q + 4, c * P:(c + 1) * P]
                    src = ps[:, tc % 4, :] if m < 2 else ps[:, tc % 4, :].rearrange("p (i n) -> p i n", i=4)
                    nc.scalar.activation(dst, src, ACT.Copy).then_inc(s_tc, 1)
                    tc += 1
                if m < 2:
                    wt, f = ((w["up_w"], up_f), (w["gate_w"], gate_f))[m]
                    rotated(4, lambda i: f[:, i:i + 1], lambda i: (wt[:, i, 0, c * 512:(c + 1) * 512],))
            sc.wait_ge(s_factors, 2)
            rotated(NJ, lambda i: down_f[:, i:i + 1], lambda i: (w["down_w"][:, i, 0, :],))

        @block.tensor
        def _(pe):
            pe.wait_ge(s_attw, 16 * 6)
            pe.wait_ge(s_bo, 1)
            for k in range(KT):
                mm = nc.tensor.matmul(ps[:, 0, :], b_uv_rep[:, k, :], attr[:, A_O + k, :], start=k == 0, stop=k == KT - 1)
            mm.then_inc(s_bo, 1)
            pe.wait_ge(s_pool, 4)
            pe.wait_ge(s_small, 16 * 10)
            pe.wait_ge(s_bo_used, 1)
            tr = hp = 0
            done = 0
            for m, c in chunks:
                done += len(stages(m))
                pe.wait_ge(s_add, done)
                pe.wait_ge(s_sub, done)
                for q in range(4):
                    if tr >= 4:
                        pe.wait_ge(s_tc, tr - 3)
                    for i in range(4):
                        blk = (i * 4 + q) if m < 2 else (q * 4 + i)
                        mm = nc.tensor.transpose(ps[:, tr % 4, i * P:(i + 1) * P], natural(m, c)[:, blk * P:(blk + 1) * P],
                                                 ident32[:])
                    mm.then_inc(s_tp, 1)
                    tr += 1
                if m < 2:
                    for q in range(4):
                        pe.wait_ge(s_tc, tr - 3 + q)
                        if hp >= 4:
                            pe.wait_ge(s_wlo, hp - 3)
                        nc.tensor.matmul(ps[:, 4 + hp % 4, :], had[:], hadT[:, q * 512:(q + 1) * 512],
                                         start=True, stop=True).then_inc(s_hp, 1)
                        hp += 1
            for i in range(NJ):
                pe.wait_ge(s_tc, 48)
                pe.wait_ge(s_wlo, hp - 3)
                nc.tensor.matmul(ps[:, 4 + hp % 4, :], had[:], w["down_raw"][:, i, :],
                                 start=True, stop=True).then_inc(s_hp, 1)
                hp += 1

        @block.vector
        def _(dve):
            chain = [0]

            def link(ins):
                chain[0] += 1
                ins.then_inc(s_own, 1)
                dve.wait_ge(s_own, chain[0])

            ts, tt_, stt = nc.vector.tensor_scalar, nc.vector.tensor_tensor, nc.vector.scalar_tensor_tensor

            def biggest(out_, in_, ax=AX.X):
                link(nc.vector.tensor_reduce(out_, in_, ax, ALU.max, apply_absolute_value=True))

            link(nc.vector.memset(w["ones"][:], 1.0))
            for pick, rows, value in ((w["pick_q"], (0, 64), ROW_SHIFT), (w["pick_k"], (32, 96), 1.0)):
                link(nc.vector.memset(pick[:], 0.0))
                for r in rows:
                    link(nc.vector.memset(pick[r:r + 1, :], value))
            link(nc.vector.memset(m_own[:], 0.0))
            link(nc.vector.memset(one[:], 1.0))

            dve.wait_ge(s_small, 16 * 10)
            dve.wait_ge(s_bias, 16 * 3)
            for k in range(KT):
                link(ts(b_uv_rep[:, k, :], had[:], 0.0, b_uv_col[:, k:k + 1], ALU.mult, ALU.add))
            nc.vector.memset(one[:], 1.0).then_inc(s_bo, 1)
            link(tt_(prod[:], ws_up[:], ws_gate[:], ALU.mult))
            link(tt_(prod[:], prod[:], su_dp[:], ALU.mult))

            dve.wait_ge(s_attw, 16 * 6)
            for col, lo, n in ((C_KR, A_KR, KT), (C_O, A_O, KT), (C_DQ, A_DQ, 1), (C_DKV, A_DKV, 1), (C_QR, A_QR, 1),
                               (C_UV, A_UV, 1)):
                biggest(m_own[:, col:col + 1], attr[:, lo:lo + n, :].rearrange("p k n -> p (k n)"))
            biggest(m_own[:, C_SU:C_SU + 1], su_ug[:])
            biggest(m_own[:, C_PROD:C_PROD + 1], prod[:])
            for i in range(2):
                biggest(m_bias[:, i:i + 1], b512[:, i, :])
            dve.wait_ge(s_up, 16 * CH)
            biggest(m_own[:, C_UP:C_UP + 1], nat[0][:].rearrange("p i n -> p (i n)"))
            biggest(m_own[:, C_DOWN:C_DOWN + 1], c_raw[:])
            dve.wait_ge(s_gate, 16 * CH)
            chain[0] += 1
            nc.vector.tensor_reduce(m_own[:, C_GATE:C_GATE + 1], nat[1][:].rearrange("p i n -> p (i n)"), AX.X, ALU.max,
                                    apply_absolute_value=True).then_inc(s_own, 1)
            dve.wait_ge(s_own, chain[0])
            nc.vector.tensor_copy(bound[:, 0:1], one[:, 0:1]).then_inc(s_max, 1)
            dve.wait_ge(s_maxall, 1)

            def scale_of(col, top):
                cs = slice(col, col + 1)
                link(ts(bound[:, cs], bound[:, cs], 1e-30, None, ALU.max))
                link(ts(bound[:, cs].bitcast(U32), bound[:, cs].bitcast(U32), 0x7F800000, None, ALU.bitwise_and))
                link(nc.vector.reciprocal(inv[:, cs], bound[:, cs]))
                link(ts(scale[:, cs], inv[:, cs], top, None, ALU.mult))

            def sc1(col):
                return scale[:, col:col + 1]

            for col in (C_DQ, C_DKV):
                link(stt(out=bound[:, col:col + 1], in0=m_all[:, C_DOWN:C_DOWN + 1], scalar=1.0 / D,
                         in1=m_all[:, col:col + 1], op0=ALU.mult, op1=ALU.max))
                scale_of(col, W_TOP)
            link(stt(out=bound[:, C_KR:C_KR + 1], in0=m_bias[:, 0:1], scalar=1.0 / D, in1=m_all[:, C_KR:C_KR + 1],
                     op0=ALU.mult, op1=ALU.max))
            scale_of(C_KR, W_TOP)
            link(ts(m_bias[:, 2:3], m_bias[:, 1:2], sc1(C_DQ), 2.0 ** -22, ALU.mult, ALU.mult))
            link(tt_(bound[:, C_QR:C_QR + 1], m_bias[:, 2:3], m_all[:, C_QR:C_QR + 1], ALU.max))
            scale_of(C_QR, W_TOP)
            link(nc.vector.tensor_copy(bound[:, C_UV:C_UV + 1], m_all[:, C_UV:C_UV + 1]))
            scale_of(C_UV, W_TOP)
            dve.wait_ge(s_bo, 2)
            link(tt_(bo, bo, ps[:, 0, :], ALU.add))
            biggest(m_bias[:, 3:4], bo)
            link(ts(m_bias[:, 4:5], sc1(C_DKV), sc1(C_UV), V_SHIFT, ALU.mult, ALU.mult))
            link(ts(m_bias[:, 5:6], m_bias[:, 3:4], m_bias[:, 4:5], 2.0 ** -22, ALU.mult, ALU.mult))
            link(tt_(bound[:, C_O:C_O + 1], m_bias[:, 5:6], m_all[:, C_O:C_O + 1], ALU.max))
            scale_of(C_O, W_TOP)
            for col in (C_UP, C_GATE):
                link(tt_(bound[:, col:col + 1], m_all[:, col:col + 1], m_all[:, C_SU:C_SU + 1], ALU.mult))
                scale_of(col, W_TOP)
            for f, col in ((up_f, C_UP), (gate_f, C_GATE)):
                link(ts(f[:], su_ug[:], sc1(col), float(D) ** -0.5, ALU.mult, ALU.mult))
            nc.vector.memset(one[:], 1.0).then_inc(s_factors, 1)
            link(tt_(w["c_bias"][:], c_raw[:], scale[:, C_DQ:C_DKV + 1], ALU.mult))

            def bias_rows(dst, src, rows, factor1, factor2):
                link(ts(src, src, factor1, factor2, ALU.mult, ALU.mult))
                link(nc.vector.tensor_copy(split32[:, 0, 0:256].bitcast(F16), src))
                link(tt_(split32[:, 0, 256:512].bitcast(F16), src, split32[:, 0, 0:256].bitcast(F16), ALU.subtract))
                for r, half in zip(rows, range(2)):
                    link(nc.vector.tensor_copy(dst[r:r + 1, :], split32[r:r + 1, 0, 256 * half:256 * half + 256].bitcast(F16)))

            link(nc.vector.memset(w["bias_qk"][:], 0.0))
            link(nc.vector.memset(w["bias_o"][:], 0.0))
            link(ts(m_bias[:, 6:7], sc1(C_DQ), sc1(C_QR), 1.0 / ROW_SHIFT, ALU.mult, ALU.mult))
            bias_rows(w["bias_qk"], b512[:, 0, :], (32, 96), sc1(C_KR), 1.0)
            bias_rows(w["bias_qk"], b512[:, 1, :], (0, 64), m_bias[:, 6:7], 1.0)
            link(ts(m_bias[:, 7:8], m_bias[:, 4:5], sc1(C_O), None, ALU.mult))
            bias_rows(w["bias_o"], bo, (0, 64), m_bias[:, 7:8], 1.0 / ROW_SHIFT)
            link(ts(w["eps_y"][:], m_bias[:, 7:8], m_bias[:, 7:8], EPS, ALU.mult, ALU.mult))
            link(ts(w["exp_scale"][:], bound[:, C_DQ:C_DQ + 1], bound[:, C_QR:C_QR + 1], 1.0 / W_TOP ** 2,
                    ALU.mult, ALU.mult))
            link(ts(w["exp_scale"][:], w["exp_scale"][:], bound[:, C_KR:C_KR + 1],
                    1.0 / (W_TOP * Q_SHIFT * K_SHIFT * DH ** 0.5), ALU.mult, ALU.mult))
            link(ts(w["half_gate"][:], ws_gate[:], bound[:, C_GATE:C_GATE + 1], 0.5 / W_TOP, ALU.mult, ALU.mult))
            nc.vector.memset(one[:], 1.0).then_inc(s_bo_used, 1)

            hi_n = 0
            for n in range(A_N):
                col = C_KR if n < A_O else C_O if n < A_DQ else {A_DQ: C_DQ, A_DKV: C_DKV, A_QR: C_QR, A_UV: C_UV}[n]
                ts(split32[:, n % 2, :], attr[:, n, :], sc1(col), None, ALU.mult).then_inc(s_scaled, 1)
                dve.wait_ge(s_scaled, n + 1)
                dve.wait_ge(s_hi, n + 1)
                nc.vector.tensor_tensor(w["att_w"][:, n, 1, :], split32[:, n % 2, :], w["att_w"][:, n, 0, :],
                                        ALU.subtract).then_inc(s_lo, 1)

            k = 0
            hp = 0

            def rotated_low(n_tiles, fac, dst):
                nonlocal hp
                for i in range(n_tiles):
                    hi, lo = dst(i)
                    dve.wait_ge(s_whi, hp + 1)
                    stt(out=lo, in0=ps[:, 4 + hp % 4, :], scalar=fac(i), in1=hi, op0=ALU.mult,
                        op1=ALU.subtract).then_inc(s_wlo, 1)
                    hp += 1

            def up_low(m, c):
                wt, f = ((w["up_w"], up_f), (w["gate_w"], gate_f))[m]
                cols = slice(c * 512, (c + 1) * 512)
                rotated_low(4, lambda i: f[:, i:i + 1], lambda i: (wt[:, i, 0, cols], wt[:, i, 1, cols]))

            for n, (m, c) in enumerate(chunks):
                if m == 2 and c == 0:
                    dve.wait_ge(s_down, 16 * CH)
                    for cc in range(CH):
                        link(ts(natural(2, cc), natural(2, cc), ws_dp[:, cc:cc + 1], None, ALU.mult))
                    biggest(m_own[:, C_DOWN:C_DOWN + 1], nat[0][:].rearrange("p i n -> p (i n)"))
                    nc.vector.memset(one[:], 1.0).then_inc(s_max, 1)
                    dve.wait_ge(s_maxall, 2)
                    link(tt_(bound[:, C_DOWN:C_DOWN + 1], m_all[:, C_DOWN:C_DOWN + 1], m_all[:, C_PROD:C_PROD + 1],
                             ALU.mult))
                    scale_of(C_DOWN, D_TOP)
                    link(ts(down_f[:], prod[:], sc1(C_DOWN), float(INTER) ** -0.5, ALU.mult, ALU.mult))
                    link(ts(m_bias[:, 2:3], sc1(C_UP), sc1(C_GATE), sc1(C_DOWN), ALU.mult, ALU.mult))
                    link(ts(m_bias[:, 2:3], m_bias[:, 2:3], 2.0 * H_SHIFT, None, ALU.mult))
                    link(ts(w["eps_f"][:], m_bias[:, 2:3], m_bias[:, 2:3], EPS, ALU.mult, ALU.mult))
                    nc.vector.memset(one[:], 1.0).then_inc(s_factors, 1)
                    nc.vector.memset(m_bias[:], 1.0).then_inc(s_dscaled, CH)
                for i, (h, _) in enumerate(stages(m)):
                    src, dst = (natural(m, c), fly[:]) if i % 2 == 0 else (fly[:], natural(m, c))
                    dve.wait_ge(s_sub, k)
                    dve.wait_ge(s_add, k)
                    x0, x1 = halves(src, m, h)
                    tt_(halves(dst, m, h)[0], x0, x1, ALU.add).then_inc(s_add, 1)
                    k += 1
                if 1 <= n and chunks[n - 1][0] < 2:
                    up_low(*chunks[n - 1])
            rotated_low(NJ, lambda i: down_f[:, i:i + 1], lambda i: (w["down_w"][:, i, 0, :], w["down_w"][:, i, 1, :]))



def program(nc, a, out, y_dram):
    ctx = ExitStack()
    with ctx:
        def sb(name, shape, dt, where=ctx):
            return where.enter_context(nc.sbuf_tensor(name, shape, dt))

        def sem(name):
            return ctx.enter_context(nc.semaphore(name))

        ps = ctx.enter_context(nc.psum_tensor("ps", [P, 8, 512], F32))
        ps16 = ps[:].bitcast(F16)

        att_w = sb("att_w", [P, A_N, 2, 512], F16)
        up_w = sb("up_w", [P, KT, 2, INTER], F16)
        gate_w = sb("gate_w", [P, KT, 2, INTER], F16)
        down_w = sb("down_w", [P, NJ, 2, D], F16)
        att_raw = att_w[:].rearrange("p a b n -> p (a b n)").bitcast(F32).rearrange("p (a n) -> p a n", a=A_N)
        down_raw = down_w[:].rearrange("p a b n -> p (a b n)").bitcast(F32).rearrange("p (a n) -> p a n", a=NJ)
        bias_qk = sb("bias_qk", [P, 512], F16)
        bias_o = sb("bias_o", [P, 512], F16)
        pick_q = sb("pick_q", [P, P], F16)
        pick_k = sb("pick_k", [P, P], F16)
        ident = sb("ident", [P, P], F16)
        ones = sb("ones", [P, DH], F16)
        rope = sb("rope", [P, 4, T, DH], F32)
        scale = sb("scale", [P, C_N], F32)
        c_bias = sb("c_bias", [P, 2], F32)
        exp_scale = sb("exp_scale", [P, 1], F32)
        eps_y = sb("eps_y", [P, 1], F32)
        eps_f = sb("eps_f", [P, 1], F32)
        half_gate = sb("half_gate", [P, NJ], F32)
        mhalf = sb("mhalf", [P, 1], F32)

        setup_block(nc, a, ps, ps16, sem, sb, dict(
            att_w=att_w, up_w=up_w, gate_w=gate_w, down_w=down_w, att_raw=att_raw, down_raw=down_raw,
            bias_qk=bias_qk, bias_o=bias_o, pick_q=pick_q, pick_k=pick_k, ident=ident, ones=ones, rope=rope,
            scale=scale, c_bias=c_bias, exp_scale=exp_scale, eps_y=eps_y, eps_f=eps_f,
            half_gate=half_gate, mhalf=mhalf))

        xt = sb("xt", [P, 2, D], F32)
        scr = sb("scr", [P, 2, D], F32)
        nhl = sb("nhl", [P, 2, D], F16)
        xT = sb("xT", [P, 2, KT, S], F16)
        cT = sb("cT", [P, 2, 2, S], F16)
        tok = sb("tok", [P, 2, T, HG, STACK], F16)
        mtok = sb("mtok", [P, T, HG, DH], F16)
        kT = sb("kT", [P, HG, S], F16)
        qT = sb("qT", [P, HG, S], F16)
        v = sb("v", [P, T, 2, D], F16)
        p32 = sb("p32", [P, 2, 512], F32)
        pr = sb("pr", [P, 2, 2, HG, HALF], F16)
        oT = sb("oT", [P, NG, 2, S], F16)
        x2T = sb("x2T", [P, 2, KT, S], F16)
        act = sb("act", [P, 2, HALF], F32)
        hid = sb("hid", [P, 2, 2, HALF], F16)
        yt = sb("yt", [P, 2, D], F32)
        st1 = sb("st1", [P, T, 6], F32)
        mv1 = sb("mv1", [P, T, 2], F32)
        st2 = sb("st2", [P, T, 6], F32)
        mv2 = sb("mv2", [P, T, 2], F32)
        st3 = sb("st3", [P, T, 6], F32)
        mv3 = sb("mv3", [P, T, 2], F32)
        st4 = sb("st4", [P, T, 6], F32)
        mv4 = sb("mv4", [P, T, 2], F32)
        ve = sb("ve", [P, 4, T], F32)
        rs = sb("rs", [P, 4, T], F32)
        nmr = sb("nmr", [P, 4, T], F32)
        carry = sb("carry", [P, 1], F32)
        mx = sb("mx", [P, T, HG], F32)

        work = [ps[:, 0, :], ps[:, 1, :]]
        work16 = [ps16[:, 0, :], ps16[:, 1, :]]
        o_acc, den_acc = ps[:, 2, :], ps[:, 3, :]
        ffn_ps = [ps[:, 4, :], ps[:, 5, :]]
        down_ps = [ps[:, 6, :], ps[:, 7, :]]

        credit = {}

        def counted(name, per_batch):
            s = sem(name)
            credit[name] = (s, per_batch)
            return s

        filled = [counted(f"filled{k}", IPB) for k in range(2)]
        freed = [counted(f"freed{k}", IPB) for k in range(2)]
        x_in = [counted(f"x_in{k}", 16 * T) for k in range(2)]
        ln1_norm = counted("ln1_norm", T)
        part_hi = counted("part_hi", NS)
        scr_free = counted("scr_free", NS)
        cv_hi = counted("cv_hi", 2 + T)
        x_var = counted("x_var", T)
        x_rs = counted("x_rs", T)
        rope_sum = counted("rope_sum", 2 * NG)
        neg_max = counted("neg_max", NG)
        p_hi = counted("p_hi", NST)
        p_lo = counted("p_lo", NST)
        av_done = counted("av_done", NAV)
        o_freed = counted("o_freed", NG)
        oy_var = counted("oy_var", T)
        oy_rs = counted("oy_rs", T)
        y_var = counted("y_var", T)
        y_rs = counted("y_rs", T)
        y_ready = counted("y_ready", T)
        ln2_norm = counted("ln2_norm", T)
        y_out = [counted(f"y_out{k}", 16 * T // 2) for k in range(2)]
        f_filled = counted("f_filled", 2 * NJ)
        f_freed = counted("f_freed", 2 * NJ)
        tanh_done = counted("tanh_done", 2 * NJ)
        h_hi = counted("h_hi", 2 * NJ)
        h_lo = counted("h_lo", 2 * NJ)
        down_done = counted("down_done", 2 * NJ)
        f_var = counted("f_var", T)
        f_rs = counted("f_rs", T)
        fin_done = counted("fin_done", T)
        y_in = [counted(f"y_in{k}", 16 * T // 2) for k in range(2)]
        out_done = [counted(f"out_done{k}", 16 * T // 2) for k in range(2)]
        own_count = {f"{n}{i}": T for n in "xoyf" for i in "ab"} | dict(m=NG, r=NG, on=T, fn=T, fs=T, h=2 * NJ)
        own_sem = {n: counted(f"own_{n}", c) for n, c in own_count.items()}
        init_own = sem("init_own")
        primed = sem("primed")
        tok_init = sem("tok_init")

        def fill(b, step):
            return (b + 1) * IPB + ITEM[step] // 2 + 1

        def bank(step):
            return ITEM[step] % 2

        def of(sem_, per, b, n):
            return sem_, (b + 1) * per + n + 1

        block = ctx.enter_context(nc.Block())

        def run(eng, parts):
            for step in ATT:
                if step[0] in parts:
                    parts[step[0]](0, *step[1:])
            with eng.Fori(1, NB) as b:
                for step in BOTH:
                    if step[0] in parts:
                        parts[step[0]](b - 1 if step[0] in ("ffn", "flush", "fin") else b, *step[1:])
            for step in FFN:
                if step[0] in parts:
                    parts[step[0]](NB - 1, *step[1:])

        @block.sync
        def _(sp):
            for s, n in credit.values():
                sp.sem_inc(s, n)
            sp.sem_inc(primed, 1)
            x_v = a["x"].rearrange("b (t p) d -> b t p d", p=P)
            y_v = y_dram.rearrange("b (t p) d -> b t p d", p=P)
            out_v = out.rearrange("b (t p) d -> b t p d", p=P)

            def load_x(b, r):
                k = r % 2
                if r < 2:
                    sp.wait_ge(*of(ln2_norm, T, b - 1, T - 2 + r))
                    sp.wait_ge(*of(y_out[k], 16 * T // 2, b - 1, 16 * T // 2 - 1))
                elif r < T + 2:
                    sp.wait_ge(*of(ln1_norm, T, b, r - 2))
                else:
                    sp.wait_ge(*of(ln2_norm, T, b, r - 2 - T))
                    sp.wait_ge(*of(y_out[k], 16 * T // 2, b, 15))
                sp.dma_start(xt[:, k, :], x_v[b, r % T]).then_inc(x_in[k], 16)

            def ln1(b, t):
                load_x(b, t)

            def proj(b, g, w):
                if g == 0 and w == 0:
                    load_x(b, T)
                    load_x(b, T + 1)

            def o(b, t):
                sp.wait_ge(*of(y_ready, T, b, t))
                sp.dma_start(y_v[b, t], xt[:, t % 2, :]).then_inc(y_out[t % 2], 16)

            def ln2(b, t):
                if t < 2:
                    load_x(b, T + 2 + t)

            def ffn(b, f):
                if f % NJ == 8:
                    for tt in range(2):
                        n = 2 * (f // NJ) + tt
                        sp.wait_ge(*of(y_out[tt], 16 * T // 2, b, 16 * (n // 2) + 15))
                        sp.wait_ge(*of(out_done[tt], 16 * T // 2, b, 16 * (n // 2) - 1))
                        sp.dma_start(yt[:, tt, :], y_v[b, n]).then_inc(y_in[tt], 16)

            def fin(b, hf, tt):
                sp.wait_ge(*of(fin_done, T, b, 2 * hf + tt))
                sp.dma_start(out_v[b, 2 * hf + tt], yt[:, tt, :]).then_inc(out_done[tt], 16)

            run(sp, dict(ln1=ln1, proj=proj, o=o, ln2=ln2, ffn=ffn, fin=fin))
            for k in range(2):
                sp.wait_ge(*of(out_done[k], 16 * T // 2, NB - 1, 16 * T // 2 - 1))
                sp.wait_ge(*of(y_out[k], 16 * T // 2, NB - 1, 16 * T // 2 - 1))

        @block.tensor
        def _(pe):
            pe.wait_ge(primed, 1)
            pe.wait_ge(tok_init, 3)

            def item(b, step, *after):
                k = bank(step)
                pe.wait_ge(freed[k], (b + 1) * IPB + ITEM[step] // 2)
                other = [ITEM[s] // 2 + 1 for s in after if bank(s) != k]
                if other:
                    pe.wait_ge(freed[1 - k], (b + 1) * IPB + max(other))
                return k

            def transposes(b, step):
                k = item(b, step)
                pe.wait_ge(*of(scr_free, NS, b, SCR[step]))
                for part in range(2):
                    for kt in range(KT):
                        col = (part * KT + kt) * P
                        mm = nc.tensor.transpose(work16[k][:, col:col + P], nhl[:, part, kt * P:(kt + 1) * P], ident[:])
                mm.then_inc(filled[k], 1)

            def ln1(b, t):
                transposes(b, ("ln1", t))

            def ln2(b, t):
                transposes(b, ("ln2", t))

            def c(b, w):
                step = ("c", w)
                k = item(b, step, ("ln1", T - 2), ("ln1", T - 1))
                for kt in range(KT):
                    for n, (pw, px) in enumerate(PASSES):
                        mm = nc.tensor.matmul(work[k], att_w[:, A_DQ + w, pw, kt * P:(kt + 1) * P], xT[:, px, kt, :],
                                              start=kt == n == 0, stop=kt == KT - 1 and n == 2)
                mm.then_inc(filled[k], 1)

            def v_(b, t):
                step = ("v", t)
                k = item(b, step, ("c", 1))
                for n, (pc, pw) in enumerate(PASSES):
                    mm = nc.tensor.matmul(work[k], cT[:, 1, pc, t * P:(t + 1) * P], att_w[:, A_UV, pw, :],
                                          start=n == 0, stop=n == 2)
                mm.then_inc(filled[k], 1)

            def proj(b, g, w):
                step = ("proj", g, w)
                k = item(b, step, ("c", 0))
                cols = slice(g * P, (g + 1) * P)
                pick = (pick_k, pick_q)[w]
                nc.tensor.matmul(work[k].rearrange("p (t n) -> p t n", t=T), pick[:],
                                 bias_qk[:, cols].unsqueeze(1).to_broadcast([P, T, P]),
                                 start=True, stop=False, skip_group_check=True)
                for t in range(T):
                    for kt in range(KT if w == 0 else 1):
                        for pa, pw in PASSES:
                            lhs = xT[:, pa, kt, t * P:(t + 1) * P] if w == 0 else cT[:, 0, pa, t * P:(t + 1) * P]
                            tile = A_KR + kt if w == 0 else A_QR
                            mm = nc.tensor.matmul(work[k][:, t * P:(t + 1) * P], lhs, att_w[:, tile, pw, cols],
                                                  start=False, stop=True, skip_group_check=True)
                mm.then_inc(filled[k], 1)

            def stack(b, g, w, j):
                step = ("stack", g, w, j)
                k = item(b, step)
                pe.wait_ge(*of(scr_free, NS, b, SCR[("proj", g, w)]))
                for hh in range(2):
                    for t in range(T):
                        col = (hh * T + t) * P
                        mm = nc.tensor.transpose(work16[k][0:STACK, col:col + P], tok[:, w, t, 2 * j + hh, :], ident[:])
                mm.then_inc(filled[k], 1)

            def smax(b, g, h, t):
                step = ("smax", g, h, t)
                k = item(b, step, *[("stack", g, w, h // 2) for w in range(2) if h % 2 == 0 and t < 2])
                nc.tensor.matmul(work[k], qT[0:STACK, h, t * P:(t + 1) * P], kT[0:STACK, h, :],
                                 start=True, stop=True).then_inc(filled[k], 1)

            def maxrow(b, g, j):
                step = ("maxrow", g, j)
                k = item(b, step)
                pe.wait_ge(*of(neg_max, NG, b, g))
                for hh in range(2):
                    for t in range(T):
                        col = (hh * T + t) * P
                        mm = nc.tensor.transpose(work16[k][STACK:P, col:col + P], mtok[:, t, 2 * j + hh, :], ident[:])
                mm.then_inc(filled[k], 1)

            def st(b, g, u, j):
                step = ("st", g, u, j)
                k = item(b, step, *[("maxrow", g, j)] * (u == 0))
                kt, qh = divmod(u, 2)
                for hh in range(2):
                    mm = nc.tensor.matmul(work[k][:, hh * HALF:(hh + 1) * HALF], kT[:, 2 * j + hh, kt * P:(kt + 1) * P],
                                          qT[:, 2 * j + hh, qh * HALF:(qh + 1) * HALF], start=True, stop=True)
                mm.then_inc(filled[k], 1)

            def av(b, g, u):
                kt, qh = divmod(u, 2)
                n = g * 2 * T + u
                pe.wait_ge(*of(p_lo, NST, b, 2 * n + 1))
                if u == 0:
                    pe.wait_ge(*of(o_freed, NG, b, g - 1))
                    s = ("v", T - 1)
                    pe.wait_ge(freed[bank(s)], fill(b, s))
                q = slice(qh * HALF, (qh + 1) * HALF)
                for i, (pv, pp) in enumerate(PASSES):
                    for h in range(HG):
                        head = (g * HG + h) * DH
                        nc.tensor.matmul(o_acc[h * DH:(h + 1) * DH, q], v[:, kt, pv, head:head + DH],
                                         pr[:, n % 2, pp, h, :], start=u == 0 and i == 0, stop=True,
                                         skip_group_check=True)
                for pp in range(2):
                    for h in range(HG):
                        mm = nc.tensor.matmul(den_acc[h * DH:(h + 1) * DH, q], ones[:], pr[:, n % 2, pp, h, :],
                                              start=u == 0 and pp == 0, stop=True, skip_group_check=True)
                mm.then_inc(av_done, 1)

            def o(b, t):
                step = ("o", t)
                k = item(b, step)
                pe.wait_ge(*of(scr_free, NS, b, SCR[("norm", NG - 1)]))
                nc.tensor.matmul(work[k], pick_q[:], bias_o[:], start=True, stop=False)
                for g in range(NG):
                    for n, (po, pw) in enumerate(PASSES):
                        mm = nc.tensor.matmul(work[k], oT[:, g, po, t * P:(t + 1) * P], att_w[:, A_O + g, pw, :],
                                              start=False, stop=g == NG - 1 and n == 2)
                mm.then_inc(filled[k], 1)

            def down(b, f):
                hf, j = divmod(f, NJ)
                pe.wait_ge(*of(h_lo, 2 * NJ, b, f))
                for tt in range(2):
                    if j == 0:
                        pe.wait_ge(*of(fin_done, T, b, 2 * hf + tt - 2))
                    for n, (ph, pw) in enumerate(PASSES):
                        mm = nc.tensor.matmul(down_ps[tt], hid[:, f % 2, ph, tt * P:(tt + 1) * P], down_w[:, j, pw, :],
                                              start=j == n == 0, stop=j == NJ - 1 and n == 2)
                mm.then_inc(down_done, 1)

            def ffn(b, f):
                hf, j = divmod(f, NJ)
                if f == 0:
                    s = ("ln2", T - 1)
                    pe.wait_ge(freed[bank(s)], fill(b, s))
                pe.wait_ge(f_freed, (b + 1) * 2 * NJ + f - 1)
                for half, w in enumerate((gate_w, up_w)):
                    for kt in range(KT):
                        for n, (pw, px) in enumerate(PASSES):
                            mm = nc.tensor.matmul(ffn_ps[f % 2][:, half * HALF:(half + 1) * HALF],
                                                  w[:, kt, pw, j * P:(j + 1) * P],
                                                  x2T[:, px, kt, hf * HALF:(hf + 1) * HALF],
                                                  start=kt == n == 0, stop=kt == KT - 1 and n == 2)
                mm.then_inc(f_filled, 1)
                if j >= 2:
                    down(b, f - 2)

            def flush(b, hf):
                down(b, hf * NJ + NJ - 2)
                down(b, hf * NJ + NJ - 1)

            run(pe, dict(ln1=ln1, ln2=ln2, c=c, v=v_, proj=proj, stack=stack, smax=smax, maxrow=maxrow,
                         st=st, av=av, o=o, ffn=ffn, flush=flush))

        @block.scalar
        def _(sc):
            sc.wait_ge(primed, 1)
            sc.wait_ge(tok_init, 3)

            def got(b, step):
                k = bank(step)
                sc.wait_ge(filled[k], fill(b, step))
                return k

            def high(out_, in_, b, step):
                nc.scalar.activation(out_, in_, ACT.Copy).then_inc(part_hi, 1)

            def ln1(b, t):
                sc.wait_ge(*of(ln1_norm, T, b, t))
                s, bb = (("ln1", t - 1), b) if t else (("ln2", T - 1), b - 1)
                sc.wait_ge(filled[bank(s)], fill(bb, s))
                high(nhl[:, 0, :], scr[:, t % 2, :], b, ("ln1", t))

            def ln2(b, t):
                sc.wait_ge(*of(ln2_norm, T, b, t))
                s = ("ln2", t - 1) if t else ("ln1", T - 1)
                sc.wait_ge(filled[bank(s)], fill(b, s))
                high(nhl[:, 0, :], scr[:, t % 2, :], b, ("ln2", t))

            def c(b, w):
                step = ("c", w)
                k = got(b, step)
                nc.scalar.activation(cT[:, w, 0, :], work[k], ACT.Identity, bias=c_bias[:, w:w + 1]).then_inc(cv_hi, 1)

            def v_(b, t):
                k = got(b, ("v", t))
                sc.wait_ge(*of(av_done, NAV, b - 1, NAV - 1))
                nc.scalar.activation(v[:, t, 0, :], work[k], ACT.Copy, scale=V_SHIFT).then_inc(cv_hi, 1)

            def proj(b, g, w):
                sc.wait_ge(*of(rope_sum, 2 * NG, b, 2 * g + w))
                s, bb = (("stack", g - 1, w, 1), b) if g else (("stack", NG - 1, w, 1), b - 1)
                sc.wait_ge(filled[bank(s)], fill(bb, s))
                dst = tok[:, w].rearrange("p t h (r d) -> p (t h) r d", r=3)
                dst = dst[:, :, 0:3:2, :] if w == 0 else dst[:, :, 0:2, :]
                src = scr[:, 0, :].rearrange("p (n r d) -> p n r d", r=1, d=DH).to_broadcast([P, T * HG, 2, DH])
                nc.scalar.activation(dst, src, ACT.Copy).then_inc(part_hi, 1)

            def stack(b, g, w, j):
                if w == 0:
                    return
                step = ("stack", g, w, j)
                k = got(b, step)
                nc.scalar.activation(qT[0:STACK, 2 * j:2 * j + 2, :].rearrange("p h s -> p (h s)"),
                                     work16[k][0:STACK, :], ACT.Copy).then_inc(freed[k], 1)

            def maxrow(b, g, j):
                step = ("maxrow", g, j)
                k = got(b, step)
                nc.scalar.activation(qT[STACK:P, 2 * j:2 * j + 2, :].rearrange("p h s -> p (h s)"),
                                     work16[k][STACK:P, :], ACT.Copy).then_inc(freed[k], 1)

            def prob_high(b, n):
                u, j = divmod(n, 2)
                s = ("st", u // (2 * T), u % (2 * T), j)
                sc.wait_ge(freed[bank(s)], fill(b, s))
                sc.wait_ge(*of(av_done, NAV, b, u - 2))
                nc.scalar.activation(pr[:, u % 2, 0, 2 * j:2 * j + 2, :].rearrange("p h q -> p (h q)"),
                                     p32[:, n % 2, :], ACT.Copy).then_inc(p_hi, 1)

            def st(b, g, u, j):
                step = ("st", g, u, j)
                k = got(b, step)
                n = (g * 2 * T + u) * 2 + j
                sc.wait_ge(*of(p_lo, NST, b, n - 2))
                nc.scalar.activation(p32[:, n % 2, :], work[k], ACT.Exp, scale=exp_scale[:, 0:1]).then_inc(freed[k], 1)
                if (u, j) != (0, 0):
                    prob_high(b, n - 1)
                if (u, j) == (2 * T - 1, 1):
                    prob_high(b, n)

            def norm(b, g):
                step = ("norm", g)
                sc.wait_ge(*of(o_freed, NG, b, g))
                s = ("o", T - 1)
                sc.wait_ge(filled[bank(s)], fill(b - 1, s))
                high(oT[:, g, 0, :], scr[:, 0, :], b, step)

            def h_high(b, f):
                sc.wait_ge(*of(f_freed, 2 * NJ, b, f))
                sc.wait_ge(*of(down_done, 2 * NJ, b, f - 2))
                nc.scalar.activation(hid[:, f % 2, 0, :], act[:, f % 2, :], ACT.Copy).then_inc(h_hi, 1)

            def ffn(b, f):
                hf, j = divmod(f, NJ)
                sc.wait_ge(*of(f_filled, 2 * NJ, b, f))
                sc.wait_ge(*of(h_lo, 2 * NJ, b, f - 2))
                nc.scalar.activation(act[:, f % 2, :], ffn_ps[f % 2][:, 0:HALF], ACT.Tanh,
                                     scale=half_gate[:, j:j + 1]).then_inc(tanh_done, 1)
                if j:
                    h_high(b, f - 1)

            def flush(b, hf):
                h_high(b, hf * NJ + NJ - 1)

            run(sc, dict(ln1=ln1, ln2=ln2, c=c, v=v_, proj=proj, stack=stack, maxrow=maxrow, st=st, norm=norm,
                         ffn=ffn, flush=flush))

        @block.vector
        def _(dve):
            def got(b, step):
                k = bank(step)
                dve.wait_ge(filled[k], fill(b, step))
                return k

            nc.vector.memset(kT[STACK:P, :, :].rearrange("p h s -> p (h s)"), 0.0).then_inc(init_own, 1)
            dve.wait_ge(init_own, 1)
            nc.vector.memset(kT[STACK:STACK + 2, :, :].rearrange("p h s -> p (h s)"), MAX_SHIFT).then_inc(tok_init, 1)
            nc.vector.memset(mtok[:].rearrange("p t h d -> p (t h d)"), 0.0).then_inc(tok_init, 1)
            nc.vector.memset(mhalf[:], -0.5).then_inc(tok_init, 1)
            dve.wait_ge(primed, 1)
            dve.wait_ge(tok_init, 3)

            def tied(b, key, ins):
                kind = key[0]
                ins.then_inc(own_sem[kind], 1)
                n = own_count[kind]
                dve.wait_ge(own_sem[kind], (b + 1) * n + key[1] + 1)

            def stats(b, kind, n, src, st_, mv_, t, eps):
                tied(b, (kind + "a", n), nc.vector.bn_stats(st_[:, t, :], src))
                nc.vector.memset(carry[:], 0.0)
                tied(b, (kind + "b", n), nc.vector.bn_aggr(mv_[:, t, :], st_[:, t, :]))
                row = dict(x=0, o=1, y=2, f=3)[kind]
                done = dict(x=x_var, o=oy_var, y=y_var, f=f_var)[kind]
                nc.vector.tensor_scalar(ve[:, row, t:t + 1], mv_[:, t, 1:2], eps, None, ALU.add).then_inc(done, 1)

            def ln1(b, t):
                k = t % 2
                dve.wait_ge(*of(x_in[k], 16 * T, b, 16 * (t // 2) + 15))
                stats(b, "x", t, xt[:, k, :], st1, mv1, t, EPS)
                dve.wait_ge(*of(x_rs, T, b, t))
                dve.wait_ge(*of(scr_free, NS, b, SCR[("ln1", t)] - 2))
                nc.vector.tensor_scalar(scr[:, k, :], xt[:, k, :], mv1[:, t, 0:1], rs[:, 0, t:t + 1],
                                        ALU.subtract, ALU.mult).then_inc(ln1_norm, 1)
                step = ("ln1", t)
                k2 = got(b, step)
                nc.vector.tensor_copy(xT[:, :, :, t * P:(t + 1) * P],
                                      work16[k2].rearrange("p (a k n) -> p a k n", a=2, k=KT)).then_inc(freed[k2], 1)

            def c(b, w):
                k = got(b, ("c", w))
                dve.wait_ge(*of(cv_hi, 2 + T, b, w))
                nc.vector.scalar_tensor_tensor(out=cT[:, w, 1, :], in0=work[k], scalar=c_bias[:, w:w + 1],
                                               in1=cT[:, w, 0, :], op0=ALU.add, op1=ALU.subtract).then_inc(freed[k], 1)

            def v_(b, t):
                k = got(b, ("v", t))
                dve.wait_ge(*of(cv_hi, 2 + T, b, 2 + t))
                nc.vector.scalar_tensor_tensor(out=v[:, t, 1, :], in0=work[k], scalar=V_SHIFT, in1=v[:, t, 0, :],
                                               op0=ALU.mult, op1=ALU.subtract).then_inc(freed[k], 1)

            def proj(b, g, w):
                step = ("proj", g, w)
                k = got(b, step)
                dve.wait_ge(*of(scr_free, NS, b, SCR[step] - 1))
                src = work[k].rearrange("p (t h d) -> p t h d", t=T, h=HG)
                for i in range(2):
                    table = rope[:, 2 * w + i].unsqueeze(2).to_broadcast([P, T, HG, DH])
                    ins = nc.vector.tensor_tensor(scr[:, i, :].rearrange("p (t h d) -> p t h d", t=T, h=HG),
                                                  src, table, ALU.mult)
                ins.then_inc(freed[k], 1)

            def stack(b, g, w, j):
                if w == 1:
                    return
                k = got(b, ("stack", g, w, j))
                nc.vector.tensor_copy(kT[0:STACK, 2 * j:2 * j + 2, :].rearrange("p h s -> p (h s)"),
                                      work16[k][0:STACK, :]).then_inc(freed[k], 1)

            def smax(b, g, h, t):
                k = got(b, ("smax", g, h, t))
                ins = nc.vector.reduce_max(mx[:, t, h:h + 1], work[k], AX.X)
                ins.then_inc(freed[k], 1)
                if (h, t) == (HG - 1, T - 1):
                    for q in range(2):
                        s = ("smax", g, h, t - q)
                        dve.wait_ge(freed[bank(s)], fill(b, s))
                    tied(b, ("m", g), nc.vector.tensor_scalar(mtok[:, :, :, 0], mx[:], -1.0 / MAX_SHIFT, None, ALU.mult))
                    nc.vector.scalar_tensor_tensor(out=mtok[:, :, :, 1], in0=mx[:], scalar=-1.0 / MAX_SHIFT,
                                                   in1=mtok[:, :, :, 0], op0=ALU.mult,
                                                   op1=ALU.subtract).then_inc(neg_max, 1)

            def norm(b, g):
                dve.wait_ge(*of(av_done, NAV, b, (g + 1) * 2 * T - 1))
                dve.wait_ge(*of(scr_free, NS, b, SCR[("norm", g)] - 1))
                tied(b, ("r", g), nc.vector.reciprocal(scr[:, 0, :], den_acc))
                nc.vector.tensor_tensor(scr[:, 0, :], o_acc, scr[:, 0, :], ALU.mult).then_inc(o_freed, 1)

            def o(b, t):
                step = ("o", t)
                k, kx = got(b, step), t % 2
                stats(b, "o", t, work[k], st2, mv2, t, eps_y[:, 0:1])
                dve.wait_ge(*of(oy_rs, T, b, t))
                tied(b, ("on", t), nc.vector.scalar_tensor_tensor(out=nmr[:, 1, t:t + 1], in0=mv2[:, t, 0:1], scalar=-1.0,
                                                                  in1=rs[:, 1, t:t + 1], op0=ALU.mult, op1=ALU.mult))
                dve.wait_ge(*of(x_in[kx], 16 * T, b, 16 * (T // 2 + t // 2) + 15))
                nc.vector.scalar_tensor_tensor(out=xt[:, kx, :], in0=work[k], scalar=rs[:, 1, t:t + 1],
                                               in1=xt[:, kx, :], op0=ALU.mult, op1=ALU.add).then_inc(freed[k], 1)
                dve.wait_ge(freed[k], fill(b, step))
                nc.vector.tensor_scalar(xt[:, kx, :], xt[:, kx, :], nmr[:, 1, t:t + 1], None,
                                        ALU.add).then_inc(y_ready, 1)
                dve.wait_ge(*of(y_ready, T, b, t))
                stats(b, "y", t, xt[:, kx, :], st3, mv3, t, EPS)
                dve.wait_ge(*of(y_rs, T, b, t))
                dve.wait_ge(*of(scr_free, NS, b, SCR[("ln2", t)] - (1 if t == 0 else 2)))
                nc.vector.tensor_scalar(scr[:, kx, :], xt[:, kx, :], mv3[:, t, 0:1], rs[:, 2, t:t + 1],
                                        ALU.subtract, ALU.mult).then_inc(ln2_norm, 1)

            def ln2(b, t):
                k = got(b, ("ln2", t))
                if t == 0:
                    dve.wait_ge(*of(f_filled, 2 * NJ, b - 1, 2 * NJ - 1))
                nc.vector.tensor_copy(x2T[:, :, :, t * P:(t + 1) * P],
                                      work16[k].rearrange("p (a k n) -> p a k n", a=2, k=KT)).then_inc(freed[k], 1)

            def ffn(b, f):
                k = f % 2
                dve.wait_ge(*of(tanh_done, 2 * NJ, b, f))
                tied(b, ("h", f), nc.vector.scalar_tensor_tensor(out=act[:, k, :], in0=act[:, k, :], scalar=1.0,
                                                                 in1=ffn_ps[k][:, 0:HALF], op0=ALU.add, op1=ALU.mult))
                nc.vector.scalar_tensor_tensor(out=act[:, k, :], in0=ffn_ps[k][:, HALF:2 * HALF], scalar=H_SHIFT,
                                               in1=act[:, k, :], op0=ALU.mult, op1=ALU.mult).then_inc(f_freed, 1)

            def fin(b, hf, tt):
                n = 2 * hf + tt
                dve.wait_ge(*of(down_done, 2 * NJ, b, hf * NJ + NJ - 1))
                stats(b, "f", n, down_ps[tt], st4, mv4, n, eps_f[:, 0:1])
                dve.wait_ge(*of(f_rs, T, b, n))
                tied(b, ("fn", n), nc.vector.scalar_tensor_tensor(out=nmr[:, 3, n:n + 1], in0=mv4[:, n, 0:1], scalar=-1.0,
                                                                  in1=rs[:, 3, n:n + 1], op0=ALU.mult, op1=ALU.mult))
                dve.wait_ge(*of(y_in[tt], 16 * T // 2, b, 16 * hf + 15))
                tied(b, ("fs", n), nc.vector.scalar_tensor_tensor(out=yt[:, tt, :], in0=down_ps[tt],
                                                                  scalar=rs[:, 3, n:n + 1], in1=yt[:, tt, :],
                                                                  op0=ALU.mult, op1=ALU.add))
                nc.vector.tensor_scalar(yt[:, tt, :], yt[:, tt, :], nmr[:, 3, n:n + 1], None,
                                        ALU.add).then_inc(fin_done, 1)

            run(dve, dict(ln1=ln1, ln2=ln2, c=c, v=v_, proj=proj, stack=stack, smax=smax, norm=norm, o=o,
                          ffn=ffn, fin=fin))

        @block.gpsimd
        def _(pool):
            pool.wait_ge(primed, 1)
            pool.wait_ge(tok_init, 3)

            def root(b, row, t, var, rs_):
                pool.wait_ge(*of(var, T, b, t))
                nc.gpsimd.tensor_tensor(rs[:, row, t:t + 1], ve[:, row, t:t + 1], mhalf[:], ALU.pow).then_inc(rs_, 1)

            def low(b, step, out_, in_, hi):
                pool.wait_ge(*of(part_hi, NS, b, SCR[step]))
                nc.gpsimd.tensor_tensor(out_, in_, hi, ALU.subtract).then_inc(scr_free, 1)

            def ln1(b, t):
                root(b, 0, t, x_var, x_rs)
                low(b, ("ln1", t), nhl[:, 1, :], scr[:, t % 2, :], nhl[:, 0, :])

            def o(b, t):
                root(b, 1, t, oy_var, oy_rs)
                root(b, 2, t, y_var, y_rs)

            def ln2(b, t):
                low(b, ("ln2", t), nhl[:, 1, :], scr[:, t % 2, :], nhl[:, 0, :])

            def proj(b, g, w):
                s = ("proj", g, w)
                k = bank(s)
                pool.wait_ge(freed[k], fill(b, s))
                a1 = scr[:, 0, :].rearrange("p (n r d) -> p n r d", r=2, d=DH // 2)
                a2 = scr[:, 1, :].rearrange("p (n r d) -> p n r d", r=2, d=DH // 2)
                nc.gpsimd.tensor_tensor(a1[:, :, 0, :], a1[:, :, 0, :], a2[:, :, 1, :], ALU.add)
                nc.gpsimd.tensor_tensor(a1[:, :, 1, :], a1[:, :, 1, :], a2[:, :, 0, :], ALU.add).then_inc(rope_sum, 1)
                pool.wait_ge(*of(part_hi, NS, b, SCR[s]))
                dst = tok[:, w].rearrange("p t h (r d) -> p (t h) r d", r=3)
                nc.gpsimd.tensor_tensor(dst[:, :, 1 + w, :], scr[:, 0, :].rearrange("p (n d) -> p n d", d=DH),
                                        dst[:, :, 0, :], ALU.subtract).then_inc(scr_free, 1)

            def prob_low(b, n):
                pool.wait_ge(*of(p_hi, NST, b, n))
                u, j = divmod(n, 2)
                dst = pr[:, u % 2, :, 2 * j:2 * j + 2, :]
                nc.gpsimd.tensor_tensor(dst[:, 1].rearrange("p h q -> p (h q)"), p32[:, n % 2, :],
                                        dst[:, 0].rearrange("p h q -> p (h q)"), ALU.subtract).then_inc(p_lo, 1)

            def st(b, g, u, j):
                n = (g * 2 * T + u) * 2 + j
                prob_low(b, n)

            def norm(b, g):
                low(b, ("norm", g), oT[:, g, 1, :], scr[:, 0, :], oT[:, g, 0, :])

            def h_low(b, f):
                pool.wait_ge(*of(h_hi, 2 * NJ, b, f))
                nc.gpsimd.tensor_tensor(hid[:, f % 2, 1, :], act[:, f % 2, :], hid[:, f % 2, 0, :],
                                        ALU.subtract).then_inc(h_lo, 1)

            def ffn(b, f):
                if f % NJ:
                    h_low(b, f - 1)

            def flush(b, hf):
                h_low(b, hf * NJ + NJ - 1)

            def fin(b, hf, tt):
                root(b, 3, 2 * hf + tt, f_var, f_rs)

            run(pool, dict(ln1=ln1, ln2=ln2, o=o, proj=proj, st=st, norm=norm, ffn=ffn, flush=flush, fin=fin))


_PRE = {"x": "L0_attn_x"} | {n: "L0_attn_" + n for n in (
    "W_dkv", "b_dkv", "W_dq", "b_dq", "W_uv", "b_uv", "W_qr", "b_qr", "W_kr", "b_kr", "W_o", "b_o")} | {
    n: "L0_ffn_" + n for n in ("SU_ug", "SU_dp", "Wscale_ug", "Wscale_dp", "W_up", "W_gate", "W_down")}


def constants():
    inv_freq = (1.0 / 10000.0 ** (np.arange(0, DH, 2, dtype=np.float32) / np.float32(DH))).astype(np.float32)
    freqs = np.arange(S, dtype=np.float32)[:, None] * inv_freq[None, :]
    cos, sin = np.cos(freqs), np.sin(freqs)
    cos2, sin2 = np.concatenate([cos, cos], 1), np.concatenate([sin, -sin], 1)
    rope = np.stack([cos2 * K_SHIFT, sin2 * K_SHIFT, cos2 * Q_SHIFT, sin2 * Q_SHIFT]).astype(np.float32)
    had = np.ones((1, 1), np.float32)
    while had.shape[0] < P:
        had = np.block([[had, had], [had, -had]])
    return {"rope": rope, "had": had.astype(np.float32)}


def kernel(**inputs):
    import concourse.bacc as _bacc
    from concourse.bass_utils import run_bass_kernel_spmd as _run

    nc = _bacc.Bacc("TRN2", target_bir_lowering=False, num_devices=1)
    arrays, args = {}, {}
    data = {n: np.ascontiguousarray(inputs[full]) for n, full in _PRE.items()} | constants()
    for name, x in data.items():
        arrays[f"in_{name}"] = x
        args[name] = nc.dram_tensor(f"in_{name}", x.shape, mybir.dt.from_np(x.dtype), kind="ExternalInput").ap()
    out = nc.dram_tensor("out_0", (NB, S, D), F32, kind="ExternalOutput").ap()
    y = nc.dram_tensor("y_mid", (NB, S, D), F32, kind="Internal").ap()
    program(nc, args, out, y)
    r = _run(nc, [arrays], core_ids=[0])
    return r.results[0]["out_0"]
```

```python
from contextlib import ExitStack

import numpy as np

import concourse.bass as bass
from concourse import mybir

F32 = mybir.dt.float32
F16 = mybir.dt.float16
U32 = mybir.dt.uint32
ALU = mybir.AluOpType
ACT = mybir.ActivationFunctionType
AX = mybir.AxisListType
RMAX = bass.bass_isa.ReduceOp.max

P = 128
NB, S, D = 8, 512, 512
T = S // P
KT = D // P
NH, DH = 16, 32
HG = P // DH
NG = NH // HG
INTER = 2048
NJ = INTER // P
HALF = 256
STACK = 3 * DH
EPS = 1e-5
PASSES = ((0, 0), (0, 1), (1, 0))

W_TOP = 16.0
D_TOP = 256.0
Q_SHIFT, K_SHIFT = 2.0 ** -17, 2.0 ** -4
V_SHIFT = 2.0 ** -12
MAX_SHIFT = 2.0 ** 15
H_SHIFT = 2.0 ** -14
ROW_SHIFT = 2.0 ** 12

A_KR, A_O, A_DQ, A_DKV, A_QR, A_UV, A_N = 0, 4, 8, 9, 10, 11, 12
(C_DQ, C_DKV, C_QR, C_KR, C_UV, C_O, C_UP, C_GATE, C_DOWN, C_SU, C_PROD, C_N) = range(12)


def ffn_steps():
    out = []
    for f in range(2 * NJ):
        out += [("gate", f), ("up", f)]
        if f >= 2:
            out.append(("down", f - 2))
        if f == NJ + 2:
            out += [("fin", 0, 0), ("fin", 0, 1)]
    return out + [("down", 2 * NJ - 2), ("down", 2 * NJ - 1), ("fin", 1, 0), ("fin", 1, 1)]


def att_steps():
    out = [("x", 0), ("x", 1), 1, ("xn", 0), ("xn", 1), 1, ("ln1", 0), ("x", 2), 1, ("ln1", 1), ("x", 3), 2,
           ("xn", 2), ("xn", 3), 2, ("ln1", 2), 1, ("ln1", 3), 1, ("c", 1), ("c", 0), 1]
    out += [("v", 0), ("v", 1), ("v", 2), ("v", 3), ("proj", 0, 0), ("proj", 0, 1), 2]
    for g in range(NG):
        out += [("stack", g, 0, 0), ("stack", g, 0, 1), 1, ("stack", g, 1, 0), ("stack", g, 1, 1), 1]
        for n in range(HG * T):
            out.append(("smax", g, n // T, n % T))
            if n % 3 == 2:
                out.append(1)
        out += [1, ("maxrow", g, 0), ("maxrow", g, 1)]
        for u in range(2 * T):
            out += [("st", g, u, 0), ("st", g, u, 1)]
            if g + 1 < NG and u in (1, 4):
                out.append(("proj", g + 1, u // 4))
            out.append(1)
            if u:
                out.append(("av", g, u - 1))
        out += [1, ("av", g, 2 * T - 1), ("norm", g)]
    out += [2, ("o", 0), ("o", 1), 1, ("oy", 0), ("oy", 1), 2, ("on", 0), ("on", 1), 2, ("ln2", 0), ("ln2", 1), "NEXT",
            ("o", 2), ("o", 3), 2, ("oy", 2), ("oy", 3), 2, ("on", 2), ("on", 3), 2, ("ln2", 2), 1, ("ln2", 3)]
    return out


def weave(plan, ffn, ahead):
    now, nxt = list(ffn[ahead:]), list(ffn[:ahead])
    out, pieces, delta = [], now, -1

    def take(n):
        while pieces and (n or pieces[0][0] == "fin"):
            n -= pieces[0][0] != "fin"
            out.append((delta, pieces.pop(0)))

    for step in plan:
        if step == "NEXT":
            take(len(pieces))
            pieces, delta = nxt, 0
        elif isinstance(step, int):
            take(step)
        else:
            out.append((0, step))
    assert not pieces
    return out


PLAN = att_steps()
ATT = [s for s in PLAN if isinstance(s, tuple)]
FFN = ffn_steps()
AHEAD = sum(s for s in PLAN[PLAN.index("NEXT"):] if isinstance(s, int))
BOTH = weave(PLAN, FFN, AHEAD)
HEAD = [(d, s) for d, s in BOTH if d == 0]
REST = [(0, s) for s in FFN[AHEAD:]]
ITEMS = [s for s in ATT if s[0] in ("ln1", "c", "v", "proj", "stack", "smax", "maxrow", "st", "o", "ln2")]
ITEM = {s: n for n, s in enumerate(ITEMS)}
IPB = len(ITEMS) // 2
assert len(ITEMS) % 2 == 0
SCRATCH = [s for s in ATT if s[0] in ("xn", "proj", "norm", "on")]
SCR = {s: n for n, s in enumerate(SCRATCH)}
NS = len(SCRATCH)
NST = NG * 2 * T * 2
NAV = NG * 2 * T


def setup_block(nc, a, ps, ps16, sem, sb, w):
    with ExitStack() as stage:
        def tmp(name, shape, dt=F32):
            return sb(name, shape, dt, stage)

        scale = w["scale"]
        nat = [tmp("nat0", [P, NJ, D]), tmp("nat1", [P, NJ, D])]
        fly = tmp("fly", [P, 2048])
        hadT = tmp("hadT", [P, 2048])
        ident32 = tmp("ident32", [P, P])
        had = tmp("had", [P, P])
        b512 = hadT[:, 0:1024].rearrange("p (i n) -> p i n", n=512)
        bo = fly[:, 0:512]
        b_uv_col = tmp("b_uv_col", [P, KT])
        b_uv_rep = fly[:, 512:1024].rearrange("p (k n) -> p k n", k=KT)
        c_raw = tmp("c_raw", [P, 2])
        su_ug = tmp("su_ug", [P, KT])
        su_dp = tmp("su_dp", [P, NJ])
        ws_up = tmp("ws_up", [P, NJ])
        ws_gate = tmp("ws_gate", [P, NJ])
        ws_dp = tmp("ws_dp", [P, KT])
        prod = tmp("prod", [P, NJ])
        m_own = tmp("m_own", [P, C_N])
        m_all = tmp("m_all", [P, C_N])
        m_bias = tmp("m_bias", [P, 8])
        bound = tmp("bound", [P, C_N])
        inv = tmp("inv", [P, C_N])
        one = tmp("one", [P, 8])
        up_f = tmp("up_f", [P, KT])
        gate_f = tmp("gate_f", [P, KT])
        down_f = tmp("down_f", [P, NJ])
        split32 = hadT[:, 1024:2048].rearrange("p (i n) -> p i n", n=512)

        s_attw, s_bias, s_small = sem("s_attw"), sem("s_bias"), sem("s_small")
        s_up, s_gate, s_down = sem("s_up"), sem("s_gate"), sem("s_down")
        s_own = sem("s_own")
        s_pool = sem("s_pool")
        s_max, s_maxall = sem("s_max"), sem("s_maxall")
        s_bo, s_bo_used = sem("s_bo"), sem("s_bo_used")
        s_scaled, s_hi, s_lo = sem("s_scaled"), sem("s_hi"), sem("s_lo")
        s_add, s_sub = sem("s_add"), sem("s_sub")
        s_tp, s_tc, s_hp = sem("s_tp"), sem("s_tc"), sem("s_hp")
        s_whi, s_wlo = sem("s_whi"), sem("s_wlo")
        s_factors = sem("s_factors")
        s_dscaled = sem("s_dscaled")

        attr = w["att_raw"]
        CH = 4
        chunks = [(m, c) for m in range(3) for c in range(CH)]

        def natural(m, c):
            return nat[m % 2][:, 4 * c:4 * c + 4, :].rearrange("p i n -> p (i n)")

        def stages(m):
            return [(1, 2), (2, 1)] if m < 2 else [(1, 8), (2, 4), (4, 2), (8, 1)]

        def halves(t, m, h):
            n = 2048 // (2 * h * P)
            r = t.rearrange("p (n r q) -> p n r q", n=n, r=2)
            return r[:, :, 0, :], r[:, :, 1, :]

        n_tr = 0
        block = stage.enter_context(nc.Block())

        @block.sync
        def _(sp):
            sp.dma_start(attr[:, A_KR:A_KR + KT, :], a["W_kr"].rearrange("(k p) n -> p k n", p=P)).then_inc(s_attw, 16)
            sp.dma_start(attr[:, A_O:A_O + KT, :], a["W_o"].rearrange("(k p) n -> p k n", p=P)).then_inc(s_attw, 16)
            sp.dma_start(attr[:, A_DQ, :].rearrange("p (k n) -> p k n", k=KT),
                         a["W_dq"].rearrange("(k p) n -> p k n", p=P)).then_inc(s_attw, 16)
            sp.dma_start(attr[:, A_DKV, :].rearrange("p (k n) -> p k n", k=KT),
                         a["W_dkv"].rearrange("(k p) n -> p k n", p=P)).then_inc(s_attw, 16)
            sp.dma_start(attr[:, A_QR, :], a["W_qr"]).then_inc(s_attw, 16)
            sp.dma_start(attr[:, A_UV, :], a["W_uv"]).then_inc(s_attw, 16)
            for m, (name, s) in enumerate((("W_up", s_up), ("W_gate", s_gate))):
                src = a[name].rearrange("(i p) n -> p i n", p=P)
                for c in range(CH):
                    sp.dma_start(nat[m][:, 4 * c:4 * c + 4, :], src[:, 4 * c:4 * c + 4, :]).then_inc(s, 16)
            src = a["W_down"].rearrange("(o p) n -> p o n", p=P)
            sp.wait_ge(s_tp, CH * 4)
            for c in range(CH):
                sp.dma_start(natural(2, c), src[:, c, :]).then_inc(s_down, 16)

        @block.gpsimd
        def _(pool):
            nc.gpsimd.memset(ident32[:], 0.0).then_inc(s_pool, 1)
            nc.gpsimd.memset(w["ident"][:], 0.0).then_inc(s_pool, 1)
            pool.wait_ge(s_pool, 2)
            for t in (ident32, w["ident"]):
                nc.gpsimd.affine_select(out=t[:], in_=t[:], compare_op=ALU.not_equal, fill=1.0, base=0,
                                        pattern=[[-1, P]], channel_multiplier=1).then_inc(s_pool, 1)
            pool.wait_ge(s_max, 1)
            nc.gpsimd.partition_all_reduce(m_all[:, 0:C_N], m_own[:, 0:C_N], P, RMAX).then_inc(s_maxall, 1)
            k = 0
            for n, (m, c) in enumerate(chunks):
                if m == 2 and c == 0:
                    pool.wait_ge(s_max, 2)
                    nc.gpsimd.partition_all_reduce(m_all[:, C_DOWN:C_DOWN + 1], m_own[:, C_DOWN:C_DOWN + 1], P,
                                                   RMAX).then_inc(s_maxall, 1)
                pool.wait_ge((s_up, s_gate, s_dscaled)[m], 16 * CH if m < 2 else c + 1)
                for i, (h, _) in enumerate(stages(m)):
                    src, dst = (natural(m, c), fly[:]) if i % 2 == 0 else (fly[:], natural(m, c))
                    if i:
                        pool.wait_ge(s_add, k)
                    elif n:
                        pool.wait_ge(s_add, k)
                    if k == 0:
                        pool.wait_ge(s_bo_used, 1)
                    x0, x1 = halves(src, m, h)
                    nc.gpsimd.tensor_tensor(halves(dst, m, h)[1], x0, x1, ALU.subtract).then_inc(s_sub, 1)
                    k += 1
                    pool.wait_ge(s_sub, k)

        @block.scalar
        def _(sc):
            for dst, name in ((b512[:, 0, :], "b_kr"), (b512[:, 1, :], "b_qr"), (bo, "b_o")):
                sc.dma_start(dst, a[name].partition_broadcast(P)).then_inc(s_bias, 16)
            small = [(b_uv_col[:], a["b_uv"].rearrange("(k p) -> p k", p=P)),
                     (c_raw[:, 0:1], a["b_dq"].rearrange("(p o) -> p o", o=1)),
                     (c_raw[:, 1:2], a["b_dkv"].rearrange("(p o) -> p o", o=1)),
                     (su_ug[:], a["SU_ug"].rearrange("(k p) -> p k", p=P)),
                     (su_dp[:], a["SU_dp"].rearrange("(k p) -> p k", p=P)),
                     (ws_up[:], a["Wscale_ug"][0:INTER].rearrange("(k p) -> p k", p=P)),
                     (ws_gate[:], a["Wscale_ug"][INTER:2 * INTER].rearrange("(k p) -> p k", p=P)),
                     (ws_dp[:], a["Wscale_dp"].rearrange("(k p) -> p k", p=P)),
                     (w["rope"][:], a["rope"].rearrange("i (t p) d -> p i t d", p=P)),
                     (had[:], a["had"])]
            for dst, src in small:
                sc.dma_start(dst, src, allow_slow_non_contiguous=True).then_inc(s_small, 16)
            for n in range(A_N):
                sc.wait_ge(s_scaled, n + 1)
                nc.scalar.activation(w["att_w"][:, n, 0, :], split32[:, n % 2, :], ACT.Copy).then_inc(s_hi, 1)
            hp = 0
            tc = 0

            def rotated(n_tiles, fac, dst):
                nonlocal hp
                for i in range(n_tiles):
                    sc.wait_ge(s_hp, hp + 1)
                    nc.scalar.activation(dst(i)[0], ps[:, 4 + hp % 4, :], ACT.Copy, scale=fac(i)).then_inc(s_whi, 1)
                    hp += 1

            sc.wait_ge(s_factors, 1)
            sc.wait_ge(s_lo, A_N)
            for n, (m, c) in enumerate(chunks):
                for q in range(4):
                    sc.wait_ge(s_tp, tc + 1)
                    if m < 2:
                        if tc >= 4:
                            sc.wait_ge(s_hp, tc - 3)
                        dst = hadT[:, q * 512:(q + 1) * 512]
                    else:
                        if tc == 32:
                            sc.wait_ge(s_wlo, 32)
                        dst = w["down_raw"][:, 4 * q:4 * q + 4, c * P:(c + 1) * P]
                    src = ps[:, tc % 4, :] if m < 2 else ps[:, tc % 4, :].rearrange("p (i n) -> p i n", i=4)
                    nc.scalar.activation(dst, src, ACT.Copy).then_inc(s_tc, 1)
                    tc += 1
                if m < 2:
                    wt, f = ((w["up_w"], up_f), (w["gate_w"], gate_f))[m]
                    rotated(4, lambda i: f[:, i:i + 1], lambda i: (wt[:, i, 0, c * 512:(c + 1) * 512],))
            sc.wait_ge(s_factors, 2)
            rotated(NJ, lambda i: down_f[:, i:i + 1], lambda i: (w["down_w"][:, i, 0, :],))

        @block.tensor
        def _(pe):
            pe.wait_ge(s_attw, 16 * 6)
            pe.wait_ge(s_bo, 1)
            for k in range(KT):
                mm = nc.tensor.matmul(ps[:, 0, :], b_uv_rep[:, k, :], attr[:, A_O + k, :], start=k == 0, stop=k == KT - 1)
            mm.then_inc(s_bo, 1)
            pe.wait_ge(s_pool, 4)
            pe.wait_ge(s_small, 16 * 10)
            pe.wait_ge(s_bo_used, 1)
            tr = hp = 0
            done = 0
            for m, c in chunks:
                done += len(stages(m))
                pe.wait_ge(s_add, done)
                pe.wait_ge(s_sub, done)
                for q in range(4):
                    if tr >= 4:
                        pe.wait_ge(s_tc, tr - 3)
                    for i in range(4):
                        blk = (i * 4 + q) if m < 2 else (q * 4 + i)
                        mm = nc.tensor.transpose(ps[:, tr % 4, i * P:(i + 1) * P], natural(m, c)[:, blk * P:(blk + 1) * P],
                                                 ident32[:])
                    mm.then_inc(s_tp, 1)
                    tr += 1
                if m < 2:
                    for q in range(4):
                        pe.wait_ge(s_tc, tr - 3 + q)
                        if hp >= 4:
                            pe.wait_ge(s_wlo, hp - 3)
                        nc.tensor.matmul(ps[:, 4 + hp % 4, :], had[:], hadT[:, q * 512:(q + 1) * 512],
                                         start=True, stop=True).then_inc(s_hp, 1)
                        hp += 1
            for i in range(NJ):
                pe.wait_ge(s_tc, 48)
                pe.wait_ge(s_wlo, hp - 3)
                nc.tensor.matmul(ps[:, 4 + hp % 4, :], had[:], w["down_raw"][:, i, :],
                                 start=True, stop=True).then_inc(s_hp, 1)
                hp += 1

        @block.vector
        def _(dve):
            chain = [0]

            def link(ins):
                chain[0] += 1
                ins.then_inc(s_own, 1)
                dve.wait_ge(s_own, chain[0])

            ts, tt_, stt = nc.vector.tensor_scalar, nc.vector.tensor_tensor, nc.vector.scalar_tensor_tensor

            def biggest(out_, in_, ax=AX.X):
                link(nc.vector.tensor_reduce(out_, in_, ax, ALU.max, apply_absolute_value=True))

            link(nc.vector.memset(w["ones"][:], 1.0))
            for pick, rows, value in ((w["pick_q"], (0, 64), ROW_SHIFT), (w["pick_k"], (32, 96), 1.0)):
                link(nc.vector.memset(pick[:], 0.0))
                for r in rows:
                    link(nc.vector.memset(pick[r:r + 1, :], value))
            link(nc.vector.memset(m_own[:], 0.0))
            link(nc.vector.memset(one[:], 1.0))

            dve.wait_ge(s_small, 16 * 10)
            dve.wait_ge(s_bias, 16 * 3)
            for k in range(KT):
                link(ts(b_uv_rep[:, k, :], had[:], 0.0, b_uv_col[:, k:k + 1], ALU.mult, ALU.add))
            nc.vector.memset(one[:], 1.0).then_inc(s_bo, 1)
            link(tt_(prod[:], ws_up[:], ws_gate[:], ALU.mult))
            link(tt_(prod[:], prod[:], su_dp[:], ALU.mult))

            dve.wait_ge(s_attw, 16 * 6)
            for col, lo, n in ((C_KR, A_KR, KT), (C_O, A_O, KT), (C_DQ, A_DQ, 1), (C_DKV, A_DKV, 1), (C_QR, A_QR, 1),
                               (C_UV, A_UV, 1)):
                biggest(m_own[:, col:col + 1], attr[:, lo:lo + n, :].rearrange("p k n -> p (k n)"))
            biggest(m_own[:, C_SU:C_SU + 1], su_ug[:])
            biggest(m_own[:, C_PROD:C_PROD + 1], prod[:])
            for i in range(2):
                biggest(m_bias[:, i:i + 1], b512[:, i, :])
            dve.wait_ge(s_up, 16 * CH)
            biggest(m_own[:, C_UP:C_UP + 1], nat[0][:].rearrange("p i n -> p (i n)"))
            biggest(m_own[:, C_DOWN:C_DOWN + 1], c_raw[:])
            dve.wait_ge(s_gate, 16 * CH)
            chain[0] += 1
            nc.vector.tensor_reduce(m_own[:, C_GATE:C_GATE + 1], nat[1][:].rearrange("p i n -> p (i n)"), AX.X, ALU.max,
                                    apply_absolute_value=True).then_inc(s_own, 1)
            dve.wait_ge(s_own, chain[0])
            nc.vector.tensor_copy(bound[:, 0:1], one[:, 0:1]).then_inc(s_max, 1)
            dve.wait_ge(s_maxall, 1)

            def scale_of(col, top):
                cs = slice(col, col + 1)
                link(ts(bound[:, cs], bound[:, cs], 1e-30, None, ALU.max))
                link(ts(bound[:, cs].bitcast(U32), bound[:, cs].bitcast(U32), 0x7F800000, None, ALU.bitwise_and))
                link(nc.vector.reciprocal(inv[:, cs], bound[:, cs]))
                link(ts(scale[:, cs], inv[:, cs], top, None, ALU.mult))

            def sc1(col):
                return scale[:, col:col + 1]

            for col in (C_DQ, C_DKV):
                link(stt(out=bound[:, col:col + 1], in0=m_all[:, C_DOWN:C_DOWN + 1], scalar=1.0 / D,
                         in1=m_all[:, col:col + 1], op0=ALU.mult, op1=ALU.max))
                scale_of(col, W_TOP)
            link(stt(out=bound[:, C_KR:C_KR + 1], in0=m_bias[:, 0:1], scalar=1.0 / D, in1=m_all[:, C_KR:C_KR + 1],
                     op0=ALU.mult, op1=ALU.max))
            scale_of(C_KR, W_TOP)
            link(ts(m_bias[:, 2:3], m_bias[:, 1:2], sc1(C_DQ), 2.0 ** -22, ALU.mult, ALU.mult))
            link(tt_(bound[:, C_QR:C_QR + 1], m_bias[:, 2:3], m_all[:, C_QR:C_QR + 1], ALU.max))
            scale_of(C_QR, W_TOP)
            link(nc.vector.tensor_copy(bound[:, C_UV:C_UV + 1], m_all[:, C_UV:C_UV + 1]))
            scale_of(C_UV, W_TOP)
            dve.wait_ge(s_bo, 2)
            link(tt_(bo, bo, ps[:, 0, :], ALU.add))
            biggest(m_bias[:, 3:4], bo)
            link(ts(m_bias[:, 4:5], sc1(C_DKV), sc1(C_UV), V_SHIFT, ALU.mult, ALU.mult))
            link(ts(m_bias[:, 5:6], m_bias[:, 3:4], m_bias[:, 4:5], 2.0 ** -22, ALU.mult, ALU.mult))
            link(tt_(bound[:, C_O:C_O + 1], m_bias[:, 5:6], m_all[:, C_O:C_O + 1], ALU.max))
            scale_of(C_O, W_TOP)
            for col in (C_UP, C_GATE):
                link(tt_(bound[:, col:col + 1], m_all[:, col:col + 1], m_all[:, C_SU:C_SU + 1], ALU.mult))
                scale_of(col, W_TOP)
            for f, col in ((up_f, C_UP), (gate_f, C_GATE)):
                link(ts(f[:], su_ug[:], sc1(col), float(D) ** -0.5, ALU.mult, ALU.mult))
            nc.vector.memset(one[:], 1.0).then_inc(s_factors, 1)
            link(tt_(w["c_bias"][:], c_raw[:], scale[:, C_DQ:C_DKV + 1], ALU.mult))

            def bias_rows(dst, src, rows, factor1, factor2):
                link(ts(src, src, factor1, factor2, ALU.mult, ALU.mult))
                link(nc.vector.tensor_copy(split32[:, 0, 0:256].bitcast(F16), src))
                link(tt_(split32[:, 0, 256:512].bitcast(F16), src, split32[:, 0, 0:256].bitcast(F16), ALU.subtract))
                for r, half in zip(rows, range(2)):
                    link(nc.vector.tensor_copy(dst[r:r + 1, :], split32[r:r + 1, 0, 256 * half:256 * half + 256].bitcast(F16)))

            link(nc.vector.memset(w["bias_qk"][:], 0.0))
            link(nc.vector.memset(w["bias_o"][:], 0.0))
            link(ts(m_bias[:, 6:7], sc1(C_DQ), sc1(C_QR), 1.0 / ROW_SHIFT, ALU.mult, ALU.mult))
            bias_rows(w["bias_qk"], b512[:, 0, :], (32, 96), sc1(C_KR), 1.0)
            bias_rows(w["bias_qk"], b512[:, 1, :], (0, 64), m_bias[:, 6:7], 1.0)
            link(ts(m_bias[:, 7:8], m_bias[:, 4:5], sc1(C_O), None, ALU.mult))
            bias_rows(w["bias_o"], bo, (0, 64), m_bias[:, 7:8], 1.0 / ROW_SHIFT)
            link(ts(w["eps_y"][:], m_bias[:, 7:8], m_bias[:, 7:8], EPS, ALU.mult, ALU.mult))
            link(ts(w["exp_scale"][:], bound[:, C_DQ:C_DQ + 1], bound[:, C_QR:C_QR + 1], 1.0 / W_TOP ** 2,
                    ALU.mult, ALU.mult))
            link(ts(w["exp_scale"][:], w["exp_scale"][:], bound[:, C_KR:C_KR + 1],
                    1.0 / (W_TOP * Q_SHIFT * K_SHIFT * DH ** 0.5), ALU.mult, ALU.mult))
            link(ts(w["half_gate"][:], ws_gate[:], bound[:, C_GATE:C_GATE + 1], 0.5 / W_TOP, ALU.mult, ALU.mult))
            nc.vector.memset(one[:], 1.0).then_inc(s_bo_used, 1)

            hi_n = 0
            for n in range(A_N):
                col = C_KR if n < A_O else C_O if n < A_DQ else {A_DQ: C_DQ, A_DKV: C_DKV, A_QR: C_QR, A_UV: C_UV}[n]
                ts(split32[:, n % 2, :], attr[:, n, :], sc1(col), None, ALU.mult).then_inc(s_scaled, 1)
                dve.wait_ge(s_scaled, n + 1)
                dve.wait_ge(s_hi, n + 1)
                nc.vector.tensor_tensor(w["att_w"][:, n, 1, :], split32[:, n % 2, :], w["att_w"][:, n, 0, :],
                                        ALU.subtract).then_inc(s_lo, 1)

            k = 0
            hp = 0

            def rotated_low(n_tiles, fac, dst):
                nonlocal hp
                for i in range(n_tiles):
                    hi, lo = dst(i)
                    dve.wait_ge(s_whi, hp + 1)
                    stt(out=lo, in0=ps[:, 4 + hp % 4, :], scalar=fac(i), in1=hi, op0=ALU.mult,
                        op1=ALU.subtract).then_inc(s_wlo, 1)
                    hp += 1

            def up_low(m, c):
                wt, f = ((w["up_w"], up_f), (w["gate_w"], gate_f))[m]
                cols = slice(c * 512, (c + 1) * 512)
                rotated_low(4, lambda i: f[:, i:i + 1], lambda i: (wt[:, i, 0, cols], wt[:, i, 1, cols]))

            for n, (m, c) in enumerate(chunks):
                if m == 2 and c == 0:
                    dve.wait_ge(s_down, 16 * CH)
                    for cc in range(CH):
                        link(ts(natural(2, cc), natural(2, cc), ws_dp[:, cc:cc + 1], None, ALU.mult))
                    biggest(m_own[:, C_DOWN:C_DOWN + 1], nat[0][:].rearrange("p i n -> p (i n)"))
                    nc.vector.memset(one[:], 1.0).then_inc(s_max, 1)
                    dve.wait_ge(s_maxall, 2)
                    link(tt_(bound[:, C_DOWN:C_DOWN + 1], m_all[:, C_DOWN:C_DOWN + 1], m_all[:, C_PROD:C_PROD + 1],
                             ALU.mult))
                    scale_of(C_DOWN, D_TOP)
                    link(ts(down_f[:], prod[:], sc1(C_DOWN), float(INTER) ** -0.5, ALU.mult, ALU.mult))
                    link(ts(m_bias[:, 2:3], sc1(C_UP), sc1(C_GATE), sc1(C_DOWN), ALU.mult, ALU.mult))
                    link(ts(m_bias[:, 2:3], m_bias[:, 2:3], 2.0 * H_SHIFT, None, ALU.mult))
                    link(ts(w["eps_f"][:], m_bias[:, 2:3], m_bias[:, 2:3], EPS, ALU.mult, ALU.mult))
                    nc.vector.memset(one[:], 1.0).then_inc(s_factors, 1)
                    nc.vector.memset(m_bias[:], 1.0).then_inc(s_dscaled, CH)
                for i, (h, _) in enumerate(stages(m)):
                    src, dst = (natural(m, c), fly[:]) if i % 2 == 0 else (fly[:], natural(m, c))
                    dve.wait_ge(s_sub, k)
                    dve.wait_ge(s_add, k)
                    x0, x1 = halves(src, m, h)
                    tt_(halves(dst, m, h)[0], x0, x1, ALU.add).then_inc(s_add, 1)
                    k += 1
                if 1 <= n and chunks[n - 1][0] < 2:
                    up_low(*chunks[n - 1])
            rotated_low(NJ, lambda i: down_f[:, i:i + 1], lambda i: (w["down_w"][:, i, 0, :], w["down_w"][:, i, 1, :]))



def program(nc, a, out, y_dram):
    ctx = ExitStack()
    with ctx:
        def sb(name, shape, dt, where=ctx):
            return where.enter_context(nc.sbuf_tensor(name, shape, dt))

        def sem(name):
            return ctx.enter_context(nc.semaphore(name))

        ps = ctx.enter_context(nc.psum_tensor("ps", [P, 8, 512], F32))
        ps16 = ps[:].bitcast(F16)

        att_w = sb("att_w", [P, A_N, 2, 512], F16)
        up_w = sb("up_w", [P, KT, 2, INTER], F16)
        gate_w = sb("gate_w", [P, KT, 2, INTER], F16)
        down_w = sb("down_w", [P, NJ, 2, D], F16)
        att_raw = att_w[:].rearrange("p a b n -> p (a b n)").bitcast(F32).rearrange("p (a n) -> p a n", a=A_N)
        down_raw = down_w[:].rearrange("p a b n -> p (a b n)").bitcast(F32).rearrange("p (a n) -> p a n", a=NJ)
        bias_qk = sb("bias_qk", [P, 512], F16)
        bias_o = sb("bias_o", [P, 512], F16)
        pick_q = sb("pick_q", [P, P], F16)
        pick_k = sb("pick_k", [P, P], F16)
        ident = sb("ident", [P, P], F16)
        ones = sb("ones", [P, DH], F16)
        rope = sb("rope", [P, 4, T, DH], F32)
        scale = sb("scale", [P, C_N], F32)
        c_bias = sb("c_bias", [P, 2], F32)
        exp_scale = sb("exp_scale", [P, 1], F32)
        eps_y = sb("eps_y", [P, 1], F32)
        eps_f = sb("eps_f", [P, 1], F32)
        half_gate = sb("half_gate", [P, NJ], F32)
        mhalf = sb("mhalf", [P, 1], F32)

        setup_block(nc, a, ps, ps16, sem, sb, dict(
            att_w=att_w, up_w=up_w, gate_w=gate_w, down_w=down_w, att_raw=att_raw, down_raw=down_raw,
            bias_qk=bias_qk, bias_o=bias_o, pick_q=pick_q, pick_k=pick_k, ident=ident, ones=ones, rope=rope,
            scale=scale, c_bias=c_bias, exp_scale=exp_scale, eps_y=eps_y, eps_f=eps_f,
            half_gate=half_gate, mhalf=mhalf))

        xt = sb("xt", [P, 2, D], F32)
        scr = sb("scr", [P, 2, D], F32)
        nhl = sb("nhl", [P, 2, D], F16)
        xT = sb("xT", [P, 2, KT, S], F16)
        cT = sb("cT", [P, 2, 2, S], F16)
        tok = sb("tok", [P, 2, T, HG, STACK], F16)
        mtok = sb("mtok", [P, T, HG, DH], F16)
        kT = sb("kT", [P, HG, S], F16)
        qT = sb("qT", [P, HG, S], F16)
        v = sb("v", [P, T, 2, D], F16)
        p32 = sb("p32", [P, 2, 512], F32)
        pr = sb("pr", [P, 2, 2, HG, HALF], F16)
        oT = sb("oT", [P, NG, 2, S], F16)
        x2T = sb("x2T", [P, 2, KT, S], F16)
        act = sb("act", [P, 2, HALF], F32)
        hid = sb("hid", [P, 2, 2, HALF], F16)
        yt = sb("yt", [P, 2, D], F32)
        st1 = sb("st1", [P, T, 6], F32)
        mv1 = sb("mv1", [P, T, 2], F32)
        st2 = sb("st2", [P, T, 6], F32)
        mv2 = sb("mv2", [P, T, 2], F32)
        st3 = sb("st3", [P, T, 6], F32)
        mv3 = sb("mv3", [P, T, 2], F32)
        st4 = sb("st4", [P, T, 6], F32)
        mv4 = sb("mv4", [P, T, 2], F32)
        ve = sb("ve", [P, 4, T], F32)
        rs = sb("rs", [P, 4, T], F32)
        nmr = sb("nmr", [P, 4, T], F32)
        carry = sb("carry", [P, 1], F32)
        mx = sb("mx", [P, T, HG], F32)

        work = [ps[:, 0, :], ps[:, 1, :]]
        work16 = [ps16[:, 0, :], ps16[:, 1, :]]
        o_acc, den_acc = ps[:, 2, :], ps[:, 3, :]
        ffn_ps = [ps[:, 4, :], ps[:, 5, :]]
        down_ps = [ps[:, 6, :], ps[:, 7, :]]

        credit = {}

        def counted(name, per_batch):
            s = sem(name)
            credit[name] = (s, per_batch)
            return s

        filled = [counted(f"filled{k}", IPB) for k in range(2)]
        freed = [counted(f"freed{k}", IPB) for k in range(2)]
        x_in = [counted(f"x_in{k}", 16 * T) for k in range(2)]
        ln1_norm = counted("ln1_norm", T)
        part_hi = counted("part_hi", NS)
        scr_free = counted("scr_free", NS)
        cv_hi = counted("cv_hi", 2 + T)
        x_var = counted("x_var", T)
        x_rs = counted("x_rs", T)
        rope_sum = counted("rope_sum", 2 * NG)
        neg_max = counted("neg_max", NG)
        p_hi = counted("p_hi", NST)
        p_lo = [counted(f"p_lo{j}", NAV) for j in range(2)]
        av_done = counted("av_done", NAV)
        o_freed = counted("o_freed", NG)
        oy_var = counted("oy_var", T)
        oy_rs = counted("oy_rs", T)
        y_var = counted("y_var", T)
        y_rs = counted("y_rs", T)
        y_ready = counted("y_ready", T)
        ln2_norm = counted("ln2_norm", T)
        y_out = [counted(f"y_out{k}", 16 * T // 2) for k in range(2)]
        f_filled = counted("f_filled", 2 * NJ)
        f_freed = counted("f_freed", 2 * NJ)
        tanh_done = counted("tanh_done", 2 * NJ)
        h_hi = counted("h_hi", 2 * NJ)
        h_lo = counted("h_lo", 2 * NJ)
        down_done = counted("down_done", 2 * NJ)
        f_var = counted("f_var", T)
        f_rs = counted("f_rs", T)
        fin_done = counted("fin_done", T)
        y_in = [counted(f"y_in{k}", 16 * T // 2) for k in range(2)]
        out_done = [counted(f"out_done{k}", 16 * T // 2) for k in range(2)]
        own_count = {f"{n}{i}": T for n in "xoyf" for i in "ab"} | dict(m=NG, r=NG, on=T, fn=T, fs=T, h=2 * NJ)
        own_sem = {n: counted(f"own_{n}", c) for n, c in own_count.items()}
        init_own = sem("init_own")
        primed = sem("primed")
        tok_init = sem("tok_init")

        def fill(b, step):
            return (b + 1) * IPB + ITEM[step] // 2 + 1

        def bank(step):
            return ITEM[step] % 2

        def of(sem_, per, b, n):
            return sem_, (b + 1) * per + n + 1

        block = ctx.enter_context(nc.Block())

        def run(eng, parts):
            def steps(b, plan):
                for delta, step in plan:
                    if step[0] in parts:
                        parts[step[0]](b + delta, *step[1:])

            steps(0, HEAD)
            with eng.Fori(1, NB) as b:
                steps(b, BOTH)
            steps(NB - 1, REST)

        @block.sync
        def _(sp):
            for s, n in credit.values():
                sp.sem_inc(s, n)
            sp.sem_inc(primed, 1)
            x_v = a["x"].rearrange("b (t p) d -> b t p d", p=P)
            y_v = y_dram.rearrange("b (t p) d -> b t p d", p=P)
            out_v = out.rearrange("b (t p) d -> b t p d", p=P)

            def load_x(b, r):
                k = r % 2
                if r < 2:
                    sp.wait_ge(*of(ln2_norm, T, b - 1, T - 2 + r))
                    sp.wait_ge(*of(y_out[k], 16 * T // 2, b - 1, 16 * T // 2 - 1))
                elif r < T + 2:
                    sp.wait_ge(*of(ln1_norm, T, b, r - 2))
                else:
                    sp.wait_ge(*of(ln2_norm, T, b, r - 2 - T))
                    sp.wait_ge(*of(y_out[k], 16 * T // 2, b, 15))
                sp.dma_start(xt[:, k, :], x_v[b, r % T]).then_inc(x_in[k], 16)

            def x(b, t):
                load_x(b, t)

            def proj(b, g, w):
                if g == 0 and w == 0:
                    load_x(b, T)
                    load_x(b, T + 1)

            def oy(b, t):
                sp.wait_ge(*of(y_ready, T, b, t))
                sp.dma_start(y_v[b, t], xt[:, t % 2, :]).then_inc(y_out[t % 2], 16)

            def on(b, t):
                if t < 2:
                    load_x(b, T + 2 + t)

            def gate(b, f):
                if f % NJ == 8:
                    for tt in range(2):
                        n = 2 * (f // NJ) + tt
                        sp.wait_ge(*of(y_out[tt], 16 * T // 2, b, 16 * (n // 2) + 15))
                        sp.wait_ge(*of(out_done[tt], 16 * T // 2, b, 16 * (n // 2) - 1))
                        sp.dma_start(yt[:, tt, :], y_v[b, n]).then_inc(y_in[tt], 16)

            def fin(b, hf, tt):
                sp.wait_ge(*of(fin_done, T, b, 2 * hf + tt))
                sp.dma_start(out_v[b, 2 * hf + tt], yt[:, tt, :]).then_inc(out_done[tt], 16)

            run(sp, dict(x=x, proj=proj, oy=oy, on=on, gate=gate, fin=fin))
            for k in range(2):
                sp.wait_ge(*of(out_done[k], 16 * T // 2, NB - 1, 16 * T // 2 - 1))
                sp.wait_ge(*of(y_out[k], 16 * T // 2, NB - 1, 16 * T // 2 - 1))

        @block.tensor
        def _(pe):
            pe.wait_ge(primed, 1)
            pe.wait_ge(tok_init, 3)

            def item(b, step, *after):
                k = bank(step)
                pe.wait_ge(freed[k], (b + 1) * IPB + ITEM[step] // 2)
                other = [ITEM[s] // 2 + 1 for s in after if bank(s) != k]
                if other:
                    pe.wait_ge(freed[1 - k], (b + 1) * IPB + max(other))
                return k

            def transposes(b, step, split):
                k = item(b, step)
                pe.wait_ge(*of(scr_free, NS, b, SCR[split]))
                for part in range(2):
                    for kt in range(KT):
                        col = (part * KT + kt) * P
                        mm = nc.tensor.transpose(work16[k][:, col:col + P], nhl[:, part, kt * P:(kt + 1) * P], ident[:])
                mm.then_inc(filled[k], 1)

            def ln1(b, t):
                transposes(b, ("ln1", t), ("xn", t))

            def ln2(b, t):
                transposes(b, ("ln2", t), ("on", t))

            def c(b, w):
                step = ("c", w)
                k = item(b, step, ("ln1", T - 2), ("ln1", T - 1))
                for kt in range(KT):
                    for n, (pw, px) in enumerate(PASSES):
                        mm = nc.tensor.matmul(work[k], att_w[:, A_DQ + w, pw, kt * P:(kt + 1) * P], xT[:, px, kt, :],
                                              start=kt == n == 0, stop=kt == KT - 1 and n == 2)
                mm.then_inc(filled[k], 1)

            def v_(b, t):
                step = ("v", t)
                k = item(b, step, ("c", 1))
                for n, (pc, pw) in enumerate(PASSES):
                    mm = nc.tensor.matmul(work[k], cT[:, 1, pc, t * P:(t + 1) * P], att_w[:, A_UV, pw, :],
                                          start=n == 0, stop=n == 2)
                mm.then_inc(filled[k], 1)

            def proj(b, g, w):
                step = ("proj", g, w)
                k = item(b, step, ("c", 0))
                cols = slice(g * P, (g + 1) * P)
                pick = (pick_k, pick_q)[w]
                nc.tensor.matmul(work[k].rearrange("p (t n) -> p t n", t=T), pick[:],
                                 bias_qk[:, cols].unsqueeze(1).to_broadcast([P, T, P]),
                                 start=True, stop=False, skip_group_check=True)
                for t in range(T):
                    for kt in range(KT if w == 0 else 1):
                        for pa, pw in PASSES:
                            lhs = xT[:, pa, kt, t * P:(t + 1) * P] if w == 0 else cT[:, 0, pa, t * P:(t + 1) * P]
                            tile = A_KR + kt if w == 0 else A_QR
                            mm = nc.tensor.matmul(work[k][:, t * P:(t + 1) * P], lhs, att_w[:, tile, pw, cols],
                                                  start=False, stop=True, skip_group_check=True)
                mm.then_inc(filled[k], 1)

            def stack(b, g, w, j):
                step = ("stack", g, w, j)
                k = item(b, step)
                pe.wait_ge(*of(scr_free, NS, b, SCR[("proj", g, w)]))
                for hh in range(2):
                    for t in range(T):
                        col = (hh * T + t) * P
                        mm = nc.tensor.transpose(work16[k][0:STACK, col:col + P], tok[:, w, t, 2 * j + hh, :], ident[:])
                mm.then_inc(filled[k], 1)

            def smax(b, g, h, t):
                step = ("smax", g, h, t)
                k = item(b, step, *[("stack", g, w, h // 2) for w in range(2) if h % 2 == 0 and t < 2])
                nc.tensor.matmul(work[k], qT[0:STACK, h, t * P:(t + 1) * P], kT[0:STACK, h, :],
                                 start=True, stop=True).then_inc(filled[k], 1)

            def maxrow(b, g, j):
                step = ("maxrow", g, j)
                k = item(b, step)
                pe.wait_ge(*of(neg_max, NG, b, g))
                for hh in range(2):
                    for t in range(T):
                        col = (hh * T + t) * P
                        mm = nc.tensor.transpose(work16[k][STACK:P, col:col + P], mtok[:, t, 2 * j + hh, :], ident[:])
                mm.then_inc(filled[k], 1)

            def st(b, g, u, j):
                step = ("st", g, u, j)
                k = item(b, step, *[("maxrow", g, j)] * (u == 0))
                kt, qh = divmod(u, 2)
                for hh in range(2):
                    mm = nc.tensor.matmul(work[k][:, hh * HALF:(hh + 1) * HALF], kT[:, 2 * j + hh, kt * P:(kt + 1) * P],
                                          qT[:, 2 * j + hh, qh * HALF:(qh + 1) * HALF], start=True, stop=True)
                mm.then_inc(filled[k], 1)

            def av(b, g, u):
                kt, qh = divmod(u, 2)
                n = g * 2 * T + u
                for j in range(2):
                    pe.wait_ge(*of(p_lo[j], NAV, b, n))
                if u == 0:
                    pe.wait_ge(*of(o_freed, NG, b, g - 1))
                    s = ("v", T - 1)
                    pe.wait_ge(freed[bank(s)], fill(b, s))
                q = slice(qh * HALF, (qh + 1) * HALF)
                for i, (pv, pp) in enumerate(PASSES):
                    for h in range(HG):
                        head = (g * HG + h) * DH
                        nc.tensor.matmul(o_acc[h * DH:(h + 1) * DH, q], v[:, kt, pv, head:head + DH],
                                         pr[:, n % 2, pp, h, :], start=u == 0 and i == 0, stop=True,
                                         skip_group_check=True)
                for pp in range(2):
                    for h in range(HG):
                        mm = nc.tensor.matmul(den_acc[h * DH:(h + 1) * DH, q], ones[:], pr[:, n % 2, pp, h, :],
                                              start=u == 0 and pp == 0, stop=True, skip_group_check=True)
                mm.then_inc(av_done, 1)

            def o(b, t):
                step = ("o", t)
                k = item(b, step)
                pe.wait_ge(*of(scr_free, NS, b, SCR[("norm", NG - 1)]))
                nc.tensor.matmul(work[k], pick_q[:], bias_o[:], start=True, stop=False)
                for g in range(NG):
                    for n, (po, pw) in enumerate(PASSES):
                        mm = nc.tensor.matmul(work[k], oT[:, g, po, t * P:(t + 1) * P], att_w[:, A_O + g, pw, :],
                                              start=False, stop=g == NG - 1 and n == 2)
                mm.then_inc(filled[k], 1)

            def down(b, f):
                hf, j = divmod(f, NJ)
                pe.wait_ge(*of(h_lo, 2 * NJ, b, f))
                for tt in range(2):
                    if j == 0:
                        pe.wait_ge(*of(fin_done, T, b, 2 * hf + tt - 2))
                    for n, (ph, pw) in enumerate(PASSES):
                        mm = nc.tensor.matmul(down_ps[tt], hid[:, f % 2, ph, tt * P:(tt + 1) * P], down_w[:, j, pw, :],
                                              start=j == n == 0, stop=j == NJ - 1 and n == 2)
                mm.then_inc(down_done, 1)

            def product(b, f, half, weights):
                hf, j = divmod(f, NJ)
                for kt in range(KT):
                    for n, (pw, px) in enumerate(PASSES):
                        mm = nc.tensor.matmul(ffn_ps[f % 2][:, half * HALF:(half + 1) * HALF],
                                              weights[:, kt, pw, j * P:(j + 1) * P],
                                              x2T[:, px, kt, hf * HALF:(hf + 1) * HALF],
                                              start=kt == n == 0, stop=kt == KT - 1 and n == 2)
                return mm

            def gate(b, f):
                if f % NJ == 0:
                    tiles = [("ln2", 2 * (f // NJ) + i) for i in range(2)]
                    for s in tiles:
                        pe.wait_ge(freed[bank(s)], fill(b, s))
                pe.wait_ge(*of(f_freed, 2 * NJ, b, f - 2))
                product(b, f, 0, gate_w)

            def up(b, f):
                product(b, f, 1, up_w).then_inc(f_filled, 1)

            run(pe, dict(ln1=ln1, ln2=ln2, c=c, v=v_, proj=proj, stack=stack, smax=smax, maxrow=maxrow,
                         st=st, av=av, o=o, gate=gate, up=up, down=down))

        @block.scalar
        def _(sc):
            sc.wait_ge(primed, 1)
            sc.wait_ge(tok_init, 3)

            def got(b, step):
                k = bank(step)
                sc.wait_ge(filled[k], fill(b, step))
                return k

            def high(out_, in_, b, step):
                nc.scalar.activation(out_, in_, ACT.Copy).then_inc(part_hi, 1)

            before = {}
            tiles = [st_ for st_ in ATT if st_[0] in ("ln1", "ln2")]
            for n, tile in enumerate(tiles):
                before[tile] = (tiles[n - 1], 0 if n else -1)

            def normed_high(b, t, name, ready):
                sc.wait_ge(*of(ready, T, b, t))
                s, delta = before[name, t]
                sc.wait_ge(filled[bank(s)], fill(b + delta, s))
                high(nhl[:, 0, :], scr[:, t % 2, :], b, None)

            def xn(b, t):
                normed_high(b, t, "ln1", ln1_norm)

            def on(b, t):
                normed_high(b, t, "ln2", ln2_norm)

            def c(b, w):
                step = ("c", w)
                k = got(b, step)
                nc.scalar.activation(cT[:, w, 0, :], work[k], ACT.Identity, bias=c_bias[:, w:w + 1]).then_inc(cv_hi, 1)

            def v_(b, t):
                k = got(b, ("v", t))
                sc.wait_ge(*of(av_done, NAV, b - 1, NAV - 1))
                nc.scalar.activation(v[:, t, 0, :], work[k], ACT.Copy, scale=V_SHIFT).then_inc(cv_hi, 1)

            def proj(b, g, w):
                sc.wait_ge(*of(rope_sum, 2 * NG, b, 2 * g + w))
                s, bb = (("stack", g - 1, w, 1), b) if g else (("stack", NG - 1, w, 1), b - 1)
                sc.wait_ge(filled[bank(s)], fill(bb, s))
                dst = tok[:, w].rearrange("p t h (r d) -> p (t h) r d", r=3)
                dst = dst[:, :, 0:3:2, :] if w == 0 else dst[:, :, 0:2, :]
                src = scr[:, 0, :].rearrange("p (n r d) -> p n r d", r=1, d=DH).to_broadcast([P, T * HG, 2, DH])
                nc.scalar.activation(dst, src, ACT.Copy).then_inc(part_hi, 1)

            def stack(b, g, w, j):
                if w == 0:
                    return
                step = ("stack", g, w, j)
                k = got(b, step)
                nc.scalar.activation(qT[0:STACK, 2 * j:2 * j + 2, :].rearrange("p h s -> p (h s)"),
                                     work16[k][0:STACK, :], ACT.Copy).then_inc(freed[k], 1)

            def maxrow(b, g, j):
                step = ("maxrow", g, j)
                k = got(b, step)
                nc.scalar.activation(qT[STACK:P, 2 * j:2 * j + 2, :].rearrange("p h s -> p (h s)"),
                                     work16[k][STACK:P, :], ACT.Copy).then_inc(freed[k], 1)

            def st(b, g, u, j):
                step = ("st", g, u, j)
                k = got(b, step)
                n = (g * 2 * T + u) * 2 + j
                sc.wait_ge(*of(p_lo[j], NAV, b, n // 2 - 1))
                nc.scalar.activation(p32[:, j, :], work[k], ACT.Exp, scale=exp_scale[:, 0:1]).then_inc(freed[k], 1)

            def norm(b, g):
                step = ("norm", g)
                sc.wait_ge(*of(o_freed, NG, b, g))
                s = ("o", T - 1)
                sc.wait_ge(filled[bank(s)], fill(b - 1, s))
                high(oT[:, g, 0, :], scr[:, 0, :], b, step)

            def h_high(b, f):
                sc.wait_ge(*of(f_freed, 2 * NJ, b, f))
                sc.wait_ge(*of(down_done, 2 * NJ, b, f - 2))
                nc.scalar.activation(hid[:, f % 2, 0, :], act[:, f % 2, :], ACT.Copy).then_inc(h_hi, 1)

            def up(b, f):
                sc.wait_ge(*of(f_filled, 2 * NJ, b, f))
                sc.wait_ge(*of(h_lo, 2 * NJ, b, f - 2))
                nc.scalar.activation(act[:, f % 2, :], ffn_ps[f % 2][:, 0:HALF], ACT.Tanh,
                                     scale=half_gate[:, f % NJ:f % NJ + 1]).then_inc(tanh_done, 1)
                if f:
                    h_high(b, f - 1)

            def down(b, f):
                if f == 2 * NJ - 2:
                    h_high(b, f + 1)

            run(sc, dict(xn=xn, on=on, c=c, v=v_, proj=proj, stack=stack, maxrow=maxrow, st=st, norm=norm,
                         up=up, down=down))

        @block.vector
        def _(dve):
            def got(b, step):
                k = bank(step)
                dve.wait_ge(filled[k], fill(b, step))
                return k

            nc.vector.memset(kT[STACK:P, :, :].rearrange("p h s -> p (h s)"), 0.0).then_inc(init_own, 1)
            dve.wait_ge(init_own, 1)
            nc.vector.memset(kT[STACK:STACK + 2, :, :].rearrange("p h s -> p (h s)"), MAX_SHIFT).then_inc(tok_init, 1)
            nc.vector.memset(mtok[:].rearrange("p t h d -> p (t h d)"), 0.0).then_inc(tok_init, 1)
            nc.vector.memset(mhalf[:], -0.5).then_inc(tok_init, 1)
            dve.wait_ge(primed, 1)
            dve.wait_ge(tok_init, 3)

            def tied(b, key, ins):
                kind = key[0]
                ins.then_inc(own_sem[kind], 1)
                n = own_count[kind]
                dve.wait_ge(own_sem[kind], (b + 1) * n + key[1] + 1)

            def stats(b, kind, n, src, st_, mv_, t, eps):
                tied(b, (kind + "a", n), nc.vector.bn_stats(st_[:, t, :], src))
                nc.vector.memset(carry[:], 0.0)
                tied(b, (kind + "b", n), nc.vector.bn_aggr(mv_[:, t, :], st_[:, t, :]))
                row = dict(x=0, o=1, y=2, f=3)[kind]
                done = dict(x=x_var, o=oy_var, y=y_var, f=f_var)[kind]
                nc.vector.tensor_scalar(ve[:, row, t:t + 1], mv_[:, t, 1:2], eps, None, ALU.add).then_inc(done, 1)

            def x(b, t):
                k = t % 2
                dve.wait_ge(*of(x_in[k], 16 * T, b, 16 * (t // 2) + 15))
                stats(b, "x", t, xt[:, k, :], st1, mv1, t, EPS)

            def xn(b, t):
                k = t % 2
                dve.wait_ge(*of(x_rs, T, b, t))
                dve.wait_ge(*of(scr_free, NS, b, SCR[("xn", t)] - 2))
                nc.vector.tensor_scalar(scr[:, k, :], xt[:, k, :], mv1[:, t, 0:1], rs[:, 0, t:t + 1],
                                        ALU.subtract, ALU.mult).then_inc(ln1_norm, 1)

            def ln1(b, t):
                k2 = got(b, ("ln1", t))
                nc.vector.tensor_copy(xT[:, :, :, t * P:(t + 1) * P],
                                      work16[k2].rearrange("p (a k n) -> p a k n", a=2, k=KT)).then_inc(freed[k2], 1)

            def c(b, w):
                k = got(b, ("c", w))
                dve.wait_ge(*of(cv_hi, 2 + T, b, w))
                nc.vector.scalar_tensor_tensor(out=cT[:, w, 1, :], in0=work[k], scalar=c_bias[:, w:w + 1],
                                               in1=cT[:, w, 0, :], op0=ALU.add, op1=ALU.subtract).then_inc(freed[k], 1)

            def v_(b, t):
                k = got(b, ("v", t))
                dve.wait_ge(*of(cv_hi, 2 + T, b, 2 + t))
                nc.vector.scalar_tensor_tensor(out=v[:, t, 1, :], in0=work[k], scalar=V_SHIFT, in1=v[:, t, 0, :],
                                               op0=ALU.mult, op1=ALU.subtract).then_inc(freed[k], 1)

            def proj(b, g, w):
                step = ("proj", g, w)
                k = got(b, step)
                dve.wait_ge(*of(scr_free, NS, b, SCR[step] - 1))
                src = work[k].rearrange("p (t h d) -> p t h d", t=T, h=HG)
                for i in range(2):
                    table = rope[:, 2 * w + i].unsqueeze(2).to_broadcast([P, T, HG, DH])
                    ins = nc.vector.tensor_tensor(scr[:, i, :].rearrange("p (t h d) -> p t h d", t=T, h=HG),
                                                  src, table, ALU.mult)
                ins.then_inc(freed[k], 1)

            def stack(b, g, w, j):
                if w == 1:
                    return
                k = got(b, ("stack", g, w, j))
                nc.vector.tensor_copy(kT[0:STACK, 2 * j:2 * j + 2, :].rearrange("p h s -> p (h s)"),
                                      work16[k][0:STACK, :]).then_inc(freed[k], 1)

            def smax(b, g, h, t):
                k = got(b, ("smax", g, h, t))
                ins = nc.vector.reduce_max(mx[:, t, h:h + 1], work[k], AX.X)
                ins.then_inc(freed[k], 1)
                if (h, t) == (HG - 1, T - 1):
                    for q in range(2):
                        s = ("smax", g, h, t - q)
                        dve.wait_ge(freed[bank(s)], fill(b, s))
                    tied(b, ("m", g), nc.vector.tensor_scalar(mtok[:, :, :, 0], mx[:], -1.0 / MAX_SHIFT, None, ALU.mult))
                    nc.vector.scalar_tensor_tensor(out=mtok[:, :, :, 1], in0=mx[:], scalar=-1.0 / MAX_SHIFT,
                                                   in1=mtok[:, :, :, 0], op0=ALU.mult,
                                                   op1=ALU.subtract).then_inc(neg_max, 1)

            def st(b, g, u, j):
                s = ("st", g, u, j)
                m = g * 2 * T + u
                dve.wait_ge(freed[bank(s)], fill(b, s))
                dve.wait_ge(*of(av_done, NAV, b, m - 2))
                dst = pr[:, m % 2, :, 2 * j:2 * j + 2, :]
                hi, lo = (dst[:, i].rearrange("p h q -> p (h q)") for i in range(2))
                nc.vector.tensor_copy(hi, p32[:, j, :]).then_inc(p_hi, 1)
                if j == 1:
                    dve.wait_ge(*of(p_hi, NST, b, 2 * m + 1))
                    nc.vector.tensor_tensor(lo, p32[:, j, :], hi, ALU.subtract).then_inc(p_lo[1], 1)

            def norm(b, g):
                dve.wait_ge(*of(av_done, NAV, b, (g + 1) * 2 * T - 1))
                dve.wait_ge(*of(scr_free, NS, b, SCR[("norm", g)] - 1))
                tied(b, ("r", g), nc.vector.reciprocal(scr[:, 0, :], den_acc))
                nc.vector.tensor_tensor(scr[:, 0, :], o_acc, scr[:, 0, :], ALU.mult).then_inc(o_freed, 1)

            def o(b, t):
                step = ("o", t)
                k, kx = got(b, step), t % 2
                stats(b, "o", t, work[k], st2, mv2, t, eps_y[:, 0:1])

            def oy(b, t):
                step = ("o", t)
                k, kx = bank(step), t % 2
                dve.wait_ge(*of(oy_rs, T, b, t))
                tied(b, ("on", t), nc.vector.scalar_tensor_tensor(out=nmr[:, 1, t:t + 1], in0=mv2[:, t, 0:1], scalar=-1.0,
                                                                  in1=rs[:, 1, t:t + 1], op0=ALU.mult, op1=ALU.mult))
                dve.wait_ge(*of(x_in[kx], 16 * T, b, 16 * (T // 2 + t // 2) + 15))
                nc.vector.scalar_tensor_tensor(out=xt[:, kx, :], in0=work[k], scalar=rs[:, 1, t:t + 1],
                                               in1=xt[:, kx, :], op0=ALU.mult, op1=ALU.add).then_inc(freed[k], 1)
                dve.wait_ge(freed[k], fill(b, step))
                nc.vector.tensor_scalar(xt[:, kx, :], xt[:, kx, :], nmr[:, 1, t:t + 1], None,
                                        ALU.add).then_inc(y_ready, 1)
                dve.wait_ge(*of(y_ready, T, b, t))
                stats(b, "y", t, xt[:, kx, :], st3, mv3, t, EPS)

            def on(b, t):
                kx = t % 2
                dve.wait_ge(*of(y_rs, T, b, t))
                dve.wait_ge(*of(scr_free, NS, b, SCR[("on", t)] - (1 if t == 0 else 2)))
                nc.vector.tensor_scalar(scr[:, kx, :], xt[:, kx, :], mv3[:, t, 0:1], rs[:, 2, t:t + 1],
                                        ALU.subtract, ALU.mult).then_inc(ln2_norm, 1)

            def ln2(b, t):
                k = got(b, ("ln2", t))
                if t % 2 == 0:
                    dve.wait_ge(*of(f_filled, 2 * NJ, b - 1, (t // 2 + 1) * NJ - 1))
                nc.vector.tensor_copy(x2T[:, :, :, t * P:(t + 1) * P],
                                      work16[k].rearrange("p (a k n) -> p a k n", a=2, k=KT)).then_inc(freed[k], 1)

            def up(b, f):
                k = f % 2
                dve.wait_ge(*of(tanh_done, 2 * NJ, b, f))
                tied(b, ("h", f), nc.vector.scalar_tensor_tensor(out=act[:, k, :], in0=act[:, k, :], scalar=1.0,
                                                                 in1=ffn_ps[k][:, 0:HALF], op0=ALU.add, op1=ALU.mult))
                nc.vector.scalar_tensor_tensor(out=act[:, k, :], in0=ffn_ps[k][:, HALF:2 * HALF], scalar=H_SHIFT,
                                               in1=act[:, k, :], op0=ALU.mult, op1=ALU.mult).then_inc(f_freed, 1)

            def fin(b, hf, tt):
                n = 2 * hf + tt
                dve.wait_ge(*of(down_done, 2 * NJ, b, hf * NJ + NJ - 1))
                stats(b, "f", n, down_ps[tt], st4, mv4, n, eps_f[:, 0:1])
                dve.wait_ge(*of(f_rs, T, b, n))
                tied(b, ("fn", n), nc.vector.scalar_tensor_tensor(out=nmr[:, 3, n:n + 1], in0=mv4[:, n, 0:1], scalar=-1.0,
                                                                  in1=rs[:, 3, n:n + 1], op0=ALU.mult, op1=ALU.mult))
                dve.wait_ge(*of(y_in[tt], 16 * T // 2, b, 16 * hf + 15))
                tied(b, ("fs", n), nc.vector.scalar_tensor_tensor(out=yt[:, tt, :], in0=down_ps[tt],
                                                                  scalar=rs[:, 3, n:n + 1], in1=yt[:, tt, :],
                                                                  op0=ALU.mult, op1=ALU.add))
                nc.vector.tensor_scalar(yt[:, tt, :], yt[:, tt, :], nmr[:, 3, n:n + 1], None,
                                        ALU.add).then_inc(fin_done, 1)

            run(dve, dict(x=x, xn=xn, ln1=ln1, on=on, ln2=ln2, c=c, v=v_, proj=proj, stack=stack, smax=smax, st=st,
                          norm=norm,                          o=o, oy=oy, up=up, fin=fin))

        @block.gpsimd
        def _(pool):
            pool.wait_ge(primed, 1)
            pool.wait_ge(tok_init, 3)

            def root(b, row, t, var, rs_):
                pool.wait_ge(*of(var, T, b, t))
                nc.gpsimd.tensor_tensor(rs[:, row, t:t + 1], ve[:, row, t:t + 1], mhalf[:], ALU.pow).then_inc(rs_, 1)

            def low(b, step, out_, in_, hi):
                pool.wait_ge(*of(part_hi, NS, b, SCR[step]))
                nc.gpsimd.tensor_tensor(out_, in_, hi, ALU.subtract).then_inc(scr_free, 1)

            def x(b, t):
                root(b, 0, t, x_var, x_rs)

            def xn(b, t):
                low(b, ("xn", t), nhl[:, 1, :], scr[:, t % 2, :], nhl[:, 0, :])

            def o(b, t):
                root(b, 1, t, oy_var, oy_rs)

            def oy(b, t):
                root(b, 2, t, y_var, y_rs)

            def on(b, t):
                low(b, ("on", t), nhl[:, 1, :], scr[:, t % 2, :], nhl[:, 0, :])

            def proj(b, g, w):
                s = ("proj", g, w)
                k = bank(s)
                pool.wait_ge(freed[k], fill(b, s))
                a1 = scr[:, 0, :].rearrange("p (n r d) -> p n r d", r=2, d=DH // 2)
                a2 = scr[:, 1, :].rearrange("p (n r d) -> p n r d", r=2, d=DH // 2)
                nc.gpsimd.tensor_tensor(a1[:, :, 0, :], a1[:, :, 0, :], a2[:, :, 1, :], ALU.add)
                nc.gpsimd.tensor_tensor(a1[:, :, 1, :], a1[:, :, 1, :], a2[:, :, 0, :], ALU.add).then_inc(rope_sum, 1)
                pool.wait_ge(*of(part_hi, NS, b, SCR[s]))
                dst = tok[:, w].rearrange("p t h (r d) -> p (t h) r d", r=3)
                nc.gpsimd.tensor_tensor(dst[:, :, 1 + w, :], scr[:, 0, :].rearrange("p (n d) -> p n d", d=DH),
                                        dst[:, :, 0, :], ALU.subtract).then_inc(scr_free, 1)

            def st(b, g, u, j):
                if j == 1:
                    return
                m = g * 2 * T + u
                pool.wait_ge(*of(p_hi, NST, b, 2 * m))
                dst = pr[:, m % 2, :, 0:2, :]
                nc.gpsimd.tensor_tensor(dst[:, 1].rearrange("p h q -> p (h q)"), p32[:, 0, :],
                                        dst[:, 0].rearrange("p h q -> p (h q)"), ALU.subtract).then_inc(p_lo[0], 1)

            def norm(b, g):
                low(b, ("norm", g), oT[:, g, 1, :], scr[:, 0, :], oT[:, g, 0, :])

            def h_low(b, f):
                pool.wait_ge(*of(h_hi, 2 * NJ, b, f))
                nc.gpsimd.tensor_tensor(hid[:, f % 2, 1, :], act[:, f % 2, :], hid[:, f % 2, 0, :],
                                        ALU.subtract).then_inc(h_lo, 1)

            def up(b, f):
                if f:
                    h_low(b, f - 1)

            def down(b, f):
                if f == 2 * NJ - 2:
                    h_low(b, f + 1)

            def fin(b, hf, tt):
                root(b, 3, 2 * hf + tt, f_var, f_rs)

            run(pool, dict(x=x, xn=xn, o=o, oy=oy, on=on, proj=proj, st=st, norm=norm, up=up, down=down, fin=fin))


_PRE = {"x": "L0_attn_x"} | {n: "L0_attn_" + n for n in (
    "W_dkv", "b_dkv", "W_dq", "b_dq", "W_uv", "b_uv", "W_qr", "b_qr", "W_kr", "b_kr", "W_o", "b_o")} | {
    n: "L0_ffn_" + n for n in ("SU_ug", "SU_dp", "Wscale_ug", "Wscale_dp", "W_up", "W_gate", "W_down")}


def constants():
    inv_freq = (1.0 / 10000.0 ** (np.arange(0, DH, 2, dtype=np.float32) / np.float32(DH))).astype(np.float32)
    freqs = np.arange(S, dtype=np.float32)[:, None] * inv_freq[None, :]
    cos, sin = np.cos(freqs), np.sin(freqs)
    cos2, sin2 = np.concatenate([cos, cos], 1), np.concatenate([sin, -sin], 1)
    rope = np.stack([cos2 * K_SHIFT, sin2 * K_SHIFT, cos2 * Q_SHIFT, sin2 * Q_SHIFT]).astype(np.float32)
    had = np.ones((1, 1), np.float32)
    while had.shape[0] < P:
        had = np.block([[had, had], [had, -had]])
    return {"rope": rope, "had": had.astype(np.float32)}


def kernel(**inputs):
    import concourse.bacc as _bacc
    from concourse.bass_utils import run_bass_kernel_spmd as _run

    nc = _bacc.Bacc("TRN2", target_bir_lowering=False, num_devices=1)
    arrays, args = {}, {}
    data = {n: np.ascontiguousarray(inputs[full]) for n, full in _PRE.items()} | constants()
    for name, x in data.items():
        arrays[f"in_{name}"] = x
        args[name] = nc.dram_tensor(f"in_{name}", x.shape, mybir.dt.from_np(x.dtype), kind="ExternalInput").ap()
    out = nc.dram_tensor("out_0", (NB, S, D), F32, kind="ExternalOutput").ap()
    y = nc.dram_tensor("y_mid", (NB, S, D), F32, kind="Internal").ap()
    program(nc, args, out, y)
    r = _run(nc, [arrays], core_ids=[0])
    return r.results[0]["out_0"]
```

```python
from contextlib import ExitStack

import numpy as np

import concourse.bass as bass
from concourse import mybir

F32 = mybir.dt.float32
F16 = mybir.dt.float16
U32 = mybir.dt.uint32
ALU = mybir.AluOpType
ACT = mybir.ActivationFunctionType
AX = mybir.AxisListType
RMAX = bass.bass_isa.ReduceOp.max

P = 128
NB, S, D = 8, 512, 512
T = S // P
KT = D // P
NH, DH = 16, 32
HG = P // DH
NG = NH // HG
INTER = 2048
NJ = INTER // P
HALF = 256
STACK = 3 * DH
EPS = 1e-5
PASSES = ((0, 0), (0, 1), (1, 0))

W_TOP = 16.0
D_TOP = 256.0
Q_SHIFT, K_SHIFT = 2.0 ** -17, 2.0 ** -4
V_SHIFT = 2.0 ** -12
MAX_SHIFT = 2.0 ** 15
H_SHIFT = 2.0 ** -14
ROW_SHIFT = 2.0 ** 12

A_KR, A_O, A_DQ, A_DKV, A_QR, A_UV, A_N = 0, 4, 8, 9, 10, 11, 12
(C_DQ, C_DKV, C_QR, C_KR, C_UV, C_O, C_UP, C_GATE, C_DOWN, C_SU, C_PROD, C_CB, C_N) = range(13)


def ffn_steps():
    out = []
    for f in range(2 * NJ):
        out += [("gate", f), ("up", f)]
        if f >= 2:
            out.append(("down", f - 2))
        if f == NJ + 2:
            out += [("fin", 0, 0), ("fin", 0, 1)]
    return out + [("down", 2 * NJ - 2), ("down", 2 * NJ - 1), ("fin", 1, 0), ("fin", 1, 1)]


FILL = (
    "01021000021000000000",
    "0201010101000102010101011011000010001001000001010",
    "0201010101000102010101011011000010001001000001010",
    "0201010101000102010101011011000010001001000001010",
    "12010101010001010102010100001002001000010001010",
    "01000000001111200",
)


def att_steps():
    start = [("x", 0), ("x", 1), ("xn", 0), ("xn", 1), ("ln1", 0), ("x", 2), ("ln1", 1), ("x", 3), ("xn", 2), ("xn", 3),
             ("ln1", 2), ("ln1", 3), ("c", 1), ("c", 0), ("proj", 0, 0), ("v", 0), ("v", 1), ("v", 2), ("v", 3), ("proj", 0, 1)]
    groups = []
    for g in range(NG):
        out = [("stack", g, w, j) for w in range(2) for j in range(2)]
        out += [("smax", g, n // T, n % T) for n in range(HG * T)]
        out += [("maxrow", g, 0), ("maxrow", g, 1)]
        for u in range(2 * T):
            out += [("st", g, u, 0), ("st", g, u, 1)]
            if g + 1 < NG and u in (1, 4):
                out.append(("proj", g + 1, u // 4))
            if u:
                out.append(("av", g, u - 1))
        groups.append(out + [("av", g, 2 * T - 1), ("norm", g)])
    end = [("o", 0), ("o", 1), ("oy", 0), ("oy", 1), ("on", 0), ("on", 1), ("ln2", 0), ("ln2", 1), "NEXT",
           ("o", 2), ("o", 3), ("oy", 2), ("oy", 3), ("on", 2), ("on", 3), ("ln2", 2), ("ln2", 3)]
    plan = []
    for steps, fill in zip([start] + groups + [end], FILL):
        assert len(steps) == len(fill)
        for step, n in zip(steps, fill):
            plan += [step, int(n)]
    return plan


def weave(plan, ffn, ahead):
    now, nxt = list(ffn[ahead:]), list(ffn[:ahead])
    out, pieces, delta = [], now, -1

    def take(n):
        while pieces and (n or pieces[0][0] == "fin"):
            n -= pieces[0][0] != "fin"
            out.append((delta, pieces.pop(0)))

    for step in plan:
        if step == "NEXT":
            take(len(pieces))
            pieces, delta = nxt, 0
        elif isinstance(step, int):
            take(step)
        else:
            out.append((0, step))
    assert not pieces
    return out


PLAN = att_steps()
ATT = [s for s in PLAN if isinstance(s, tuple)]
FFN = ffn_steps()
AHEAD = sum(s for s in PLAN[PLAN.index("NEXT"):] if isinstance(s, int))
BOTH = weave(PLAN, FFN, AHEAD)
HEAD = [(d, s) for d, s in BOTH if d == 0]
REST = [(0, s) for s in FFN[AHEAD:]]
ITEMS = [s for s in ATT if s[0] in ("ln1", "c", "v", "proj", "stack", "smax", "maxrow", "st", "o", "ln2")]
ITEM = {s: n for n, s in enumerate(ITEMS)}
IPB = len(ITEMS) // 2
assert len(ITEMS) % 2 == 0
SCRATCH = [s for s in ATT if s[0] in ("xn", "proj", "norm", "on")]
SCR = {s: n for n, s in enumerate(SCRATCH)}
NS = len(SCRATCH)
NST = NG * 2 * T * 2
NAV = NG * 2 * T


def setup_block(nc, a, ps, sem, sb, w):
    with ExitStack() as stage:
        def tmp(name, shape, dt=F32):
            return sb(name, shape, dt, stage)

        scale = w["scale"]
        nat = [tmp("nat0", [P, NJ, D]), tmp("nat1", [P, NJ, D])]
        fly = tmp("fly", [P, 2048])
        hadT = tmp("hadT", [P, 2048])
        ident32 = tmp("ident32", [P, P])
        had = tmp("had", [P, P])
        room = w["gate_w"][:].rearrange("p a b n -> p (a b n)").bitcast(F32)
        b512 = room[:, 0:1024].rearrange("p (i n) -> p i n", n=512)
        bo = room[:, 1024:1536]
        b_uv_col = tmp("b_uv_col", [P, KT])
        b_uv_rep = room[:, 1536:2048].rearrange("p (k n) -> p k n", k=KT)
        c_raw = tmp("c_raw", [P, 2])
        su_ug = tmp("su_ug", [P, KT])
        su_dp = tmp("su_dp", [P, NJ])
        ws_up = tmp("ws_up", [P, NJ])
        ws_gate = tmp("ws_gate", [P, NJ])
        ws_dp = tmp("ws_dp", [P, KT])
        prod = tmp("prod", [P, NJ])
        m_own = tmp("m_own", [P, C_N])
        m_all = tmp("m_all", [P, C_N])
        m_bias = tmp("m_bias", [P, 8])
        bound = tmp("bound", [P, C_N])
        inv = tmp("inv", [P, C_N])
        one = tmp("one", [P, 8])
        up_f = tmp("up_f", [P, KT])
        gate_f = tmp("gate_f", [P, KT])
        down_f = tmp("down_f", [P, NJ])
        split32 = nat[0][:, 0:2, :]
        parts = room[:, 2048:2560]

        s_attw, s_bias, s_small = sem("s_attw"), sem("s_bias"), sem("s_small")
        s_up, s_gate, s_down = sem("s_up"), sem("s_gate"), sem("s_down")
        s_own = sem("s_own")
        s_pool = sem("s_pool")
        s_upmax = sem("s_upmax")
        s_max, s_maxall = sem("s_max"), sem("s_maxall")
        s_bo, s_scales = sem("s_bo"), sem("s_scales")
        s_scaled, s_hi, s_lo = sem("s_scaled"), sem("s_hi"), sem("s_lo")
        s_add, s_sub = sem("s_add"), sem("s_sub")
        s_tp, s_tc, s_hp = sem("s_tp"), sem("s_tc"), sem("s_hp")
        s_whi, s_wlo = sem("s_whi"), sem("s_wlo")
        s_factors = sem("s_factors")
        s_dscaled = sem("s_dscaled")

        attr = w["att_raw"]
        down = w["down_raw"].rearrange("p a n -> p (a n)")
        down_t = nat[0]
        CH = 4
        chunks = [(m, c) for m in range(3) for c in range(CH)]

        def natural(m, c):
            if m == 2:
                return down[:, c * INTER:(c + 1) * INTER]
            return nat[m][:, 4 * c:4 * c + 4, :].rearrange("p i n -> p (i n)")

        def stages(m):
            return (1, 2) if m < 2 else (1, 2, 4, 8)

        def halves(t, m, h):
            n = 2048 // (2 * h * P)
            r = t.rearrange("p (n r q) -> p n r q", n=n, r=2)
            return r[:, :, 0, :], r[:, :, 1, :]

        def butterfly(m, c, i, h):
            src, dst = (natural(m, c), fly[:]) if i % 2 == 0 else (fly[:], natural(m, c))
            return *halves(src, m, h), *halves(dst, m, h), h * P // 3

        block = stage.enter_context(nc.Block())

        @block.sync
        def _(sp):
            sp.dma_start(attr[:, A_KR:A_KR + KT, :], a["W_kr"].rearrange("(k p) n -> p k n", p=P)).then_inc(s_attw, 16)
            sp.dma_start(attr[:, A_O:A_O + KT, :], a["W_o"].rearrange("(k p) n -> p k n", p=P)).then_inc(s_attw, 16)
            sp.dma_start(attr[:, A_DQ, :].rearrange("p (k n) -> p k n", k=KT),
                         a["W_dq"].rearrange("(k p) n -> p k n", p=P)).then_inc(s_attw, 16)
            sp.dma_start(attr[:, A_DKV, :].rearrange("p (k n) -> p k n", k=KT),
                         a["W_dkv"].rearrange("(k p) n -> p k n", p=P)).then_inc(s_attw, 16)
            sp.dma_start(attr[:, A_QR, :], a["W_qr"]).then_inc(s_attw, 16)
            sp.dma_start(attr[:, A_UV, :], a["W_uv"]).then_inc(s_attw, 16)
            for m, (name, s) in enumerate((("W_up", s_up), ("W_gate", s_gate))):
                src = a[name].rearrange("(i p) n -> p i n", p=P)
                for c in range(CH):
                    sp.dma_start(nat[m][:, 4 * c:4 * c + 4, :], src[:, 4 * c:4 * c + 4, :]).then_inc(s, 16)
            src = a["W_down"].rearrange("(o p) n -> p o n", p=P)
            for c in range(CH):
                sp.dma_start(natural(2, c), src[:, c, :]).then_inc(s_down, 16)

        @block.gpsimd
        def _(pool):
            nc.gpsimd.memset(ident32[:], 0.0).then_inc(s_pool, 1)
            nc.gpsimd.memset(w["ident"][:], 0.0).then_inc(s_pool, 1)
            pool.wait_ge(s_pool, 2)
            for t in (ident32, w["ident"]):
                nc.gpsimd.affine_select(out=t[:], in_=t[:], compare_op=ALU.not_equal, fill=1.0, base=0,
                                        pattern=[[-1, P]], channel_multiplier=1).then_inc(s_pool, 1)
            k = 0

            def differences(m, c):
                nonlocal k
                if m < 2:
                    pool.wait_ge((s_up, s_gate)[m], 16 * CH)
                if k == 0:
                    pool.wait_ge(s_upmax, 1)
                for i, h in enumerate(stages(m)):
                    if k:
                        pool.wait_ge(s_add, k)
                        pool.wait_ge(s_sub, k)
                    x0, x1, _, diff, cut = butterfly(m, c, i, h)
                    nc.gpsimd.tensor_tensor(diff[:, :, cut:], x0[:, :, cut:], x1[:, :, cut:],
                                            ALU.subtract).then_inc(s_sub, 1)
                    k += 1

            for c in range(CH):
                differences(0, c)
            pool.wait_ge(s_max, 1)
            nc.gpsimd.partition_all_reduce(m_all[:, 0:C_N], m_own[:, 0:C_N], P, RMAX).then_inc(s_maxall, 1)
            for c in range(CH):
                differences(1, c)
            for c in range(CH):
                for n in range(4 * c, min(4 * c + 4, A_N)):
                    pool.wait_ge(s_hi, n + 1)
                    nc.gpsimd.tensor_tensor(w["att_w"][:, n, 1, :], split32[:, n % 2, :], w["att_w"][:, n, 0, :],
                                            ALU.subtract).then_inc(s_lo, 1)
                differences(2, c)

        @block.scalar
        def _(sc):
            for dst, name in ((b512[:, 0, :], "b_kr"), (b512[:, 1, :], "b_qr"), (bo, "b_o")):
                sc.dma_start(dst, a[name].partition_broadcast(P)).then_inc(s_bias, 16)
            small = [(b_uv_col[:], a["b_uv"].rearrange("(k p) -> p k", p=P)),
                     (c_raw[:, 0:1], a["b_dq"].rearrange("(p o) -> p o", o=1)),
                     (c_raw[:, 1:2], a["b_dkv"].rearrange("(p o) -> p o", o=1)),
                     (su_ug[:], a["SU_ug"].rearrange("(k p) -> p k", p=P)),
                     (su_dp[:], a["SU_dp"].rearrange("(k p) -> p k", p=P)),
                     (ws_up[:], a["Wscale_ug"][0:INTER].rearrange("(k p) -> p k", p=P)),
                     (ws_gate[:], a["Wscale_ug"][INTER:2 * INTER].rearrange("(k p) -> p k", p=P)),
                     (ws_dp[:], a["Wscale_dp"].rearrange("(k p) -> p k", p=P)),
                     (w["rope"][:], a["rope"].rearrange("i (t p) d -> p i t d", p=P)),
                     (had[:], a["had"])]
            for dst, src in small:
                sc.dma_start(dst, src, allow_slow_non_contiguous=True).then_inc(s_small, 16)
            sc.wait_ge(s_down, 16 * CH)
            sc.wait_ge(s_small, 16 * 10)
            for c in range(CH):
                nc.scalar.activation(natural(2, c), natural(2, c), ACT.Copy, scale=ws_dp[:, c:c + 1]).then_inc(s_dscaled, 1)
            hp = 0
            tc = 0

            def rotated(n_tiles, fac, dst):
                nonlocal hp
                for i in range(n_tiles):
                    sc.wait_ge(s_hp, hp + 1)
                    nc.scalar.activation(dst(i), ps[:, 4 + hp % 4, :], ACT.Copy, scale=fac(i)).then_inc(s_whi, 1)
                    hp += 1

            sc.wait_ge(s_factors, 1)
            for n, (m, c) in enumerate(chunks):
                if n == 4:
                    sc.wait_ge(s_scales, 1)
                for q in range(4):
                    sc.wait_ge(s_tp, tc + 1)
                    if m == 2 and tc == 32:
                        sc.wait_ge(s_lo, A_N)
                    if m < 2:
                        if tc >= 4:
                            sc.wait_ge(s_hp, tc - 3)
                        dst = hadT[:, q * 512:(q + 1) * 512]
                    else:
                        dst = down_t[:, 4 * q:4 * q + 4, c * P:(c + 1) * P]
                    src = ps[:, tc % 4, :] if m < 2 else ps[:, tc % 4, :].rearrange("p (i n) -> p i n", i=4)
                    nc.scalar.activation(dst, src, ACT.Copy).then_inc(s_tc, 1)
                    tc += 1
                    if CH <= n < CH + 3:
                        i = (n - CH) * 4 + q
                        col = C_KR if i < A_O else C_O if i < A_DQ else (C_DQ, C_DKV, C_QR, C_UV)[i - A_DQ]
                        if i == 0:
                            sc.wait_ge(s_scales, 1)
                        if i >= 2:
                            sc.wait_ge(s_lo, i - 1)
                        nc.scalar.activation(split32[:, i % 2, :], attr[:, i, :], ACT.Copy,
                                             scale=scale[:, col:col + 1]).then_inc(s_scaled, 1)
                        sc.wait_ge(s_scaled, i + 1)
                        nc.scalar.activation(w["att_w"][:, i, 0, :], split32[:, i % 2, :], ACT.Copy).then_inc(s_hi, 1)
                if m < 2:
                    wt, f = ((w["up_w"], up_f), (w["gate_w"], gate_f))[m]
                    rotated(4, lambda i: f[:, i:i + 1], lambda i: wt[:, i, 0, c * 512:(c + 1) * 512])
            rotated(NJ, lambda i: down_f[:, i:i + 1], lambda i: w["down_w"][:, i, 0, :])

        @block.tensor
        def _(pe):
            pe.wait_ge(s_pool, 4)
            tr = hp = 0
            done = 0
            for m, c in chunks:
                done += len(stages(m))
                pe.wait_ge(s_add, done)
                pe.wait_ge(s_sub, done)
                for q in range(4):
                    if tr >= 4:
                        pe.wait_ge(s_tc, tr - 3)
                    for i in range(4):
                        blk = (i * 4 + q) if m < 2 else (q * 4 + i)
                        mm = nc.tensor.transpose(ps[:, tr % 4, i * P:(i + 1) * P], natural(m, c)[:, blk * P:(blk + 1) * P],
                                                 ident32[:])
                    mm.then_inc(s_tp, 1)
                    tr += 1
                if (m, c) == (0, 0):
                    pe.wait_ge(s_attw, 16 * 6)
                    pe.wait_ge(s_small, 16 * 10)
                    pe.wait_ge(s_bo, 1)
                    for k in range(KT):
                        mm = nc.tensor.matmul(ps[:, 7, :], b_uv_rep[:, k, :], attr[:, A_O + k, :], start=k == 0,
                                              stop=k == KT - 1)
                    mm.then_inc(s_bo, 1)
                if m < 2:
                    for q in range(4):
                        pe.wait_ge(s_tc, tr - 3 + q)
                        if hp == 3:
                            pe.wait_ge(s_scales, 1)
                        if hp >= 4:
                            pe.wait_ge(s_wlo, hp - 3)
                        nc.tensor.matmul(ps[:, 4 + hp % 4, :], had[:], hadT[:, q * 512:(q + 1) * 512],
                                         start=True, stop=True).then_inc(s_hp, 1)
                        hp += 1
            for i in range(NJ):
                pe.wait_ge(s_tc, 3 * 4 * CH)
                pe.wait_ge(s_wlo, hp - 3)
                nc.tensor.matmul(ps[:, 4 + hp % 4, :], had[:], down_t[:, i, :],
                                 start=True, stop=True).then_inc(s_hp, 1)
                hp += 1

        @block.vector
        def _(dve):
            chain = [0]

            def link(ins):
                chain[0] += 1
                ins.then_inc(s_own, 1)
                dve.wait_ge(s_own, chain[0])

            ts, tt_, stt = nc.vector.tensor_scalar, nc.vector.tensor_tensor, nc.vector.scalar_tensor_tensor

            def biggest(out_, in_, ax=AX.X):
                link(nc.vector.tensor_reduce(out_, in_, ax, ALU.max, apply_absolute_value=True))

            link(nc.vector.memset(w["ones"][:], 1.0))
            for pick, rows, value in ((w["pick_q"], (0, 64), ROW_SHIFT), (w["pick_k"], (32, 96), 1.0)):
                link(nc.vector.memset(pick[:], 0.0))
                for r in rows:
                    link(nc.vector.memset(pick[r:r + 1, :], value))
            link(nc.vector.memset(m_own[:], 0.0))
            link(nc.vector.memset(one[:], 1.0))

            dve.wait_ge(s_attw, 16 * 6)
            for col, lo, n in ((C_KR, A_KR, KT), (C_O, A_O, KT), (C_DQ, A_DQ, 1), (C_DKV, A_DKV, 1), (C_QR, A_QR, 1),
                               (C_UV, A_UV, 1)):
                biggest(m_own[:, col:col + 1], attr[:, lo:lo + n, :].rearrange("p k n -> p (k n)"))
            k = 0

            def sums(m, c):
                nonlocal k
                for i, h in enumerate(stages(m)):
                    dve.wait_ge(s_sub, k)
                    dve.wait_ge(s_add, k)
                    x0, x1, total, diff, cut = butterfly(m, c, i, h)
                    tt_(diff[:, :, 0:cut], x0[:, :, 0:cut], x1[:, :, 0:cut], ALU.subtract)
                    tt_(total, x0, x1, ALU.add).then_inc(s_add, 1)
                    k += 1

            dve.wait_ge(s_up, 16 * CH)
            biggest(m_own[:, C_UP:C_UP + 1], nat[0][:].rearrange("p i n -> p (i n)"))
            nc.vector.memset(one[:], 1.0).then_inc(s_upmax, 1)
            for c in range(CH):
                sums(0, c)
            dve.wait_ge(s_gate, 16 * CH)
            biggest(m_own[:, C_GATE:C_GATE + 1], nat[1][:].rearrange("p i n -> p (i n)"))
            dve.wait_ge(s_small, 16 * 10)
            dve.wait_ge(s_bias, 16 * 3)
            for i in range(KT):
                link(ts(b_uv_rep[:, i, :], had[:], 0.0, b_uv_col[:, i:i + 1], ALU.mult, ALU.add))
            nc.vector.memset(one[:], 1.0).then_inc(s_bo, 1)
            link(tt_(prod[:], ws_up[:], ws_gate[:], ALU.mult))
            link(tt_(prod[:], prod[:], su_dp[:], ALU.mult))

            biggest(m_own[:, C_SU:C_SU + 1], su_ug[:])
            biggest(m_own[:, C_PROD:C_PROD + 1], prod[:])
            biggest(m_own[:, C_CB:C_CB + 1], c_raw[:])
            for i in range(2):
                biggest(m_bias[:, i:i + 1], b512[:, i, :])
            dve.wait_ge(s_dscaled, CH)
            biggest(m_own[:, C_DOWN:C_DOWN + 1], down)
            nc.vector.memset(one[:], 1.0).then_inc(s_max, 1)
            dve.wait_ge(s_maxall, 1)

            def scale_of(col, top):
                cs = slice(col, col + 1)
                link(ts(bound[:, cs], bound[:, cs], 1e-30, None, ALU.max))
                link(ts(bound[:, cs].bitcast(U32), bound[:, cs].bitcast(U32), 0x7F800000, None, ALU.bitwise_and))
                link(nc.vector.reciprocal(inv[:, cs], bound[:, cs]))
                link(ts(scale[:, cs], inv[:, cs], top, None, ALU.mult))

            def sc1(col):
                return scale[:, col:col + 1]

            for col, other in ((C_UP, C_SU), (C_GATE, C_SU), (C_DOWN, C_PROD)):
                link(tt_(bound[:, col:col + 1], m_all[:, col:col + 1], m_all[:, other:other + 1], ALU.mult))
                scale_of(col, D_TOP if col == C_DOWN else W_TOP)
            for f, src, col, n in ((up_f, su_ug, C_UP, D), (gate_f, su_ug, C_GATE, D), (down_f, prod, C_DOWN, INTER)):
                link(ts(f[:], src[:], sc1(col), float(n) ** -0.5, ALU.mult, ALU.mult))
            nc.vector.memset(one[:], 1.0).then_inc(s_factors, 1)
            link(ts(m_bias[:, 2:3], sc1(C_UP), sc1(C_GATE), sc1(C_DOWN), ALU.mult, ALU.mult))
            link(ts(m_bias[:, 2:3], m_bias[:, 2:3], 2.0 * H_SHIFT, None, ALU.mult))
            link(ts(w["eps_f"][:], m_bias[:, 2:3], m_bias[:, 2:3], EPS, ALU.mult, ALU.mult))
            for col in (C_DQ, C_DKV):
                link(stt(out=bound[:, col:col + 1], in0=m_all[:, C_CB:C_CB + 1], scalar=1.0 / D,
                         in1=m_all[:, col:col + 1], op0=ALU.mult, op1=ALU.max))
                scale_of(col, W_TOP)
            link(stt(out=bound[:, C_KR:C_KR + 1], in0=m_bias[:, 0:1], scalar=1.0 / D, in1=m_all[:, C_KR:C_KR + 1],
                     op0=ALU.mult, op1=ALU.max))
            scale_of(C_KR, W_TOP)
            link(ts(m_bias[:, 2:3], m_bias[:, 1:2], sc1(C_DQ), 2.0 ** -22, ALU.mult, ALU.mult))
            link(tt_(bound[:, C_QR:C_QR + 1], m_bias[:, 2:3], m_all[:, C_QR:C_QR + 1], ALU.max))
            scale_of(C_QR, W_TOP)
            link(nc.vector.tensor_copy(bound[:, C_UV:C_UV + 1], m_all[:, C_UV:C_UV + 1]))
            scale_of(C_UV, W_TOP)
            dve.wait_ge(s_bo, 2)
            link(tt_(bo, bo, ps[:, 7, :], ALU.add))
            biggest(m_bias[:, 3:4], bo)
            link(ts(m_bias[:, 4:5], sc1(C_DKV), sc1(C_UV), V_SHIFT, ALU.mult, ALU.mult))
            link(ts(m_bias[:, 5:6], m_bias[:, 3:4], m_bias[:, 4:5], 2.0 ** -22, ALU.mult, ALU.mult))
            link(tt_(bound[:, C_O:C_O + 1], m_bias[:, 5:6], m_all[:, C_O:C_O + 1], ALU.max))
            scale_of(C_O, W_TOP)
            link(tt_(w["c_bias"][:], c_raw[:], scale[:, C_DQ:C_DKV + 1], ALU.mult))

            def bias_rows(dst, src, rows, factor1, factor2):
                link(ts(src, src, factor1, factor2, ALU.mult, ALU.mult))
                link(nc.vector.tensor_copy(parts[:, 0:256].bitcast(F16), src))
                link(tt_(parts[:, 256:512].bitcast(F16), src, parts[:, 0:256].bitcast(F16), ALU.subtract))
                for r, half in zip(rows, range(2)):
                    link(nc.vector.tensor_copy(dst[r:r + 1, :], parts[r:r + 1, 256 * half:256 * half + 256].bitcast(F16)))

            link(nc.vector.memset(w["bias_qk"][:], 0.0))
            link(nc.vector.memset(w["bias_o"][:], 0.0))
            link(ts(m_bias[:, 6:7], sc1(C_DQ), sc1(C_QR), 1.0 / ROW_SHIFT, ALU.mult, ALU.mult))
            bias_rows(w["bias_qk"], b512[:, 0, :], (32, 96), sc1(C_KR), 1.0)
            bias_rows(w["bias_qk"], b512[:, 1, :], (0, 64), m_bias[:, 6:7], 1.0)
            link(ts(m_bias[:, 7:8], m_bias[:, 4:5], sc1(C_O), None, ALU.mult))
            bias_rows(w["bias_o"], bo, (0, 64), m_bias[:, 7:8], 1.0 / ROW_SHIFT)
            link(ts(w["eps_y"][:], m_bias[:, 7:8], m_bias[:, 7:8], EPS, ALU.mult, ALU.mult))
            link(ts(w["exp_scale"][:], bound[:, C_DQ:C_DQ + 1], bound[:, C_QR:C_QR + 1], 1.0 / W_TOP ** 2,
                    ALU.mult, ALU.mult))
            link(ts(w["exp_scale"][:], w["exp_scale"][:], bound[:, C_KR:C_KR + 1],
                    1.0 / (W_TOP * Q_SHIFT * K_SHIFT * DH ** 0.5), ALU.mult, ALU.mult))
            link(ts(w["half_gate"][:], ws_gate[:], bound[:, C_GATE:C_GATE + 1], 0.5 / W_TOP, ALU.mult, ALU.mult))
            nc.vector.memset(one[:], 1.0).then_inc(s_scales, 1)
            hp = 0

            def rotated_low(n_tiles, fac, dst):
                nonlocal hp
                for i in range(n_tiles):
                    hi, lo = dst(i)
                    dve.wait_ge(s_whi, hp + 1)
                    stt(out=lo, in0=ps[:, 4 + hp % 4, :], scalar=fac(i), in1=hi, op0=ALU.mult,
                        op1=ALU.subtract).then_inc(s_wlo, 1)
                    hp += 1

            def up_low(m, c):
                wt, f = ((w["up_w"], up_f), (w["gate_w"], gate_f))[m]
                cols = slice(c * 512, (c + 1) * 512)
                rotated_low(4, lambda i: f[:, i:i + 1], lambda i: (wt[:, i, 0, cols], wt[:, i, 1, cols]))

            for c in range(2):
                sums(1, c)
                up_low(0, c)
            sums(1, 2)
            sums(1, 3)
            up_low(0, 2)
            up_low(0, 3)
            for c in range(CH):
                sums(2, c)
                up_low(1, c)
            rotated_low(NJ, lambda i: down_f[:, i:i + 1], lambda i: (w["down_w"][:, i, 0, :], w["down_w"][:, i, 1, :]))


def program(nc, a, out, y_dram):
    ctx = ExitStack()
    with ctx:
        def sb(name, shape, dt, where=ctx):
            return where.enter_context(nc.sbuf_tensor(name, shape, dt))

        def sem(name):
            return ctx.enter_context(nc.semaphore(name))

        ps = ctx.enter_context(nc.psum_tensor("ps", [P, 8, 512], F32))
        ps16 = ps[:].bitcast(F16)

        att_w = sb("att_w", [P, A_N, 2, 512], F16)
        up_w = sb("up_w", [P, KT, 2, INTER], F16)
        gate_w = sb("gate_w", [P, KT, 2, INTER], F16)
        down_w = sb("down_w", [P, NJ, 2, D], F16)
        att_raw = att_w[:].rearrange("p a b n -> p (a b n)").bitcast(F32).rearrange("p (a n) -> p a n", a=A_N)
        down_raw = down_w[:].rearrange("p a b n -> p (a b n)").bitcast(F32).rearrange("p (a n) -> p a n", a=NJ)
        bias_qk = sb("bias_qk", [P, 512], F16)
        bias_o = sb("bias_o", [P, 512], F16)
        pick_q = sb("pick_q", [P, P], F16)
        pick_k = sb("pick_k", [P, P], F16)
        ident = sb("ident", [P, P], F16)
        ones = sb("ones", [P, DH], F16)
        rope = sb("rope", [P, 4, T, DH], F32)
        scale = sb("scale", [P, C_N], F32)
        c_bias = sb("c_bias", [P, 2], F32)
        exp_scale = sb("exp_scale", [P, 1], F32)
        eps_y = sb("eps_y", [P, 1], F32)
        eps_f = sb("eps_f", [P, 1], F32)
        half_gate = sb("half_gate", [P, NJ], F32)
        mhalf = sb("mhalf", [P, 1], F32)

        setup_block(nc, a, ps, sem, sb, dict(
            att_w=att_w, up_w=up_w, gate_w=gate_w, down_w=down_w, att_raw=att_raw, down_raw=down_raw,
            bias_qk=bias_qk, bias_o=bias_o, pick_q=pick_q, pick_k=pick_k, ident=ident, ones=ones, rope=rope,
            scale=scale, c_bias=c_bias, exp_scale=exp_scale, eps_y=eps_y, eps_f=eps_f,
            half_gate=half_gate, mhalf=mhalf))

        xt = sb("xt", [P, 2, D], F32)
        scr = sb("scr", [P, 2, D], F32)
        nhl = sb("nhl", [P, 2, D], F16)
        xT = sb("xT", [P, 2, KT, S], F16)
        cT = sb("cT", [P, 2, 2, S], F16)
        tok = sb("tok", [P, 2, T, HG, STACK], F16)
        mtok = sb("mtok", [P, T, HG, DH], F16)
        kT = sb("kT", [P, HG, S], F16)
        qT = sb("qT", [P, HG, S], F16)
        v = sb("v", [P, T, 2, D], F16)
        p32 = sb("p32", [P, 2, 512], F32)
        pr = sb("pr", [P, 2, 2, HG, HALF], F16)
        oT = sb("oT", [P, NG, 2, S], F16)
        x2T = sb("x2T", [P, 2, KT, S], F16)
        act = sb("act", [P, 2, HALF], F32)
        hid = sb("hid", [P, 2, 2, HALF], F16)
        yt = sb("yt", [P, 2, D], F32)
        st1 = sb("st1", [P, T, 6], F32)
        mv1 = sb("mv1", [P, T, 2], F32)
        st2 = sb("st2", [P, T, 6], F32)
        mv2 = sb("mv2", [P, T, 2], F32)
        st3 = sb("st3", [P, T, 6], F32)
        mv3 = sb("mv3", [P, T, 2], F32)
        st4 = sb("st4", [P, T, 6], F32)
        mv4 = sb("mv4", [P, T, 2], F32)
        ve = sb("ve", [P, 4, T], F32)
        rs = sb("rs", [P, 4, T], F32)
        nmr = sb("nmr", [P, 4, T], F32)
        carry = sb("carry", [P, 1], F32)
        mx = sb("mx", [P, T, HG], F32)

        work = [ps[:, 0, :], ps[:, 1, :]]
        work16 = [ps16[:, 0, :], ps16[:, 1, :]]
        o_acc, den_acc = ps[:, 2, :], ps[:, 3, :]
        ffn_ps = [ps[:, 4, :], ps[:, 5, :]]
        down_ps = [ps[:, 6, :], ps[:, 7, :]]

        credit = {}

        def counted(name, per_batch):
            s = sem(name)
            credit[name] = (s, per_batch)
            return s

        filled = [counted(f"filled{k}", IPB) for k in range(2)]
        freed = [counted(f"freed{k}", IPB) for k in range(2)]
        x_in = [counted(f"x_in{k}", 16 * T) for k in range(2)]
        part_hi = counted("part_hi", NS)
        scr_free = counted("scr_free", NS)
        cv_hi = counted("cv_hi", 2 + T)
        x_var = counted("x_var", T)
        x_rs = counted("x_rs", T)
        rope_sum = counted("rope_sum", 2 * NG)
        neg_max = counted("neg_max", NG)
        p_hi = counted("p_hi", NST)
        p_lo = [counted(f"p_lo{j}", NAV) for j in range(2)]
        av_done = counted("av_done", NAV)
        o_freed = counted("o_freed", NG)
        oy_var = counted("oy_var", T)
        oy_rs = counted("oy_rs", T)
        y_var = counted("y_var", T)
        y_rs = counted("y_rs", T)
        y_ready = counted("y_ready", T)
        y_out = [counted(f"y_out{k}", 16 * T // 2) for k in range(2)]
        f_filled = counted("f_filled", 2 * NJ)
        f_freed = counted("f_freed", 2 * NJ)
        tanh_done = counted("tanh_done", 2 * NJ)
        h_hi = counted("h_hi", 2 * NJ)
        h_lo = counted("h_lo", 2 * NJ)
        down_done = counted("down_done", 2 * NJ)
        f_var = counted("f_var", T)
        f_rs = counted("f_rs", T)
        fin_done = counted("fin_done", T)
        y_in = [counted(f"y_in{k}", 16 * T // 2) for k in range(2)]
        out_done = [counted(f"out_done{k}", 16 * T // 2) for k in range(2)]
        own_count = {f"{n}{i}": T for n in "xoyf" for i in "ab"} | dict(m=NG, r=NG, on=T, fn=T, fs=T, h=2 * NJ)
        own_sem = {n: counted(f"own_{n}", c) for n, c in own_count.items()}
        init_own = sem("init_own")
        primed = sem("primed")
        tok_init = sem("tok_init")

        def fill(b, step):
            return (b + 1) * IPB + ITEM[step] // 2 + 1

        def bank(step):
            return ITEM[step] % 2

        def of(sem_, per, b, n):
            return sem_, (b + 1) * per + n + 1

        block = ctx.enter_context(nc.Block())

        def run(eng, parts):
            def steps(b, plan):
                for delta, step in plan:
                    if step[0] in parts:
                        parts[step[0]](b + delta, *step[1:])

            steps(0, HEAD)
            with eng.Fori(1, NB) as b:
                steps(b, BOTH)
            steps(NB - 1, REST)

        @block.sync
        def _(sp):
            for s, n in credit.values():
                sp.sem_inc(s, n)
            sp.sem_inc(primed, 1)
            x_v = a["x"].rearrange("b (t p) d -> b t p d", p=P)
            y_v = y_dram.rearrange("b (t p) d -> b t p d", p=P)
            out_v = out.rearrange("b (t p) d -> b t p d", p=P)

            def load_x(b, r):
                k = r % 2
                if r < 2:
                    sp.wait_ge(*of(part_hi, NS, b - 1, SCR[("on", T - 2 + r)]))
                    sp.wait_ge(*of(y_out[k], 16 * T // 2, b - 1, 16 * T // 2 - 1))
                elif r < T + 2:
                    sp.wait_ge(*of(part_hi, NS, b, SCR[("xn", r - 2)]))
                else:
                    sp.wait_ge(*of(part_hi, NS, b, SCR[("on", r - 2 - T)]))
                    sp.wait_ge(*of(y_out[k], 16 * T // 2, b, 15))
                sp.dma_start(xt[:, k, :], x_v[b, r % T]).then_inc(x_in[k], 16)

            def x(b, t):
                load_x(b, t)

            def proj(b, g, w):
                if g == 0 and w == 0:
                    load_x(b, T)
                    load_x(b, T + 1)

            def oy(b, t):
                sp.wait_ge(*of(y_ready, T, b, t))
                sp.dma_start(y_v[b, t], xt[:, t % 2, :]).then_inc(y_out[t % 2], 16)

            def on(b, t):
                if t < 2:
                    load_x(b, T + 2 + t)

            def gate(b, f):
                if f % NJ == 8:
                    for tt in range(2):
                        n = 2 * (f // NJ) + tt
                        sp.wait_ge(*of(y_out[tt], 16 * T // 2, b, 16 * (n // 2) + 15))
                        sp.wait_ge(*of(out_done[tt], 16 * T // 2, b, 16 * (n // 2) - 1))
                        sp.dma_start(yt[:, tt, :], y_v[b, n]).then_inc(y_in[tt], 16)

            def fin(b, hf, tt):
                sp.wait_ge(*of(fin_done, T, b, 2 * hf + tt))
                sp.dma_start(out_v[b, 2 * hf + tt], yt[:, tt, :]).then_inc(out_done[tt], 16)

            run(sp, dict(x=x, proj=proj, oy=oy, on=on, gate=gate, fin=fin))
            for k in range(2):
                sp.wait_ge(*of(out_done[k], 16 * T // 2, NB - 1, 16 * T // 2 - 1))
                sp.wait_ge(*of(y_out[k], 16 * T // 2, NB - 1, 16 * T // 2 - 1))

        @block.tensor
        def _(pe):
            pe.wait_ge(primed, 1)
            pe.wait_ge(tok_init, 3)

            def item(b, step, *after):
                k = bank(step)
                pe.wait_ge(freed[k], (b + 1) * IPB + ITEM[step] // 2)
                other = [ITEM[s] // 2 + 1 for s in after if bank(s) != k]
                if other:
                    pe.wait_ge(freed[1 - k], (b + 1) * IPB + max(other))
                return k

            def transposes(b, step, split):
                k = item(b, step)
                pe.wait_ge(*of(scr_free, NS, b, SCR[split]))
                for part in range(2):
                    for kt in range(KT):
                        col = (part * KT + kt) * P
                        mm = nc.tensor.transpose(work16[k][:, col:col + P], nhl[:, part, kt * P:(kt + 1) * P], ident[:])
                mm.then_inc(filled[k], 1)

            def ln1(b, t):
                transposes(b, ("ln1", t), ("xn", t))

            def ln2(b, t):
                transposes(b, ("ln2", t), ("on", t))

            def c(b, w):
                step = ("c", w)
                k = item(b, step, ("ln1", T - 2), ("ln1", T - 1))
                for kt in range(KT):
                    for n, (pw, px) in enumerate(PASSES):
                        mm = nc.tensor.matmul(work[k], att_w[:, A_DQ + w, pw, kt * P:(kt + 1) * P], xT[:, px, kt, :],
                                              start=kt == n == 0, stop=kt == KT - 1 and n == 2)
                mm.then_inc(filled[k], 1)

            def v_(b, t):
                step = ("v", t)
                k = item(b, step, ("c", 1))
                for n, (pc, pw) in enumerate(PASSES):
                    mm = nc.tensor.matmul(work[k], cT[:, 1, pc, t * P:(t + 1) * P], att_w[:, A_UV, pw, :],
                                          start=n == 0, stop=n == 2)
                mm.then_inc(filled[k], 1)

            def proj(b, g, w):
                step = ("proj", g, w)
                k = item(b, step, *[("c", 0)] * w)
                cols = slice(g * P, (g + 1) * P)
                pick = (pick_k, pick_q)[w]
                nc.tensor.matmul(work[k].rearrange("p (t n) -> p t n", t=T), pick[:],
                                 bias_qk[:, cols].unsqueeze(1).to_broadcast([P, T, P]),
                                 start=True, stop=False, skip_group_check=True)
                for t in range(T):
                    for kt in range(KT if w == 0 else 1):
                        for pa, pw in PASSES:
                            lhs = xT[:, pa, kt, t * P:(t + 1) * P] if w == 0 else cT[:, 0, pa, t * P:(t + 1) * P]
                            tile = A_KR + kt if w == 0 else A_QR
                            mm = nc.tensor.matmul(work[k][:, t * P:(t + 1) * P], lhs, att_w[:, tile, pw, cols],
                                                  start=False, stop=True, skip_group_check=True)
                mm.then_inc(filled[k], 1)

            def stack(b, g, w, j):
                step = ("stack", g, w, j)
                k = item(b, step)
                pe.wait_ge(*of(scr_free, NS, b, SCR[("proj", g, w)]))
                for hh in range(2):
                    for t in range(T):
                        col = (hh * T + t) * P
                        mm = nc.tensor.transpose(work16[k][0:STACK, col:col + P], tok[:, w, t, 2 * j + hh, :], ident[:])
                mm.then_inc(filled[k], 1)

            def smax(b, g, h, t):
                step = ("smax", g, h, t)
                k = item(b, step, *[("stack", g, w, h // 2) for w in range(2) if h % 2 == 0 and t < 2])
                nc.tensor.matmul(work[k], qT[0:STACK, h, t * P:(t + 1) * P], kT[0:STACK, h, :],
                                 start=True, stop=True).then_inc(filled[k], 1)

            def maxrow(b, g, j):
                step = ("maxrow", g, j)
                k = item(b, step)
                pe.wait_ge(*of(neg_max, NG, b, g))
                for hh in range(2):
                    for t in range(T):
                        col = (hh * T + t) * P
                        mm = nc.tensor.transpose(work16[k][STACK:P, col:col + P], mtok[:, t, 2 * j + hh, :], ident[:])
                mm.then_inc(filled[k], 1)

            def st(b, g, u, j):
                step = ("st", g, u, j)
                k = item(b, step, *[("maxrow", g, j)] * (u == 0))
                kt, qh = divmod(u, 2)
                for hh in range(2):
                    mm = nc.tensor.matmul(work[k][:, hh * HALF:(hh + 1) * HALF], kT[:, 2 * j + hh, kt * P:(kt + 1) * P],
                                          qT[:, 2 * j + hh, qh * HALF:(qh + 1) * HALF], start=True, stop=True)
                mm.then_inc(filled[k], 1)

            def av(b, g, u):
                kt, qh = divmod(u, 2)
                n = g * 2 * T + u
                for j in range(2):
                    pe.wait_ge(*of(p_lo[j], NAV, b, n))
                if u == 0:
                    pe.wait_ge(*of(o_freed, NG, b, g - 1))
                    s = ("v", T - 1)
                    pe.wait_ge(freed[bank(s)], fill(b, s))
                q = slice(qh * HALF, (qh + 1) * HALF)
                for i, (pv, pp) in enumerate(PASSES):
                    for h in range(HG):
                        head = (g * HG + h) * DH
                        nc.tensor.matmul(o_acc[h * DH:(h + 1) * DH, q], v[:, kt, pv, head:head + DH],
                                         pr[:, n % 2, pp, h, :], start=u == 0 and i == 0, stop=True,
                                         skip_group_check=True)
                for pp in range(2):
                    for h in range(HG):
                        mm = nc.tensor.matmul(den_acc[h * DH:(h + 1) * DH, q], ones[:], pr[:, n % 2, pp, h, :],
                                              start=u == 0 and pp == 0, stop=True, skip_group_check=True)
                mm.then_inc(av_done, 1)

            def o(b, t):
                step = ("o", t)
                k = item(b, step)
                nc.tensor.matmul(work[k], pick_q[:], bias_o[:], start=True, stop=False)
                for g in range(NG):
                    pe.wait_ge(*of(scr_free, NS, b, SCR[("norm", g)]))
                    for n, (po, pw) in enumerate(PASSES):
                        mm = nc.tensor.matmul(work[k], oT[:, g, po, t * P:(t + 1) * P], att_w[:, A_O + g, pw, :],
                                              start=False, stop=g == NG - 1 and n == 2)
                mm.then_inc(filled[k], 1)

            def down(b, f):
                hf, j = divmod(f, NJ)
                pe.wait_ge(*of(h_lo, 2 * NJ, b, f))
                for tt in range(2):
                    if j == 0:
                        pe.wait_ge(*of(fin_done, T, b, 2 * hf + tt - 2))
                    for n, (ph, pw) in enumerate(PASSES):
                        mm = nc.tensor.matmul(down_ps[tt], hid[:, f % 2, ph, tt * P:(tt + 1) * P], down_w[:, j, pw, :],
                                              start=j == n == 0, stop=j == NJ - 1 and n == 2)
                mm.then_inc(down_done, 1)

            def product(b, f, half, weights):
                hf, j = divmod(f, NJ)
                for kt in range(KT):
                    for n, (pw, px) in enumerate(PASSES):
                        mm = nc.tensor.matmul(ffn_ps[f % 2][:, half * HALF:(half + 1) * HALF],
                                              weights[:, kt, pw, j * P:(j + 1) * P],
                                              x2T[:, px, kt, hf * HALF:(hf + 1) * HALF],
                                              start=kt == n == 0, stop=kt == KT - 1 and n == 2)
                return mm

            def gate(b, f):
                if f % NJ == 0:
                    tiles = [("ln2", 2 * (f // NJ) + i) for i in range(2)]
                    for s in tiles:
                        pe.wait_ge(freed[bank(s)], fill(b, s))
                pe.wait_ge(*of(f_freed, 2 * NJ, b, f - 2))
                product(b, f, 0, gate_w)

            def up(b, f):
                product(b, f, 1, up_w).then_inc(f_filled, 1)

            run(pe, dict(ln1=ln1, ln2=ln2, c=c, v=v_, proj=proj, stack=stack, smax=smax, maxrow=maxrow,
                         st=st, av=av, o=o, gate=gate, up=up, down=down))

        @block.scalar
        def _(sc):
            sc.wait_ge(primed, 1)
            sc.wait_ge(tok_init, 3)

            def got(b, step):
                k = bank(step)
                sc.wait_ge(filled[k], fill(b, step))
                return k

            def c(b, w):
                step = ("c", w)
                k = got(b, step)
                nc.scalar.activation(cT[:, w, 0, :], work[k], ACT.Identity, bias=c_bias[:, w:w + 1]).then_inc(cv_hi, 1)

            def v_(b, t):
                k = got(b, ("v", t))
                sc.wait_ge(*of(av_done, NAV, b - 1, NAV - 1))
                nc.scalar.activation(v[:, t, 0, :], work[k], ACT.Copy, scale=V_SHIFT).then_inc(cv_hi, 1)

            def proj(b, g, w):
                sc.wait_ge(*of(rope_sum, 2 * NG, b, 2 * g + w))
                s, bb = (("stack", g - 1, w, 1), b) if g else (("stack", NG - 1, w, 1), b - 1)
                sc.wait_ge(filled[bank(s)], fill(bb, s))
                dst = tok[:, w].rearrange("p t h (r d) -> p (t h) r d", r=3)
                dst = dst[:, :, 0:3:2, :] if w == 0 else dst[:, :, 0:2, :]
                src = scr[:, 0, :].rearrange("p (n r d) -> p n r d", r=1, d=DH).to_broadcast([P, T * HG, 2, DH])
                nc.scalar.activation(dst, src, ACT.Copy).then_inc(part_hi, 1)

            def stack(b, g, w, j):
                step = ("stack", g, w, j)
                k = got(b, step)
                nc.scalar.activation((kT, qT)[w][0:STACK, 2 * j:2 * j + 2, :].rearrange("p h s -> p (h s)"),
                                     work16[k][0:STACK, :], ACT.Copy).then_inc(freed[k], 1)

            def maxrow(b, g, j):
                step = ("maxrow", g, j)
                k = got(b, step)
                nc.scalar.activation(qT[STACK:P, 2 * j:2 * j + 2, :].rearrange("p h s -> p (h s)"),
                                     work16[k][STACK:P, :], ACT.Copy).then_inc(freed[k], 1)

            def st(b, g, u, j):
                step = ("st", g, u, j)
                k = got(b, step)
                n = (g * 2 * T + u) * 2 + j
                sc.wait_ge(*of(p_lo[j], NAV, b, n // 2 - 1))
                nc.scalar.activation(p32[:, j, :], work[k], ACT.Exp, scale=exp_scale[:, 0:1]).then_inc(freed[k], 1)

            def norm(b, g):
                sc.wait_ge(*of(o_freed, NG, b, g))
                s = ("o", T - 1)
                sc.wait_ge(filled[bank(s)], fill(b - 1, s))
                nc.scalar.activation(oT[:, g, 0, :], scr[:, 0, :], ACT.Copy).then_inc(part_hi, 1)

            def h_high(b, f):
                sc.wait_ge(*of(f_freed, 2 * NJ, b, f))
                sc.wait_ge(*of(down_done, 2 * NJ, b, f - 2))
                nc.scalar.activation(hid[:, f % 2, 0, :], act[:, f % 2, :], ACT.Copy).then_inc(h_hi, 1)

            def up(b, f):
                sc.wait_ge(*of(f_filled, 2 * NJ, b, f))
                sc.wait_ge(*of(h_lo, 2 * NJ, b, f - 2))
                nc.scalar.activation(act[:, f % 2, :], ffn_ps[f % 2][:, 0:HALF], ACT.Tanh,
                                     scale=half_gate[:, f % NJ:f % NJ + 1]).then_inc(tanh_done, 1)
                if f:
                    h_high(b, f - 1)

            def down(b, f):
                if f == 2 * NJ - 2:
                    h_high(b, f + 1)

            run(sc, dict(c=c, v=v_, proj=proj, stack=stack, maxrow=maxrow, st=st, norm=norm,
                         up=up, down=down))

        @block.vector
        def _(dve):
            def got(b, step):
                k = bank(step)
                dve.wait_ge(filled[k], fill(b, step))
                return k

            nc.vector.memset(kT[STACK:P, :, :].rearrange("p h s -> p (h s)"), 0.0).then_inc(init_own, 1)
            dve.wait_ge(init_own, 1)
            nc.vector.memset(kT[STACK:STACK + 2, :, :].rearrange("p h s -> p (h s)"), MAX_SHIFT).then_inc(tok_init, 1)
            nc.vector.memset(mtok[:].rearrange("p t h d -> p (t h d)"), 0.0).then_inc(tok_init, 1)
            nc.vector.memset(mhalf[:], -0.5).then_inc(tok_init, 1)
            dve.wait_ge(primed, 1)
            dve.wait_ge(tok_init, 3)

            def tied(b, key, ins):
                kind = key[0]
                ins.then_inc(own_sem[kind], 1)
                n = own_count[kind]
                dve.wait_ge(own_sem[kind], (b + 1) * n + key[1] + 1)

            def stats(b, kind, n, src, st_, mv_, t, eps):
                tied(b, (kind + "a", n), nc.vector.bn_stats(st_[:, t, :], src))
                nc.vector.memset(carry[:], 0.0)
                tied(b, (kind + "b", n), nc.vector.bn_aggr(mv_[:, t, :], st_[:, t, :]))
                row = dict(x=0, o=1, y=2, f=3)[kind]
                done = dict(x=x_var, o=oy_var, y=y_var, f=f_var)[kind]
                nc.vector.tensor_scalar(ve[:, row, t:t + 1], mv_[:, t, 1:2], eps, None, ALU.add).then_inc(done, 1)

            def x(b, t):
                k = t % 2
                dve.wait_ge(*of(x_in[k], 16 * T, b, 16 * (t // 2) + 15))
                stats(b, "x", t, xt[:, k, :], st1, mv1, t, EPS)

            before = {}
            tiles = [s for s in ATT if s[0] in ("ln1", "ln2")]
            for n, tile in enumerate(tiles):
                before[tile] = (tiles[n - 1], 0 if n else -1)

            def normed(b, t, step, transposed, mv_, row):
                k = t % 2
                nc.vector.tensor_scalar(scr[:, k, :], xt[:, k, :], mv_[:, t, 0:1], rs[:, row, t:t + 1],
                                        ALU.subtract, ALU.mult)
                s, delta = before[transposed, t]
                dve.wait_ge(filled[bank(s)], fill(b + delta, s))
                nc.vector.tensor_scalar(nhl[:, 0, :], xt[:, k, :], mv_[:, t, 0:1], rs[:, row, t:t + 1],
                                        ALU.subtract, ALU.mult).then_inc(part_hi, 1)
                dve.wait_ge(*of(part_hi, NS, b, SCR[step, t]))
                nc.vector.tensor_tensor(nhl[:, 1, :], scr[:, k, :], nhl[:, 0, :], ALU.subtract).then_inc(scr_free, 1)

            def xn(b, t):
                dve.wait_ge(*of(x_rs, T, b, t))
                dve.wait_ge(*of(scr_free, NS, b, SCR[("xn", t)] - 2))
                normed(b, t, "xn", "ln1", mv1, 0)

            def ln1(b, t):
                k2 = got(b, ("ln1", t))
                nc.vector.tensor_copy(xT[:, :, :, t * P:(t + 1) * P],
                                      work16[k2].rearrange("p (a k n) -> p a k n", a=2, k=KT)).then_inc(freed[k2], 1)

            def c(b, w):
                k = got(b, ("c", w))
                dve.wait_ge(*of(cv_hi, 2 + T, b, w))
                nc.vector.scalar_tensor_tensor(out=cT[:, w, 1, :], in0=work[k], scalar=c_bias[:, w:w + 1],
                                               in1=cT[:, w, 0, :], op0=ALU.add, op1=ALU.subtract).then_inc(freed[k], 1)

            def v_(b, t):
                k = got(b, ("v", t))
                dve.wait_ge(*of(cv_hi, 2 + T, b, 2 + t))
                nc.vector.scalar_tensor_tensor(out=v[:, t, 1, :], in0=work[k], scalar=V_SHIFT, in1=v[:, t, 0, :],
                                               op0=ALU.mult, op1=ALU.subtract).then_inc(freed[k], 1)

            def proj(b, g, w):
                step = ("proj", g, w)
                k = got(b, step)
                dve.wait_ge(*of(scr_free, NS, b, SCR[step] - 1))
                src = work[k].rearrange("p (t h d) -> p t h d", t=T, h=HG)
                for i in range(2):
                    table = rope[:, 2 * w + i].unsqueeze(2).to_broadcast([P, T, HG, DH])
                    ins = nc.vector.tensor_tensor(scr[:, i, :].rearrange("p (t h d) -> p t h d", t=T, h=HG),
                                                  src, table, ALU.mult)
                ins.then_inc(freed[k], 1)

            def smax(b, g, h, t):
                k = got(b, ("smax", g, h, t))
                ins = nc.vector.reduce_max(mx[:, t, h:h + 1], work[k], AX.X)
                ins.then_inc(freed[k], 1)
                if (h, t) == (HG - 1, T - 1):
                    for q in range(2):
                        s = ("smax", g, h, t - q)
                        dve.wait_ge(freed[bank(s)], fill(b, s))
                    tied(b, ("m", g), nc.vector.tensor_scalar(mtok[:, :, :, 0], mx[:], -1.0 / MAX_SHIFT, None, ALU.mult))
                    nc.vector.scalar_tensor_tensor(out=mtok[:, :, :, 1], in0=mx[:], scalar=-1.0 / MAX_SHIFT,
                                                   in1=mtok[:, :, :, 0], op0=ALU.mult,
                                                   op1=ALU.subtract).then_inc(neg_max, 1)

            def st(b, g, u, j):
                s = ("st", g, u, j)
                m = g * 2 * T + u
                dve.wait_ge(freed[bank(s)], fill(b, s))
                dve.wait_ge(*of(av_done, NAV, b, m - 2))
                dst = pr[:, m % 2, :, 2 * j:2 * j + 2, :]
                hi, lo = (dst[:, i].rearrange("p h q -> p (h q)") for i in range(2))
                nc.vector.tensor_copy(hi, p32[:, j, :]).then_inc(p_hi, 1)
                if j == 1:
                    dve.wait_ge(*of(p_hi, NST, b, 2 * m + 1))
                    nc.vector.tensor_tensor(lo, p32[:, j, :], hi, ALU.subtract).then_inc(p_lo[1], 1)

            def norm(b, g):
                dve.wait_ge(*of(av_done, NAV, b, (g + 1) * 2 * T - 1))
                dve.wait_ge(*of(scr_free, NS, b, SCR[("norm", g)] - 1))
                tied(b, ("r", g), nc.vector.reciprocal(scr[:, 0, :], den_acc))
                nc.vector.tensor_tensor(scr[:, 0, :], o_acc, scr[:, 0, :], ALU.mult).then_inc(o_freed, 1)

            def o(b, t):
                k = got(b, ("o", t))
                stats(b, "o", t, work[k], st2, mv2, t, eps_y[:, 0:1])

            def oy(b, t):
                step = ("o", t)
                k, kx = bank(step), t % 2
                dve.wait_ge(*of(oy_rs, T, b, t))
                tied(b, ("on", t), nc.vector.scalar_tensor_tensor(out=nmr[:, 1, t:t + 1], in0=mv2[:, t, 0:1], scalar=-1.0,
                                                                  in1=rs[:, 1, t:t + 1], op0=ALU.mult, op1=ALU.mult))
                dve.wait_ge(*of(x_in[kx], 16 * T, b, 16 * (T // 2 + t // 2) + 15))
                nc.vector.scalar_tensor_tensor(out=xt[:, kx, :], in0=work[k], scalar=rs[:, 1, t:t + 1],
                                               in1=xt[:, kx, :], op0=ALU.mult, op1=ALU.add).then_inc(freed[k], 1)
                dve.wait_ge(freed[k], fill(b, step))
                nc.vector.tensor_scalar(xt[:, kx, :], xt[:, kx, :], nmr[:, 1, t:t + 1], None,
                                        ALU.add).then_inc(y_ready, 1)
                dve.wait_ge(*of(y_ready, T, b, t))
                stats(b, "y", t, xt[:, kx, :], st3, mv3, t, EPS)

            def on(b, t):
                dve.wait_ge(*of(y_rs, T, b, t))
                dve.wait_ge(*of(scr_free, NS, b, SCR[("on", t)] - (1 if t == 0 else 2)))
                normed(b, t, "on", "ln2", mv3, 2)

            def ln2(b, t):
                k = got(b, ("ln2", t))
                if t % 2 == 0:
                    dve.wait_ge(*of(f_filled, 2 * NJ, b - 1, (t // 2 + 1) * NJ - 1))
                nc.vector.tensor_copy(x2T[:, :, :, t * P:(t + 1) * P],
                                      work16[k].rearrange("p (a k n) -> p a k n", a=2, k=KT)).then_inc(freed[k], 1)

            def up(b, f):
                k = f % 2
                dve.wait_ge(*of(tanh_done, 2 * NJ, b, f))
                tied(b, ("h", f), nc.vector.scalar_tensor_tensor(out=act[:, k, :], in0=act[:, k, :], scalar=1.0,
                                                                 in1=ffn_ps[k][:, 0:HALF], op0=ALU.add, op1=ALU.mult))
                nc.vector.scalar_tensor_tensor(out=act[:, k, :], in0=ffn_ps[k][:, HALF:2 * HALF], scalar=H_SHIFT,
                                               in1=act[:, k, :], op0=ALU.mult, op1=ALU.mult).then_inc(f_freed, 1)

            def fin(b, hf, tt):
                n = 2 * hf + tt
                dve.wait_ge(*of(down_done, 2 * NJ, b, hf * NJ + NJ - 1))
                stats(b, "f", n, down_ps[tt], st4, mv4, n, eps_f[:, 0:1])
                dve.wait_ge(*of(f_rs, T, b, n))
                tied(b, ("fn", n), nc.vector.scalar_tensor_tensor(out=nmr[:, 3, n:n + 1], in0=mv4[:, n, 0:1], scalar=-1.0,
                                                                  in1=rs[:, 3, n:n + 1], op0=ALU.mult, op1=ALU.mult))
                dve.wait_ge(*of(y_in[tt], 16 * T // 2, b, 16 * hf + 15))
                tied(b, ("fs", n), nc.vector.scalar_tensor_tensor(out=yt[:, tt, :], in0=down_ps[tt],
                                                                  scalar=rs[:, 3, n:n + 1], in1=yt[:, tt, :],
                                                                  op0=ALU.mult, op1=ALU.add))
                nc.vector.tensor_scalar(yt[:, tt, :], yt[:, tt, :], nmr[:, 3, n:n + 1], None,
                                        ALU.add).then_inc(fin_done, 1)

            run(dve, dict(x=x, xn=xn, ln1=ln1, on=on, ln2=ln2, c=c, v=v_, proj=proj, smax=smax, st=st, norm=norm,
                          o=o, oy=oy, up=up, fin=fin))

        @block.gpsimd
        def _(pool):
            pool.wait_ge(primed, 1)
            pool.wait_ge(tok_init, 3)

            def root(b, row, t, var, rs_):
                pool.wait_ge(*of(var, T, b, t))
                nc.gpsimd.tensor_tensor(rs[:, row, t:t + 1], ve[:, row, t:t + 1], mhalf[:], ALU.pow).then_inc(rs_, 1)

            def low(b, step, out_, in_, hi):
                pool.wait_ge(*of(part_hi, NS, b, SCR[step]))
                nc.gpsimd.tensor_tensor(out_, in_, hi, ALU.subtract).then_inc(scr_free, 1)

            def x(b, t):
                root(b, 0, t, x_var, x_rs)

            def o(b, t):
                root(b, 1, t, oy_var, oy_rs)

            def oy(b, t):
                root(b, 2, t, y_var, y_rs)

            def proj(b, g, w):
                s = ("proj", g, w)
                k = bank(s)
                pool.wait_ge(freed[k], fill(b, s))
                a1 = scr[:, 0, :].rearrange("p (n r d) -> p n r d", r=2, d=DH // 2)
                a2 = scr[:, 1, :].rearrange("p (n r d) -> p n r d", r=2, d=DH // 2)
                nc.gpsimd.tensor_tensor(a1[:, :, 0, :], a1[:, :, 0, :], a2[:, :, 1, :], ALU.add)
                nc.gpsimd.tensor_tensor(a1[:, :, 1, :], a1[:, :, 1, :], a2[:, :, 0, :], ALU.add).then_inc(rope_sum, 1)
                pool.wait_ge(*of(part_hi, NS, b, SCR[s]))
                dst = tok[:, w].rearrange("p t h (r d) -> p (t h) r d", r=3)
                nc.gpsimd.tensor_tensor(dst[:, :, 1 + w, :], scr[:, 0, :].rearrange("p (n d) -> p n d", d=DH),
                                        dst[:, :, 0, :], ALU.subtract).then_inc(scr_free, 1)

            def st(b, g, u, j):
                if j == 1:
                    return
                m = g * 2 * T + u
                pool.wait_ge(*of(p_hi, NST, b, 2 * m))
                dst = pr[:, m % 2, :, 0:2, :]
                nc.gpsimd.tensor_tensor(dst[:, 1].rearrange("p h q -> p (h q)"), p32[:, 0, :],
                                        dst[:, 0].rearrange("p h q -> p (h q)"), ALU.subtract).then_inc(p_lo[0], 1)

            def norm(b, g):
                low(b, ("norm", g), oT[:, g, 1, :], scr[:, 0, :], oT[:, g, 0, :])

            def h_low(b, f):
                pool.wait_ge(*of(h_hi, 2 * NJ, b, f))
                nc.gpsimd.tensor_tensor(hid[:, f % 2, 1, :], act[:, f % 2, :], hid[:, f % 2, 0, :],
                                        ALU.subtract).then_inc(h_lo, 1)

            def up(b, f):
                if f:
                    h_low(b, f - 1)

            def down(b, f):
                if f == 2 * NJ - 2:
                    h_low(b, f + 1)

            def fin(b, hf, tt):
                root(b, 3, 2 * hf + tt, f_var, f_rs)

            run(pool, dict(x=x, o=o, oy=oy, proj=proj, st=st, norm=norm, up=up, down=down, fin=fin))


_PRE = {"x": "L0_attn_x"} | {n: "L0_attn_" + n for n in (
    "W_dkv", "b_dkv", "W_dq", "b_dq", "W_uv", "b_uv", "W_qr", "b_qr", "W_kr", "b_kr", "W_o", "b_o")} | {
    n: "L0_ffn_" + n for n in ("SU_ug", "SU_dp", "Wscale_ug", "Wscale_dp", "W_up", "W_gate", "W_down")}


def constants():
    inv_freq = (1.0 / 10000.0 ** (np.arange(0, DH, 2, dtype=np.float32) / np.float32(DH))).astype(np.float32)
    freqs = np.arange(S, dtype=np.float32)[:, None] * inv_freq[None, :]
    cos, sin = np.cos(freqs), np.sin(freqs)
    cos2, sin2 = np.concatenate([cos, cos], 1), np.concatenate([sin, -sin], 1)
    rope = np.stack([cos2 * K_SHIFT, sin2 * K_SHIFT, cos2 * Q_SHIFT, sin2 * Q_SHIFT]).astype(np.float32)
    had = np.ones((1, 1), np.float32)
    while had.shape[0] < P:
        had = np.block([[had, had], [had, -had]])
    return {"rope": rope, "had": had.astype(np.float32)}


def kernel(**inputs):
    import concourse.bacc as _bacc
    from concourse.bass_utils import run_bass_kernel_spmd as _run

    nc = _bacc.Bacc("TRN2", target_bir_lowering=False, num_devices=1)
    arrays, args = {}, {}
    data = {n: np.ascontiguousarray(inputs[full]) for n, full in _PRE.items()} | constants()
    for name, x in data.items():
        arrays[f"in_{name}"] = x
        args[name] = nc.dram_tensor(f"in_{name}", x.shape, mybir.dt.from_np(x.dtype), kind="ExternalInput").ap()
    out = nc.dram_tensor("out_0", (NB, S, D), F32, kind="ExternalOutput").ap()
    y = nc.dram_tensor("y_mid", (NB, S, D), F32, kind="Internal").ap()
    program(nc, args, out, y)
    r = _run(nc, [arrays], core_ids=[0])
    return r.results[0]["out_0"]
```
